# Optimizing a Trainium2 kernel written in Bass

```python
import numpy as np
import jax
import jax.numpy as jnp

def _softmax(x, axis=-1):
    return jax.nn.softmax(x, axis=axis)

def _gelu(x):
    return jax.nn.gelu(x, approximate=True)

def _silu(x):
    return jax.nn.silu(x)

def _sigmoid(x):
    return jax.nn.sigmoid(x)

def _layernorm(x, axis=-1, eps=1e-05):
    m = jnp.mean(x, axis=axis, keepdims=True)
    v = jnp.var(x, axis=axis, keepdims=True)
    return (x - m) / jnp.sqrt(v + eps)

def _scatter_add(tgt, idx, src, axis=0):
    return tgt.at[idx].add(src)

def _segment_sum(src, seg, n):
    return jax.ops.segment_sum(src, seg, n)
kernel_name = 'mk_xattn_ffn_d2_seqx_r4_1a9d7b'

def setup_inputs(seed: int=0):
    np.random.seed(seed)
    _w = jnp.asarray

    def _rec_inputs():
        import jax
        import jax.numpy as jnp
        _rk = jax.random.key(seed)
        x = 4.136e-05 + 0.9999 * jax.random.normal(jax.random.fold_in(_rk, 1), (4, 512, 512), jnp.float32)
        _lenS = 512 - jax.random.randint(jax.random.fold_in(_rk, 7), (4,), 0, max(1, 512 // 4) + 1, jnp.int32)
        _lenS2 = 512 - jax.random.randint(jax.random.fold_in(_rk, 8), (4,), 0, max(1, 512 // 4) + 1, jnp.int32)
        _ctx_1024P = jax.random.normal(jax.random.fold_in(_rk, 11), (4, 16, 256), jnp.float32)
        _ctx_1024c = jax.random.dirichlet(jax.random.fold_in(_rk, 511), 0.3 * jnp.ones((16,), jnp.float32), (4, 512))
        _ctx_1024t = jnp.einsum('bsk,bkd->bsd', _ctx_1024c, _ctx_1024P)
        _ctx_1024t = _ctx_1024t * jax.lax.rsqrt(jnp.mean(jnp.square(_ctx_1024t)) + 1e-12) * 0.953939
        ctx_1024 = -0.000292821 + 1.00034 * (_ctx_1024t + 0.3 * jax.random.normal(jax.random.fold_in(_rk, 611), (4, 512, 256), jnp.float32))
        return (x, ctx_1024)
    x, ctx_1024 = _rec_inputs()

    def _L0_xattn_setup():
        import jax, jax.numpy as jnp
        import numpy as np
        import math
        B, L, DM = (2, 512, 256)
        DS, DC, EXP = (16, 4, 2)
        DI = EXP * DM
        DR = math.ceil(DM / 16)
        DT_MIN, DT_MAX, DT_FLOOR = (0.001, 0.1, 0.0001)

        def _ssm_forward(hidden_states, z, in_proj_w, conv_w, conv_b, x_proj_w, dt_proj_w, dt_proj_b, A_log, D):
            b = hidden_states.shape[0]
            x = jnp.einsum('ed,bld->bel', in_proj_w, hidden_states)
            xp = jnp.pad(x, ((0, 0), (0, 0), (DC - 1, 0)))
            xc = jax.lax.conv_general_dilated(xp, conv_w[:, None, :], window_strides=(1,), padding='VALID', dimension_numbers=('NCH', 'OIH', 'NCH'), feature_group_count=DI)
            u = jax.nn.silu(xc + conv_b[None, :, None])
            x_dbl = jnp.einsum('ke,bel->bkl', x_proj_w, u)
            dt_lo = x_dbl[:, :DR]
            Bm = x_dbl[:, DR:DR + DS]
            Cm = x_dbl[:, DR + DS:]
            delta = jax.nn.softplus(jnp.einsum('er,brl->bel', dt_proj_w, dt_lo) + dt_proj_b[None, :, None])
            A = -jnp.exp(A_log)

            def step(state, xs):
                d_t, B_t, C_t, u_t = xs
                dA = jnp.exp(d_t[..., None] * A)
                state = state * dA + (d_t * u_t)[..., None] * B_t[:, None, :]
                y_t = jnp.einsum('ben,bn->be', state, C_t)
                return (state, y_t)
            xs = (jnp.moveaxis(delta, -1, 0), jnp.moveaxis(Bm, -1, 0), jnp.moveaxis(Cm, -1, 0), jnp.moveaxis(u, -1, 0))
            state0 = jnp.zeros((b, DI, DS), delta.dtype)
            _, ys = jax.lax.scan(step, state0, xs)
            y = jnp.moveaxis(ys, 0, -1)
            y = y + D[None, :, None] * u
            y = y * jax.nn.silu(z)
            return jnp.swapaxes(y, 1, 2)
        key = jax.random.key(seed)
        ks = jax.random.split(key, 8)
        hidden_states = jax.random.normal(ks[0], (B, L, DM), jnp.float32)
        z = jax.random.normal(ks[1], (B, DI, L), jnp.float32)
        in_proj_w = jax.random.normal(ks[2], (DI, DM), jnp.float32) * DM ** (-0.5)
        conv_w = jax.random.normal(ks[3], (DI, DC), jnp.float32) * DC ** (-0.5)
        conv_b = jnp.zeros((DI,), jnp.float32)
        x_proj_w = jax.random.normal(ks[4], (DR + 2 * DS, DI), jnp.float32) * DI ** (-0.5)
        dt_std = DR ** (-0.5)
        dt_proj_w = jax.random.uniform(ks[5], (DI, DR), jnp.float32, -dt_std, dt_std)
        dt = jnp.exp(jax.random.uniform(ks[6], (DI,), jnp.float32) * (math.log(DT_MAX) - math.log(DT_MIN)) + math.log(DT_MIN))
        dt = jnp.clip(dt, DT_FLOOR)
        dt_proj_b = dt + jnp.log(-jnp.expm1(-dt))
        A_log = jnp.log(jnp.broadcast_to(jnp.arange(1, DS + 1, dtype=jnp.float32), (DI, DS)))
        D = jnp.ones((DI,), jnp.float32)
        return dict(hidden_states=hidden_states, z=z, in_proj_w=in_proj_w, conv_w=conv_w, conv_b=conv_b, x_proj_w=x_proj_w, dt_proj_w=dt_proj_w, dt_proj_b=dt_proj_b, A_log=A_log, D=D)
    _L0_xattn_all = _L0_xattn_setup()
    _L0_xattn_in = {k: v for k, v in _L0_xattn_all.items() if k in ('in_proj_w', 'conv_w', 'conv_b', 'x_proj_w', 'dt_proj_w', 'dt_proj_b', 'A_log', 'D')}
    del _L0_xattn_all

    def _L0_ffn_setup():
        import jax, jax.numpy as jnp
        import numpy as np
        from jax import lax
        E = 64
        TOP_K = 8
        SEL_K = 4
        THRESH = 0.5
        H = 512
        F_INT = 192
        B, S = (1, 512)
        key = jax.random.key(seed)
        k0, k1, k2, k3, k4 = jax.random.split(key, 5)
        return {'hidden_states': jax.random.normal(k0, (B, S, H), jnp.float32), 'gate_weight': jax.random.normal(k1, (E, H), jnp.float32) * 0.02, 'gate_up_proj': jax.random.normal(k2, (E, 2 * F_INT, H), jnp.float32) * 0.02, 'down_proj': jax.random.normal(k3, (E, H, F_INT), jnp.float32) * 0.02, 'similarity': jax.random.uniform(k4, (E, E), jnp.float32)}
    _L0_ffn_all = _L0_ffn_setup()
    _L0_ffn_in = {k: v for k, v in _L0_ffn_all.items() if k in ('gate_weight', 'gate_up_proj', 'down_proj', 'similarity')}
    del _L0_ffn_all

    def _L1_xattn_setup():
        import jax, jax.numpy as jnp
        import numpy as np
        EPS = 1e-05

        def rmsnorm(x, g, eps=EPS):
            var = jnp.mean(jnp.square(x), axis=-1, keepdims=True)
            return x * jax.lax.rsqrt(var + eps) * g
        key = jax.random.key(seed)
        ks = jax.random.split(key, 8)
        B, Sq, Skv = (2, 1024, 128)
        dim, cdim, H, D = (512, 256, 16, 128)
        inner = H * D
        s = lambda f: 1.0 / np.sqrt(f)
        return {'hidden_states': jax.random.normal(ks[0], (B, Sq, dim), jnp.float32), 'encoder_hidden_states': jax.random.normal(ks[1], (B, Skv, cdim), jnp.float32), 'Wq': jax.random.normal(ks[2], (dim, inner), jnp.float32) * s(dim), 'Wk': jax.random.normal(ks[3], (cdim, inner), jnp.float32) * s(cdim), 'Wv': jax.random.normal(ks[4], (cdim, inner), jnp.float32) * s(cdim), 'Wo': jax.random.normal(ks[5], (inner, dim), jnp.float32) * s(inner), 'gq': jnp.ones((D,), jnp.float32), 'gk': jnp.ones((D,), jnp.float32)}
    _L1_xattn_all = _L1_xattn_setup()
    _L1_xattn_in = {k: v for k, v in _L1_xattn_all.items() if k in ('Wq', 'Wk', 'Wv', 'Wo', 'gq', 'gk')}
    del _L1_xattn_all

    def _L1_ffn_setup():
        import jax, jax.numpy as jnp
        import numpy as np
        D_MODEL = 512
        D_HIDDEN = 2048
        EPS = 1e-05

        def activation_quant(x):
            scale = 127.0 / jnp.clip(jnp.max(jnp.abs(x), axis=-1, keepdims=True), EPS, None)
            return jnp.clip(jnp.round(x * scale), -128, 127) / scale

        def weight_quant(w):
            scale = 1.0 / jnp.clip(jnp.mean(jnp.abs(w)), EPS, None)
            return jnp.clip(jnp.round(w * scale), -1, 1) / scale

        def bitlinear(x, w):
            xq = x + jax.lax.stop_gradient(activation_quant(x) - x)
            wq = w + jax.lax.stop_gradient(weight_quant(w) - w)
            return jnp.einsum('bsi,oi->bso', xq, wq)
        key = jax.random.key(seed)
        k_x, k_w1, k_w2 = jax.random.split(key, 3)
        x = jax.random.normal(k_x, (4, 512, D_MODEL), dtype=jnp.float32)
        w1 = jax.random.normal(k_w1, (D_HIDDEN, D_MODEL), dtype=jnp.float32) * (1.0 / np.sqrt(D_MODEL))
        w2 = jax.random.normal(k_w2, (D_MODEL, D_HIDDEN), dtype=jnp.float32) * (1.0 / np.sqrt(D_HIDDEN))
        return {'x': x, 'w1': w1, 'w2': w2}
    _L1_ffn_all = _L1_ffn_setup()
    _L1_ffn_in = {k: v for k, v in _L1_ffn_all.items() if k in ('w1', 'w2')}
    del _L1_ffn_all
    return {'x': x, 'ctx_1024': ctx_1024, 'L0_xattn_in_proj_w': _L0_xattn_in['in_proj_w'], 'L0_xattn_conv_w': _L0_xattn_in['conv_w'], 'L0_xattn_conv_b': _L0_xattn_in['conv_b'], 'L0_xattn_x_proj_w': _L0_xattn_in['x_proj_w'], 'L0_xattn_dt_proj_w': _L0_xattn_in['dt_proj_w'], 'L0_xattn_dt_proj_b': _L0_xattn_in['dt_proj_b'], 'L0_xattn_A_log': _L0_xattn_in['A_log'], 'L0_xattn_D': _L0_xattn_in['D'], 'L0_ffn_gate_weight': _L0_ffn_in['gate_weight'], 'L0_ffn_gate_up_proj': _L0_ffn_in['gate_up_proj'], 'L0_ffn_down_proj': _L0_ffn_in['down_proj'], 'L0_ffn_similarity': _L0_ffn_in['similarity'], 'L1_xattn_Wq': _L1_xattn_in['Wq'], 'L1_xattn_Wk': _L1_xattn_in['Wk'], 'L1_xattn_Wv': _L1_xattn_in['Wv'], 'L1_xattn_Wo': _L1_xattn_in['Wo'], 'L1_xattn_gq': _L1_xattn_in['gq'], 'L1_xattn_gk': _L1_xattn_in['gk'], 'L1_ffn_w1': _L1_ffn_in['w1'], 'L1_ffn_w2': _L1_ffn_in['w2']}

def reference(x, ctx_1024, L0_xattn_in_proj_w, L0_xattn_conv_w, L0_xattn_conv_b, L0_xattn_x_proj_w, L0_xattn_dt_proj_w, L0_xattn_dt_proj_b, L0_xattn_A_log, L0_xattn_D, L0_ffn_gate_weight, L0_ffn_gate_up_proj, L0_ffn_down_proj, L0_ffn_similarity, L1_xattn_Wq, L1_xattn_Wk, L1_xattn_Wv, L1_xattn_Wo, L1_xattn_gq, L1_xattn_gk, L1_ffn_w1, L1_ffn_w2):
    import jax
    import jax.numpy as jnp

    def _L0_xattn_ref(hidden_states, z, in_proj_w, conv_w, conv_b, x_proj_w, dt_proj_w, dt_proj_b, A_log, D):
        import jax, jax.numpy as jnp
        import numpy as np
        import math
        B, L, DM = (2, 512, 256)
        DS, DC, EXP = (16, 4, 2)
        DI = EXP * DM
        DR = math.ceil(DM / 16)
        DT_MIN, DT_MAX, DT_FLOOR = (0.001, 0.1, 0.0001)

        def _ssm_forward(hidden_states, z, in_proj_w, conv_w, conv_b, x_proj_w, dt_proj_w, dt_proj_b, A_log, D):
            b = hidden_states.shape[0]
            x = jnp.einsum('ed,bld->bel', in_proj_w, hidden_states)
            xp = jnp.pad(x, ((0, 0), (0, 0), (DC - 1, 0)))
            xc = jax.lax.conv_general_dilated(xp, conv_w[:, None, :], window_strides=(1,), padding='VALID', dimension_numbers=('NCH', 'OIH', 'NCH'), feature_group_count=DI)
            u = jax.nn.silu(xc + conv_b[None, :, None])
            x_dbl = jnp.einsum('ke,bel->bkl', x_proj_w, u)
            dt_lo = x_dbl[:, :DR]
            Bm = x_dbl[:, DR:DR + DS]
            Cm = x_dbl[:, DR + DS:]
            delta = jax.nn.softplus(jnp.einsum('er,brl->bel', dt_proj_w, dt_lo) + dt_proj_b[None, :, None])
            A = -jnp.exp(A_log)

            def step(state, xs):
                d_t, B_t, C_t, u_t = xs
                dA = jnp.exp(d_t[..., None] * A)
                state = state * dA + (d_t * u_t)[..., None] * B_t[:, None, :]
                y_t = jnp.einsum('ben,bn->be', state, C_t)
                return (state, y_t)
            xs = (jnp.moveaxis(delta, -1, 0), jnp.moveaxis(Bm, -1, 0), jnp.moveaxis(Cm, -1, 0), jnp.moveaxis(u, -1, 0))
            state0 = jnp.zeros((b, DI, DS), delta.dtype)
            _, ys = jax.lax.scan(step, state0, xs)
            y = jnp.moveaxis(ys, 0, -1)
            y = y + D[None, :, None] * u
            y = y * jax.nn.silu(z)
            return jnp.swapaxes(y, 1, 2)
        return _ssm_forward(hidden_states, z, in_proj_w, conv_w, conv_b, x_proj_w, dt_proj_w, dt_proj_b, A_log, D)

    def _L0_ffn_ref(hidden_states, gate_weight, gate_up_proj, down_proj, similarity):
        import jax, jax.numpy as jnp
        import numpy as np
        from jax import lax
        E = 64
        TOP_K = 8
        SEL_K = 4
        THRESH = 0.5
        H = 512
        F_INT = 192
        B, S = (1, 512)
        b, s, h = hidden_states.shape
        x = hidden_states.reshape(-1, h)
        logits = x @ gate_weight.T
        probs = jax.nn.softmax(logits.astype(jnp.float32), axis=-1).astype(logits.dtype)
        top_val, top_idx = lax.top_k(probs, TOP_K)
        top_val = top_val / jnp.clip(top_val.sum(-1, keepdims=True), 1e-12)
        sim = similarity.astype(jnp.float32)
        diag = jnp.arange(E)
        sim = sim.at[diag, diag].set(1.0)
        primary_mask = jnp.zeros((E,), bool).at[top_idx[:, :SEL_K].reshape(-1)].set(True)
        secondary_mask = jnp.zeros((E,), bool).at[top_idx[:, SEL_K:].reshape(-1)].set(True)
        cand = jnp.where(primary_mask[None, :], sim, -jnp.inf)
        best_primary = jnp.argmax(cand, axis=-1)
        best_sim = jnp.max(cand, axis=-1)
        replace = secondary_mask & ~primary_mask & (best_sim >= THRESH)
        mapping = jnp.where(replace, best_primary, jnp.arange(E))
        rerouted = mapping[top_idx]
        rerouted = rerouted.at[:, :SEL_K].set(top_idx[:, :SEL_K])
        flat_e = rerouted.reshape(-1)
        order = jnp.argsort(flat_e)
        tok = order // TOP_K
        xs = x[tok]
        group_sizes = jnp.zeros((E,), jnp.int32).at[flat_e].add(1)
        gu = lax.ragged_dot(xs, jnp.swapaxes(gate_up_proj, 1, 2), group_sizes)
        gate, up = jnp.split(gu, 2, axis=-1)
        hact = jax.nn.silu(gate) * up
        y = lax.ragged_dot(hact, jnp.swapaxes(down_proj, 1, 2), group_sizes)
        w = top_val.reshape(-1)[order]
        out = jnp.zeros_like(x).at[tok].add(y * w[:, None])
        return out.reshape(b, s, h)

    def _L1_xattn_ref(hidden_states, encoder_hidden_states, Wq, Wk, Wv, Wo, gq, gk):
        import jax, jax.numpy as jnp
        import numpy as np
        EPS = 1e-05

        def rmsnorm(x, g, eps=EPS):
            var = jnp.mean(jnp.square(x), axis=-1, keepdims=True)
            return x * jax.lax.rsqrt(var + eps) * g
        B, Sq, _ = hidden_states.shape
        Skv = encoder_hidden_states.shape[1]
        D = gq.shape[0]
        H = Wq.shape[1] // D
        scale = 1.0 / np.sqrt(D)
        q = (hidden_states @ Wq).reshape(B, Sq, H, D)
        k = (encoder_hidden_states @ Wk).reshape(B, Skv, H, D)
        v = (encoder_hidden_states @ Wv).reshape(B, Skv, H, D)
        q = rmsnorm(q, gq)
        k = rmsnorm(k, gk)
        scores = jnp.einsum('bqhd,bkhd->bhqk', q, k) * scale
        attn = jax.nn.softmax(scores, axis=-1)
        out = jnp.einsum('bhqk,bkhd->bqhd', attn, v)
        out = out.reshape(B, Sq, H * D)
        return out @ Wo

    def _L1_ffn_ref(x, w1, w2):
        import jax, jax.numpy as jnp
        import numpy as np
        D_MODEL = 512
        D_HIDDEN = 2048
        EPS = 1e-05

        def activation_quant(x):
            scale = 127.0 / jnp.clip(jnp.max(jnp.abs(x), axis=-1, keepdims=True), EPS, None)
            return jnp.clip(jnp.round(x * scale), -128, 127) / scale

        def weight_quant(w):
            scale = 1.0 / jnp.clip(jnp.mean(jnp.abs(w)), EPS, None)
            return jnp.clip(jnp.round(w * scale), -1, 1) / scale

        def bitlinear(x, w):
            xq = x + jax.lax.stop_gradient(activation_quant(x) - x)
            wq = w + jax.lax.stop_gradient(weight_quant(w) - w)
            return jnp.einsum('bsi,oi->bso', xq, wq)
        h = bitlinear(x, w1)
        h = jax.nn.gelu(h, approximate=False)
        return bitlinear(h, w2)
    x = x + _L0_xattn_ref(ctx_1024, _layernorm(x, axis=-1), L0_xattn_in_proj_w, L0_xattn_conv_w, L0_xattn_conv_b, L0_xattn_x_proj_w, L0_xattn_dt_proj_w, L0_xattn_dt_proj_b, L0_xattn_A_log, L0_xattn_D)
    x = x + _L0_ffn_ref(_layernorm(x, axis=-1), L0_ffn_gate_weight, L0_ffn_gate_up_proj, L0_ffn_down_proj, L0_ffn_similarity)
    x = x + _L1_xattn_ref(_layernorm(x, axis=-1), ctx_1024, L1_xattn_Wq, L1_xattn_Wk, L1_xattn_Wv, L1_xattn_Wo, L1_xattn_gq, L1_xattn_gk)
    x = x + _L1_ffn_ref(_layernorm(x, axis=-1), L1_ffn_w1, L1_ffn_w2)
    return x

_drawn_inputs = setup_inputs


def setup_inputs(seed=0):
    import zlib

    import numpy as np

    out = dict(_drawn_inputs(seed))
    spreads = {'L0_xattn_conv_b': (0.0, 0.1),
     'L0_xattn_D': (1.0, 0.2),
     'L1_xattn_gq': (1.0, 0.6),
     'L1_xattn_gk': (1.0, 0.6)}
    factors = {'L0_xattn_dt_proj_w': 4.645,
     'L0_ffn_gate_weight': 4.713,
     'L0_ffn_gate_up_proj': 4.403,
     'L0_ffn_down_proj': 4.395}
    for name, (base, spread) in spreads.items():
        noise = np.random.default_rng([zlib.crc32(name.encode()), seed]).standard_normal(out[name].shape)
        drawn = base * np.exp(spread * noise) if base else spread * noise
        out[name] = jnp.asarray(drawn.astype(out[name].dtype))
    for name, factor in factors.items():
        out[name] = (out[name] * factor).astype(out[name].dtype)
    return out
```

```python
import concourse.bass as bass
from concourse import mybir
from contextlib import ExitStack

FP32 = mybir.dt.float32
BF16 = mybir.dt.bfloat16
I32 = mybir.dt.int32
U32 = mybir.dt.uint32
ALU = mybir.AluOpType
ACT = mybir.ActivationFunctionType
AX = mybir.AxisListType

P = 128
BATCH, SEQ, DM = 4, 512, 512
ST = SEQ // P
NT = BATCH * ST
EPS = 1e-5

CD = 256
KC = CD // P
DI = 512
EC = DI // P
DS = 16
DR = 16
TAPS = 4
G = 2
NG = DS // G

NE, TOPK, SELK, THRESH = 64, 8, 4, 0.5
FI = 192
KD = DM // P
MAXT = BATCH * SEQ * TOPK // P + NE
MINT = BATCH * SEQ * TOPK // P
FILLS, FILL, FILL_Y = BATCH * NG // 2 - 1, 14, 5
T_END, T_PAIRS = 2 * P, 2 * P + NE

NH, HD, HG = 16, 128, 4
NGRP = BATCH * NH // HG

DF = 2048
KF = DF // P
FN = DM * DF // P
MAGIC = 1.5 * 2.0 ** 23
QMAX = 127.0


def ds1(i):
    return bass.ds(i, 1)


def pool_waits(pool, c, sem, value):
    pool.wait_ge(sem, value).then_inc(c.pool_passed, 1)


class Pipe:

    def __init__(self, nc, ctx):
        self.nc, self.ctx = nc, ctx

    def sb(self, name, shape, dt=FP32):
        return self.ctx.enter_context(self.nc.sbuf_tensor(name, shape, dt))

    def ps(self, name, shape, dt=FP32):
        return self.ctx.enter_context(self.nc.psum_tensor(name, shape, dt))

    def sem(self, name):
        return self.nc.alloc_semaphore(name)


def load_constants(nc, c, d):
    x_loaded = nc.alloc_semaphore("x_loaded")
    const_made = c.const_made
    with nc.Block() as block:
        @block.sync
        def _(sp):
            sp.dma_start(c.X[:, :, :], d["x"].rearrange("(t p) n -> p t n", p=P)).then_inc(x_loaded, 16)
            sp.wait_ge(x_loaded, 16)

        @block.gpsimd
        def _(pool):
            pool.memset(c.ident[:, :], 0.0).then_inc(const_made, 1)
            pool.memset(c.power[:, :], -0.5)
            pool.wait_ge(const_made, 1)
            pool.affine_select(out=c.ident[:, :], in_=c.ident[:, :], compare_op=ALU.not_equal, fill=1.0,
                               base=0, pattern=[[-1, P]], channel_multiplier=1).then_inc(const_made, 1)


def norm_statistics(nc, c, tag):
    with ExitStack() as ctx:
        p = Pipe(nc, ctx)
        block = ctx.enter_context(nc.Block())
        bn6, bn2 = p.sb(f"{tag}_bn6", [P, NT, 6]), p.sb(f"{tag}_bn2", [P, NT, 2])
        vare = p.sb(f"{tag}_vare", [P, NT])
        stats_made, aggregated = p.sem(f"{tag}_stats_made"), p.sem(f"{tag}_aggregated")
        eps_added, rooted = p.sem(f"{tag}_eps_added"), p.sem(f"{tag}_rooted")

        @block.vector
        def _(dve):
            with dve.Fori(0, NT) as t:
                dve.bn_stats(bn6[:, ds1(t), :].rearrange("p a b -> p (a b)"),
                             c.X[:, ds1(t), :].rearrange("p a b -> p (a b)")).then_inc(stats_made, 1)
            dve.wait_ge(stats_made, NT)
            for t in range(NT):
                aggr = dve.bn_aggr(bn2[:, t, :], bn6[:, t, :])
            aggr.then_inc(aggregated, 1)
            dve.wait_ge(aggregated, 1)
            dve.tensor_scalar(out=vare[:, :], in0=bn2[:, :, 1], scalar1=EPS, scalar2=None,
                              op0=ALU.add).then_inc(eps_added, 1)
            dve.wait_ge(rooted, 1)
            dve.scalar_tensor_tensor(out=c.nbias[:, :], in0=bn2[:, :, 0], scalar=-1.0, in1=c.rstd[:, :],
                                     op0=ALU.mult, op1=ALU.mult)

        @block.gpsimd
        def _(pool):
            pool.wait_ge(eps_added, 1)
            pool.tensor_tensor(out=c.rstd[:, :], in0=vare[:, :], in1=c.power[:, 0:NT],
                               op=ALU.pow).then_inc(rooted, 1)


def ssm_inputs(nc, c, m, d):
    with ExitStack() as ctx:
        p = Pipe(nc, ctx)
        block = ctx.enter_context(nc.Block())
        w_in = p.sb("w_in", [P, KC, DI])
        w_x = p.sb("w_x", [P, EC, DR + 2 * DS])
        w_dt = p.sb("w_dt", [DR, DI])
        conv_w = p.sb("conv_w", [P, EC, TAPS])
        conv_b = p.sb("conv_b", [P, EC])
        dt_b = p.sb("dt_b", [P, EC])
        a_log = p.sb("a_log", [P, EC * DS])
        d_skip = p.sb("d_skip", [P, EC])
        ctx_t = p.sb("ctx_t", [P, BATCH * KC, SEQ])
        x_pad = p.sb("x_pad", [P, EC, SEQ + TAPS - 1])
        conv = p.sb("conv", [P, EC, SEQ])
        dbc = p.sb("dbc", [DR + 2 * DS, SEQ])
        pos = p.sb("pos", [P, EC, SEQ])
        mag = p.sb("mag", [P, EC, SEQ])
        log1 = p.sb("log1", [P, EC, SEQ])
        den = conv
        ps_a = [p.ps(f"ps_a{i}", [P, SEQ]) for i in range(EC)]
        ps_x = p.ps("ps_x", [DR + 2 * DS, SEQ])
        small_loaded, ctx_loaded = p.sem("small_loaded"), p.sem("ctx_loaded")
        x_made, x_copied, padded = p.sem("x_made"), p.sem("x_copied"), p.sem("padded")
        conv_step, conv_done, u_made = p.sem("conv_step"), p.sem("conv_done"), p.sem("u_made")
        dbc_made, dbc_copied, dbc_stored = p.sem("dbc_made"), p.sem("dbc_copied"), p.sem("dbc_stored")
        mag_made = p.sem("mag_made")
        v_made, v_taken = p.sem("v_made"), p.sem("v_taken")
        exp_made, log_made = p.sem("exp_made"), p.sem("log_made")
        den_made, recip_made, ratio_made = p.sem("den_made"), p.sem("recip_made"), p.sem("ratio_made")
        sp_step, delta_made, a_exp = p.sem("sp_step"), p.sem("delta_made"), p.sem("a_exp")

        @block.sync
        def _(sp):
            col = lambda v: v.rearrange("(c p) -> p c", p=P)
            sp.dma_start(w_in[:, :, :], d["in_proj"].rearrange("(c p) e -> p c e", p=P)).then_inc(small_loaded, 16)
            sp.dma_start(ctx_t[:, :, :], d["ctx_t"].rearrange("(k p) l -> p k l", p=P)).then_inc(ctx_loaded, 16)
            sp.dma_start(w_x[:, :, :], d["x_proj"].rearrange("(c p) e -> p c e", p=P)).then_inc(small_loaded, 16)
            sp.dma_start(w_dt[:, :], d["dt_proj"]).then_inc(small_loaded, 16)
            sp.dma_start(conv_w[:, :, :], d["conv_w"].rearrange("(c p) k -> p c k", p=P)).then_inc(small_loaded, 16)
            with nc.allow_non_contiguous_dma(reason="one value a partition"):
                sp.dma_start(conv_b[:, :], col(d["conv_b"])).then_inc(small_loaded, 16)
                sp.dma_start(dt_b[:, :], col(d["dt_b"])).then_inc(small_loaded, 16)
                sp.dma_start(d_skip[:, :], col(d["d_skip"])).then_inc(small_loaded, 16)
            sp.dma_start(a_log[:, :].rearrange("p (c n) -> p c n", n=DS),
                         d["a_log"].rearrange("(c p) n -> p c n", p=P)).then_inc(small_loaded, 16)
            sp.sem_inc(dbc_stored, 16)
            with sp.Fori(0, BATCH) as b:
                sp.wait_ge(dbc_copied, b + 1)
                sp.dma_start(m.bc_dram[ds1(b), :, :].rearrange("a n l -> (a n) l"),
                             dbc[DR:DR + 2 * DS, :]).then_inc(dbc_stored, 16)
            sp.wait_ge(dbc_stored, 16 * BATCH + 16)

        @block.tensor
        def _(pe):
            pe.wait_ge(small_loaded, 128)
            pe.wait_ge(ctx_loaded, 16)
            with pe.Fori(0, BATCH) as b:
                pe.wait_ge(v_taken, b * EC + 1)
                pe.wait_ge(exp_made, b + 1)
                for ec in range(EC):
                    for k in range(KC):
                        mm = pe.matmul(ps_a[ec][:, :], w_in[:, k, ec * P:(ec + 1) * P],
                                       ctx_t[:, ds1(b * KC + k), :].rearrange("p a l -> p (a l)"),
                                       start=k == 0, stop=k == KC - 1)
                    mm.then_inc(x_made, 1)
                pe.wait_ge(u_made, b + 1)
                for ec in range(EC):
                    mm = pe.matmul(ps_x[:, :], w_x[:, ec, :],
                                   m.u[:, ds1(b * EC + ec), :].rearrange("p a l -> p (a l)"),
                                   start=ec == 0, stop=ec == EC - 1)
                mm.then_inc(dbc_made, 1)
                pe.wait_ge(dbc_copied, b + 1)
                for ec in range(EC):
                    mm = pe.matmul(ps_a[ec][:, :], w_dt[:, ec * P:(ec + 1) * P], dbc[0:DR, :],
                                   start=True, stop=True)
                mm.then_inc(v_made, 1)

        @block.scalar
        def _(act):
            act.wait_ge(small_loaded, 128)
            act.activation(m.a_neg[:, :], a_log[:, :], ACT.Exp).then_inc(a_exp, 1)
            with act.Fori(0, BATCH) as b:
                act.wait_ge(conv_done, b * EC + 1)
                for ec in range(EC):
                    act.wait_ge(x_made, b * EC + ec + 1)
                    act.activation(x_pad[:, ec, TAPS - 1:], ps_a[ec][:, :], ACT.Copy).then_inc(x_copied, 1)
                for ec in range(EC):
                    act.wait_ge(conv_done, b * EC + ec + 2)
                    u = act.activation(m.u[:, ds1(b * EC + ec), :].rearrange("p a l -> p (a l)"), conv[:, ec, :],
                                       ACT.Silu, bias=conv_b[:, ec:ec + 1])
                u.then_inc(u_made, 1)
                act.wait_ge(dbc_made, b + 1)
                act.wait_ge(dbc_stored, b * 16 + 16)
                act.activation(dbc[:, :], ps_x[:, :], ACT.Copy).then_inc(dbc_copied, 1)
                act.wait_ge(delta_made, b + 1)
                for ec in range(EC):
                    act.wait_ge(v_taken, b * EC + ec + 2)
                    v = act.activation(mag[:, ec, :], ps_a[ec][:, :], ACT.Abs, bias=dt_b[:, ec:ec + 1])
                v.then_inc(mag_made, 1)
                act.wait_ge(mag_made, b + 1)
                act.activation(mag[:, :, :], mag[:, :, :], ACT.Exp, scale=-1.0).then_inc(exp_made, 1)
                act.wait_ge(exp_made, b + 2)
                act.activation(log1[:, :, :], mag[:, :, :], ACT.Ln, bias=1.0).then_inc(log_made, 1)

        @block.vector
        def _(dve):
            dve.sem_inc(v_taken, 1)
            dve.sem_inc(ratio_made, 1)
            dve.sem_inc(exp_made, 1)
            dve.sem_inc(conv_done, 1)
            dve.memset(x_pad[:, :, 0:TAPS - 1], 0.0).then_inc(padded, 1)
            dve.wait_ge(a_exp, 1)
            dve.tensor_scalar(out=m.a_neg[:, :], in0=m.a_neg[:, :], scalar1=-1.0, scalar2=None,
                              op0=ALU.mult)
            for ec in range(EC):
                dve.tensor_scalar(out=m.d_diag[:, ec, :], in0=c.ident[:, :], scalar1=d_skip[:, ec:ec + 1],
                                  scalar2=None, op0=ALU.mult)
            dve.memset(m.d_a[:, :, :, 0:1], 0.0)
            dve.memset(m.zero2[:, :], 0.0)
            dve.memset(m.zeros[:, :], 0.0)
            dve.wait_ge(padded, 1)
            with dve.Fori(0, BATCH) as b:
                dve.wait_ge(ratio_made, b + 1)
                for ec in range(EC):
                    dve.wait_ge(x_copied, b * EC + ec + 1)
                    dve.tensor_scalar(out=conv[:, ec, :], in0=x_pad[:, ec, 0:SEQ], scalar1=conv_w[:, ec, 0:1],
                                      scalar2=None, op0=ALU.mult).then_inc(conv_step, 1)
                for k in range(1, TAPS):
                    for ec in range(EC):
                        dve.wait_ge(conv_step, b * (TAPS - 1) * EC + (k - 1) * EC + ec + 1)
                        dve.scalar_tensor_tensor(out=conv[:, ec, :], in0=x_pad[:, ec, k:k + SEQ],
                                                 scalar=conv_w[:, ec, k:k + 1], in1=conv[:, ec, :],
                                                 op0=ALU.mult, op1=ALU.add)\
                            .then_inc(conv_done if k == TAPS - 1 else conv_step, 1)
                dve.wait_ge(v_made, b + 1)
                dve.wait_ge(delta_made, b + 1)
                for ec in range(EC):
                    dve.tensor_scalar(out=pos[:, ec, :], in0=ps_a[ec][:, :], scalar1=dt_b[:, ec:ec + 1],
                                          scalar2=0.0, op0=ALU.add, op1=ALU.max).then_inc(v_taken, 1)
                dve.wait_ge(den_made, 2 * b + 2)
                dve.reciprocal(den[:, :, :], den[:, :, :]).then_inc(recip_made, 1)
                dve.wait_ge(recip_made, b + 1)
                dve.wait_ge(log_made, b + 1)
                dve.scalar_tensor_tensor(out=log1[:, :, :].rearrange("p a l -> p (a l)"),
                                         in0=log1[:, :, :].rearrange("p a l -> p (a l)"), scalar=1e-30,
                                         in1=den[:, :, :].rearrange("p a l -> p (a l)"),
                                         op0=ALU.max, op1=ALU.mult).then_inc(ratio_made, 1)

        @block.gpsimd
        def _(pool):
            pool.sem_inc(delta_made, 1)
            with pool.Fori(0, BATCH) as b:
                pool_waits(pool, c, exp_made, b + 2)
                pool.tensor_scalar(out=den[:, :, :], in0=mag[:, :, :], scalar1=1.0, scalar2=-1.0,
                                   op0=ALU.add, op1=ALU.add).then_inc(den_made, 1)
                pool_waits(pool, c, den_made, 2 * b + 1)
                pool.tensor_scalar(out=den[:, :, :], in0=den[:, :, :], scalar1=1e-30, scalar2=None,
                                   op0=ALU.max).then_inc(den_made, 1)
                pool_waits(pool, c, ratio_made, b + 2)
                pool.tensor_tensor(out=log1[:, :, :], in0=log1[:, :, :], in1=mag[:, :, :],
                                   op=ALU.mult).then_inc(sp_step, 1)
                pool_waits(pool, c, sp_step, 2 * b + 1)
                pool.tensor_tensor(out=m.delta[:, bass.ds(b * EC, EC), :], in0=log1[:, :, :], in1=pos[:, :, :],
                                   op=ALU.add).then_inc(sp_step, 1)
                pool_waits(pool, c, sp_step, 2 * b + 2)
                pool.tensor_tensor(out=m.du[:, bass.ds(b * EC, EC), :], in0=m.delta[:, bass.ds(b * EC, EC), :],
                                   in1=m.u[:, bass.ds(b * EC, EC), :], op=ALU.mult).then_inc(delta_made, 1)


def ssm_scan(nc, c, m):
    with ExitStack() as ctx:
        p = Pipe(nc, ctx)
        block = ctx.enter_context(nc.Block())
        bc = p.sb("bc", [P, 2, 2, G, SEQ])
        b_u = p.sb("b_u", [P, 2, G, SEQ])
        state = p.sb("state", [P, 2, G * SEQ])
        c_state = p.sb("c_state", [P, 2, G, SEQ])
        gate = p.sb("gate", [P, EC, SEQ])
        gated = p.sb("gated", [P, EC, SEQ])
        ps_y = [p.ps(f"ps_y{i}", [P, SEQ]) for i in range(EC)]
        ps_t = [p.ps(f"ps_t{i}", [P, DM]) for i in range(ST)]
        filled = p.sem("filled")
        bc_loaded = [p.sem("bc_loaded0"), p.sem("bc_loaded1")]
        decay_made, input_made = p.sem("decay_made"), p.sem("input_made")
        scanned, product_made, product_used = p.sem("scanned"), p.sem("product_made"), p.sem("product_used")
        y_summed, y_gated, gate_made = p.sem("y_summed"), p.sem("y_gated"), p.sem("gate_made")
        y_turned, x_added = p.sem("y_turned"), p.sem("x_added")

        def rows(k, ng, n):
            return m.bc_dram[k, n * DS + ng * G:n * DS + ng * G + G, :]

        @block.sync
        def _(sp):
            def load(k, par, b, ng):
                for n in range(2):
                    src = m.bc_dram[ds1(b), bass.ds(n * DS + ng * G, G), :]\
                        .rearrange("a n l -> a (n l)").broadcast_to([P, G * SEQ])
                    sp.dma_start(bc[:, par, n, :, :].rearrange("p g l -> p (g l)"), src)\
                        .then_inc(bc_loaded[par], 16)
            for k in range(2):
                load(k, k, 0, k)
            with sp.Fori(1, BATCH * NG // 2) as k2:
                for par in range(2):
                    k = k2 * 2 + par
                    sp.wait_ge(product_made, (k - 1) * EC + 2)
                    load(k, par, k // NG, k % NG)
                for dram, skip, n in ((m.rows_dram, 0, FILL), (m.y_dram, MINT, FILL_Y)):
                    sp.dma_start(dram[bass.ds((k2 - 1) * (n * P) + skip * P, n * P), :]
                                 .rearrange("(t p) n -> p t n", p=P),
                                 m.zeros[:, :].rearrange("p (a n) -> p a n", a=1).broadcast_to([P, n, DM]))\
                        .then_inc(filled, 16)
            sp.wait_ge(filled, 2 * 16 * FILLS)

        @block.scalar
        def _(act):
            with act.Fori(0, BATCH) as b:
                with act.Fori(0, NG) as ng:
                    for ec in range(EC):
                        q = (b * NG + ng) * EC + ec
                        act.wait_ge(scanned, q + 1)
                        for g in range(G):
                            e = act.activation(m.d_a[:, ec % 2, g, 1:], m.delta[:, ds1(b * EC + ec), 1:].rearrange("p a l -> p (a l)"),
                                               ACT.Exp, scale=m.a_neg[:, ds1(ec * DS + ng * G + g)])
                        e.then_inc(decay_made, 1)
                act.wait_ge(y_gated, b * EC + EC)
                for ec in range(EC):
                    t = b * ST + ec
                    g = act.activation(gate[:, ec, :], c.X[:, ds1(t), :].rearrange("p a l -> p (a l)"), ACT.Silu,
                                       scale=c.rstd[:, ds1(t)], bias=c.nbias[:, ds1(t)])
                g.then_inc(gate_made, 1)

        @block.gpsimd
        def _(pool):
            with pool.Fori(0, BATCH) as b:
                with pool.Fori(0, NG // 2) as n2:
                    for par in range(2):
                        pool_waits(pool, c, bc_loaded[par], (b * (NG // 2) + n2) * 32 + 32)
                        for ec in range(EC):
                            q = (b * NG + n2 * 2 + par) * EC + ec
                            pool_waits(pool, c, scanned, q + 1)
                            pool.tensor_tensor(out=b_u[:, ec % 2, :, :],
                                               in0=m.du[:, ds1(b * EC + ec), :].broadcast_to([P, G, SEQ]),
                                               in1=bc[:, par, 0, :, :], op=ALU.mult).then_inc(input_made, 1)

        @block.vector
        def _(dve):
            dve.sem_inc(scanned, 2)
            dve.sem_inc(product_made, 2)
            dve.sem_inc(y_gated, EC)
            dve.sem_inc(x_added, 1)
            with dve.Fori(0, BATCH) as b:
                with dve.Fori(0, NG // 2) as n2:
                    for par in range(2):
                        q0 = (b * NG + n2 * 2 + par) * EC
                        dve.wait_ge(bc_loaded[par], (b * (NG // 2) + n2) * 32 + 32)

                        def scan(ec):
                            dve.wait_ge(decay_made, q0 + ec + 1)
                            dve.wait_ge(input_made, q0 + ec + 1)
                            dve.wait_ge(product_made, q0 + ec + 1)
                            dve.tensor_tensor_scan(state[:, ec % 2, :],
                                                   m.d_a[:, ec % 2, :, :].rearrange("p g l -> p (g l)"),
                                                   b_u[:, ec % 2, :, :].rearrange("p g l -> p (g l)"),
                                                   0.0, ALU.mult, ALU.add).then_inc(scanned, 1)

                        def product(ec):
                            dve.wait_ge(scanned, q0 + ec + 3)
                            dve.wait_ge(product_used, q0 + ec + 1)
                            dve.tensor_tensor(out=c_state[:, ec % 2, :, :],
                                              in0=state[:, ec % 2, :].rearrange("p (g l) -> p g l", g=G),
                                              in1=bc[:, par, 1, :, :], op=ALU.mult).then_inc(product_made, 1)

                        scan(0)
                        for ec in range(1, EC):
                            scan(ec)
                            product(ec - 1)
                        product(EC - 1)
                dve.wait_ge(gate_made, b + 1)
                for ec in range(EC):
                    dve.wait_ge(y_summed, b * EC + ec + 1)
                    dve.tensor_tensor(out=gated[:, ec, :], in0=ps_y[ec][:, :], in1=gate[:, ec, :],
                                      op=ALU.mult).then_inc(y_gated, 1)
                dve.wait_ge(y_turned, b + 1)
                for j in range(ST):
                    xt = c.X[:, ds1(b * ST + j), :].rearrange("p a l -> p (a l)")
                    add = dve.tensor_tensor(out=xt, in0=ps_t[j][:, :], in1=xt, op=ALU.add)
                add.then_inc(x_added, 1)

        @block.tensor
        def _(pe):
            pe.sem_inc(product_used, 2)
            with pe.Fori(0, BATCH) as b:
                for ec in range(EC):
                    pe.wait_ge(y_gated, b * EC + ec + 1)
                    pe.matmul(ps_y[ec][:, :], m.d_diag[:, ec, :], m.u[:, ds1(b * EC + ec), :].rearrange("p a l -> p (a l)"),
                              start=True, stop=False)
                with pe.Fori(0, NG) as ng:
                    for ec in range(EC):
                        pe.wait_ge(product_made, (b * NG + ng) * EC + ec + 3)
                        for g in range(G):
                            mm = pe.matmul(ps_y[ec][:, :], c.ident[:, :], c_state[:, ec % 2, g, :],
                                           start=False, stop=False)
                        mm.then_inc(product_used, 1)
                for ec in range(EC):
                    pe.matmul(ps_y[ec][:, 0:2], c.ident[:, :], m.zero2[:, :], start=False, stop=True)\
                        .then_inc(y_summed, 1)
                pe.wait_ge(x_added, b + 1)
                for ec in range(EC):
                    pe.wait_ge(y_gated, b * EC + EC + ec + 1)
                    for j in range(ST):
                        tr = pe.transpose(ps_t[j][:, ec * P:(ec + 1) * P], gated[:, ec, j * P:(j + 1) * P],
                                          c.ident[:, :])
                tr.then_inc(y_turned, 1)


def router_logits(nc, c, m, d):
    with ExitStack() as ctx:
        p = Pipe(nc, ctx)
        block = ctx.enter_context(nc.Block())
        w_gate = p.sb("w_gate", [P, KD, NE])
        xn_t = p.sb("xn_t", [P, 2, KD, P])
        ps_xt = [p.ps(f"ps_xt{i}", [P, KD * P]) for i in range(2)]
        ps_l = [p.ps(f"ps_l{i}", [P, NE]) for i in range(2)]
        gate_loaded, normed = p.sem("gate_loaded"), p.sem("normed")
        xn_turned, xn_t_made = p.sem("xn_turned"), p.sem("xn_t_made")
        logits_made, logits_kept = p.sem("logits_made"), p.sem("logits_kept")

        @block.sync
        def _(sp):
            sp.dma_start(w_gate[:, :, :], d["gate_w"].rearrange("(k p) e -> p k e", p=P)).then_inc(gate_loaded, 16)
            sp.dma_start(m.sim[:, :], d["similarity"]).then_inc(m.sim_loaded, 16)

        @block.vector
        def _(dve):
            with dve.Fori(0, NT) as t:
                row = lambda x: x[:, ds1(t), :].rearrange("p a l -> p (a l)")
                dve.tensor_scalar(out=row(m.xn), in0=row(c.X), scalar1=c.rstd[:, ds1(t)],
                                  scalar2=c.nbias[:, ds1(t)], op0=ALU.mult, op1=ALU.add).then_inc(normed, 1)

        @block.tensor
        def _(pe):
            pe.wait_ge(gate_loaded, 16)
            for t in range(NT + 1):
                if t < NT:
                    pe.wait_ge(normed, t + 1)
                    if t >= 2:
                        pe.wait_ge(xn_t_made, t - 1)
                    for k in range(KD):
                        tr = pe.transpose(ps_xt[t % 2][:, k * P:(k + 1) * P], m.xn[:, t, k * P:(k + 1) * P],
                                          c.ident[:, :])
                    tr.then_inc(xn_turned, 1)
                if t >= 1:
                    s = t - 1
                    pe.wait_ge(xn_t_made, s + 1)
                    if s >= 2:
                        pe.wait_ge(logits_kept, s - 1)
                    for k in range(KD):
                        mm = pe.matmul(ps_l[s % 2][:, :], xn_t[:, s % 2, k, :], w_gate[:, k, :],
                                       start=k == 0, stop=k == KD - 1)
                    mm.then_inc(logits_made, 1)

        @block.scalar
        def _(act):
            for t in range(NT + 1):
                if t < NT:
                    act.wait_ge(xn_turned, t + 1)
                    if t >= 2:
                        act.wait_ge(logits_made, t - 1)
                    act.activation(xn_t[:, t % 2, :, :].rearrange("p k l -> p (k l)"), ps_xt[t % 2][:, :],
                                   ACT.Copy).then_inc(xn_t_made, 1)
                if t >= 1:
                    act.wait_ge(logits_made, t)
                    act.activation(m.logits[:, t - 1, :], ps_l[(t - 1) % 2][:, :], ACT.Copy)\
                        .then_inc(logits_kept, 1)


def route(nc, c, m):
    with ExitStack() as ctx:
        p = Pipe(nc, ctx)
        block = ctx.enter_context(nc.Block())
        iota_e = p.sb("iota_e", [P, NT, NE])
        tile_no = p.sb("tile_no", [P, 2])
        expert_no = p.sb("expert_no", [NE, 1])
        ones = p.sb("ones", [P, P], BF16)
        before = p.sb("before", [P, P], BF16)
        line1 = p.sb("line1", [P, NE])
        most, total = p.sb("most", [P, NT]), p.sb("total", [P, NT])
        top = p.sb("top", [P, NT, TOPK])
        idx = p.sb("idx", [P, NT, TOPK], U32)
        idx_f = p.sb("idx_f", [P, NT, TOPK])
        chosen = p.sb("chosen", [P, TOPK, NT, NE], BF16)
        tmp = p.sb("tmp", [P, NT, NE])
        first = p.sb("first", [P, NT, NE], BF16)
        second = p.sb("second", [P, NT, NE], BF16)
        ahead = p.sb("ahead", [P, NT + 1, NE], BF16)
        mask, cand = p.sb("mask", [NE, NE]), p.sb("cand", [NE, NE])
        best8, best_i = p.sb("best8", [NE, 8]), p.sb("best_i", [NE, 8], U32)
        r1, r2 = p.sb("r1", [NE, 1]), p.sb("r2", [NE, 1])
        map_col, map_b = p.sb("map_col", [NE, 1]), p.sb("map_b", [NE, P])
        map_row = p.sb("map_row", [P, NE])
        cnt_i, tiles = p.sb("cnt_i", [P, NE], I32), p.sb("tiles", [P, NE])
        end, base = p.sb("end", [P, NE]), p.sb("base", [P, NE])
        row_of = p.sb("row_of", [P, NT, NE])
        pos_f = p.sb("pos_f", [P, TOPK, NT])
        lt = p.sb("lt", [P, 2, NE])
        te = p.sb("te", [P, 2])
        ps_first = p.ps("ps_first", [P, NE])
        ps_fc, ps_sc = p.ps("ps_fc", [NE, 1]), p.ps("ps_sc", [NE, 1])
        ps_map = p.ps("ps_map", [P, NE])
        ps_row = [p.ps(f"ps_row{i}", [P, NT * NE // 2]) for i in range(2)]
        ps_cnt = p.ps("ps_cnt", [P, NE])
        ps_te = p.ps("ps_te", [1, 2 * P])
        consts, dve_step, exp_done = p.sem("consts"), p.sem("dve_step"), p.sem("exp_done")
        shifted, chosen_made, counted = p.sem("shifted"), p.sem("chosen_made"), p.sem("counted")
        mapped, map_spread, all_made = p.sem("mapped"), p.sem("map_spread"), p.sem("all_made")
        rows_made, te_made, te_turned = p.sem("rows_made"), p.sem("te_made"), p.sem("te_turned")
        diag_set = p.sem("diag_set")
        H = NT // 2

        @block.gpsimd
        def _(pool):
            pool.memset(before[:, :], 1.0).then_inc(diag_set, 1)
            pool.iota(iota_e[:, :, :], pattern=[[0, NT], [1, NE]], base=0, channel_multiplier=0,
                      allow_small_or_imprecise_dtypes=True)
            pool.iota(tile_no[:, :], pattern=[[P, 2]], base=0, channel_multiplier=1,
                      allow_small_or_imprecise_dtypes=True)
            pool.iota(expert_no[:, :], pattern=[[0, 1]], base=0, channel_multiplier=1,
                      allow_small_or_imprecise_dtypes=True)
            pool.memset(ones[:, :], 1.0)
            pool.memset(line1[:, :], 1.0)
            pool.memset(ahead[:, 0, :], 0.0)
            pool.wait_ge(diag_set, 1)
            pool.affine_select(out=before[:, :], in_=before[:, :], compare_op=ALU.is_gt, fill=0.0,
                               base=0, pattern=[[1, P]], channel_multiplier=-1)
            pool.wait_ge(m.sim_loaded, 16)
            pool.affine_select(out=m.sim[:, :], in_=m.sim[:, :], compare_op=ALU.not_equal, fill=1.0,
                               base=0, pattern=[[-1, NE]], channel_multiplier=1).then_inc(consts, 1)

        @block.scalar
        def _(act):
            act.wait_ge(shifted, 1)
            act.activation(m.logits[:, :, :], m.logits[:, :, :], ACT.Exp).then_inc(exp_done, 1)

        @block.vector
        def _(dve):
            n = [0]

            def link(ins):
                n[0] += 1
                ins.then_inc(dve_step, 1)
                dve.wait_ge(dve_step, n[0])

            def spread(x, last=NE):
                return x.rearrange("p (a b) -> p a b", b=1).broadcast_to([x.shape[0], x.shape[1], last])

            link(dve.tensor_reduce(most[:, :], m.logits[:, :, :], AX.X, ALU.max))
            dve.tensor_tensor(out=m.logits[:, :, :], in0=m.logits[:, :, :], in1=spread(most[:, :]),
                              op=ALU.subtract).then_inc(shifted, 1)
            dve.wait_ge(exp_done, 1)
            link(dve.tensor_reduce(total[:, :], m.logits[:, :, :], AX.X, ALU.add))
            link(dve.reciprocal(total[:, :], total[:, :]))
            link(dve.tensor_tensor(out=m.logits[:, :, :], in0=m.logits[:, :, :], in1=spread(total[:, :]),
                                   op=ALU.mult))
            for t in range(NT):
                mx = dve.max(top[:, t, :], m.logits[:, t, :])
            link(mx)
            for t in range(NT):
                mi = dve.max_index(idx[:, t, :], top[:, t, :], m.logits[:, t, :])
            link(mi)
            link(dve.tensor_reduce(total[:, :], top[:, :, :], AX.X, ALU.add))
            link(dve.tensor_scalar(out=total[:, :], in0=total[:, :], scalar1=1e-12, scalar2=None, op0=ALU.max))
            link(dve.reciprocal(total[:, :], total[:, :]))
            link(dve.tensor_tensor(out=m.weight[:, :, :], in0=top[:, :, :], in1=spread(total[:, :], TOPK),
                                   op=ALU.mult))
            link(dve.tensor_copy(idx_f[:, :, :], idx[:, :, :]))
            dve.wait_ge(consts, 1)

            def one_hot(k):
                return dve.tensor_tensor(out=chosen[:, k, :, :], in0=spread(idx_f[:, :, k]),
                                         in1=iota_e[:, :, :], op=ALU.is_equal)

            for k in range(TOPK):
                oh = one_hot(k)
            link(oh)

            def add(out, a, b):
                return dve.tensor_tensor(out=out, in0=a, in1=b, op=ALU.add)

            for out, k0 in ((first, 0), (second, SELK)):
                link(add(out[:, :, :], chosen[:, k0, :, :], chosen[:, k0 + 1, :, :]))
                link(add(out[:, :, :], out[:, :, :], chosen[:, k0 + 2, :, :]))
                link(add(out[:, :, :], out[:, :, :], chosen[:, k0 + 3, :, :]))
            dve.sem_inc(chosen_made, 1)
            dve.wait_ge(counted, 1)
            link(dve.tensor_scalar(out=mask[:, :], in0=ps_first[0:NE, :], scalar1=1.0, scalar2=None,
                                   op0=ALU.min))
            link(dve.tensor_tensor(out=cand[:, :], in0=m.sim[:, :], in1=mask[:, :], op=ALU.mult))
            link(dve.tensor_scalar(out=mask[:, :], in0=mask[:, :], scalar1=-1.0, scalar2=1e30,
                                   op0=ALU.add, op1=ALU.mult))
            link(add(cand[:, :], cand[:, :], mask[:, :]))
            link(dve.max(best8[:, :], cand[:, :]))
            link(dve.max_index(best_i[:, :], best8[:, :], cand[:, :]))
            link(dve.tensor_copy(map_col[:, :], best_i[:, 0:1]))
            link(dve.tensor_scalar(out=r1[:, :], in0=ps_fc[:, :], scalar1=0.0, scalar2=None, op0=ALU.is_equal))
            link(dve.tensor_scalar(out=r2[:, :], in0=ps_sc[:, :], scalar1=0.0, scalar2=None, op0=ALU.is_gt))
            link(dve.tensor_tensor(out=r1[:, :], in0=r1[:, :], in1=r2[:, :], op=ALU.mult))
            link(dve.tensor_scalar(out=r2[:, :], in0=best8[:, 0:1], scalar1=THRESH, scalar2=None, op0=ALU.is_ge))
            link(dve.tensor_tensor(out=r1[:, :], in0=r1[:, :], in1=r2[:, :], op=ALU.mult))
            link(dve.tensor_tensor(out=map_col[:, :], in0=map_col[:, :], in1=expert_no[:, :], op=ALU.subtract))
            link(dve.tensor_tensor(out=map_col[:, :], in0=map_col[:, :], in1=r1[:, :], op=ALU.mult))
            link(add(map_col[:, :], map_col[:, :], expert_no[:, :]))
            dve.tensor_copy(map_b[:, :], map_col[:, :].broadcast_to([NE, P])).then_inc(mapped, 1)
            dve.wait_ge(map_spread, 1)
            link(dve.tensor_copy(map_row[:, :], ps_map[:, :]))
            map_all = map_row[:, :].rearrange("p (a e) -> p a e", a=1).broadcast_to([P, NT, NE])
            for k in range(SELK, TOPK):
                link(dve.tensor_tensor(out=tmp[:, :, :], in0=chosen[:, k, :, :], in1=map_all, op=ALU.mult))
                link(dve.tensor_reduce(idx_f[:, :, k], tmp[:, :, :], AX.X, ALU.add))
                link(one_hot(k))
            for k in range(SELK, TOPK):
                link(add(first[:, :, :], first[:, :, :], chosen[:, k, :, :]))
            for t in range(NT):
                link(add(ahead[:, t + 1, :], ahead[:, t, :], first[:, t, :]))
            dve.sem_inc(all_made, 1)
            dve.wait_ge(rows_made, 1)
            link(dve.tensor_scalar(out=cnt_i[:, :], in0=ps_cnt[:, :], scalar1=float(P - 1), scalar2=None,
                                   op0=ALU.add))
            link(dve.tensor_scalar(out=cnt_i[:, :], in0=cnt_i[:, :], scalar1=7, scalar2=None,
                                   op0=ALU.logical_shift_right))
            link(dve.tensor_scalar(out=tiles[:, :], in0=cnt_i[:, :], scalar1=1.0, scalar2=None, op0=ALU.max))
            link(dve.tensor_tensor_scan(end[:, :], line1[:, :], tiles[:, :], 0.0, ALU.mult, ALU.add))
            link(dve.tensor_tensor(out=base[:, :], in0=end[:, :], in1=tiles[:, :], op=ALU.subtract))
            link(dve.tensor_scalar(out=base[:, :], in0=base[:, :], scalar1=float(P), scalar2=None, op0=ALU.mult))
            base_all = base[:, :].rearrange("p (a e) -> p a e", a=1).broadcast_to([P, H, NE])
            for h in range(2):
                link(add(row_of[:, h * H:(h + 1) * H, :],
                         ps_row[h][:, :].rearrange("p (t e) -> p t e", e=NE), base_all))
            link(dve.tensor_tensor(out=lt[:, :, :],
                                   in0=end[:, :].rearrange("p (a e) -> p a e", a=1).broadcast_to([P, 2, NE]),
                                   in1=spread(tile_no[:, :]), op=ALU.is_le))
            link(dve.tensor_reduce(te[:, :], lt[:, :, :], AX.X, ALU.add))
            dve.tensor_scalar(out=te[:, :], in0=te[:, :], scalar1=float(NE - 1), scalar2=None,
                              op0=ALU.min).then_inc(te_made, 1)
            for k in range(TOPK):
                link(dve.tensor_tensor(out=tmp[:, :, :], in0=chosen[:, k, :, :], in1=row_of[:, :, :],
                                       op=ALU.mult))
                link(dve.tensor_reduce(pos_f[:, k, :], tmp[:, :, :], AX.X, ALU.add))
                link(add(row_of[:, :, :], row_of[:, :, :], chosen[:, k, :, :]))
            link(dve.tensor_copy(m.pos[:, :, :], pos_f[:, :, :]))
            dve.wait_ge(te_turned, 1)
            dve.tensor_copy(m.table[:, 0:2 * P], ps_te[:, :])
            dve.tensor_copy(m.table[:, T_END:T_END + NE], end[0:1, :])
            link(dve.tensor_scalar(out=cnt_i[0:1, 0:1], in0=end[0:1, NE - 1:NE], scalar1=1.0, scalar2=None,
                                   op0=ALU.add))
            dve.tensor_scalar(out=m.table[:, T_PAIRS:T_PAIRS + 1], in0=cnt_i[0:1, 0:1], scalar1=1,
                              scalar2=None, op0=ALU.logical_shift_right)

        @block.tensor
        def _(pe):
            pe.wait_ge(consts, 1)
            pe.wait_ge(chosen_made, 1)
            for t in range(NT):
                st = dict(start=t == 0, stop=t == NT - 1)
                pe.matmul(ps_first[:, :], ones[:, :], first[:, t, :], **st)
                pe.matmul(ps_fc[:, :], first[:, t, :], ones[:, 0:1], **st)
                mm = pe.matmul(ps_sc[:, :], second[:, t, :], ones[:, 0:1], **st)
            mm.then_inc(counted, 1)
            pe.wait_ge(mapped, 1)
            pe.matmul(ps_map[:, :], map_b[:, :], c.ident[0:NE, 0:NE], start=True, stop=True).then_inc(map_spread, 1)
            pe.wait_ge(all_made, 1)
            for h in range(2):
                pe.matmul(ps_row[h][:, :], before[:, :],
                          first[:, h * H:(h + 1) * H, :].rearrange("p t e -> p (t e)"), start=True, stop=False)
                pe.matmul(ps_row[h][:, :], ones[:, :],
                          ahead[:, h * H:(h + 1) * H, :].rearrange("p t e -> p (t e)"), start=False, stop=True)
            pe.matmul(ps_cnt[:, :], ones[:, :], ahead[:, NT, :], start=True, stop=True).then_inc(rows_made, 1)
            pe.wait_ge(te_made, 1)
            for h in range(2):
                mm = pe.matmul(ps_te[:, h * P:(h + 1) * P], te[:, h:h + 1], c.ident[:, :], start=True, stop=True)
            mm.then_inc(te_turned, 1)


def dispatch(nc, c, m):
    with ExitStack() as ctx:
        sent = Pipe(nc, ctx).sem("sent")
        block = ctx.enter_context(nc.Block())

        @block.gpsimd
        def _(pool):
            for t in range(NT):
                for k in range(TOPK):
                    pool.indirect_dma_start(m.rows_dram, bass.IndirectOffsetOnAxis(ap=m.pos[:, k, t:t + 1], axis=0),
                                            m.xn[:, t, :], None).then_inc(sent, 16)
            pool.wait_ge(sent, 16 * NT * TOPK)


def experts(nc, c, m, d):
    with ExitStack() as ctx:
        p = Pipe(nc, ctx)
        block = ctx.enter_context(nc.Block())
        w_gu = p.sb("w_gu", [P, 2 * KD, 2 * FI])
        w_dn = p.sb("w_dn", [FI // 2, 2 * 2, DM])
        rows = [p.sb(f"rows{i}", [P, DM]) for i in range(2)]
        rows_t = [p.sb(f"rows_t{i}", [P, KD, P]) for i in range(2)]
        silu_g = [p.sb(f"silu_g{i}", [P, FI]) for i in range(2)]
        hid = [p.sb(f"hid{i}", [P, FI]) for i in range(2)]
        hid_t = [p.sb(f"hid_t{i}", [FI // 2, 2, P]) for i in range(2)]
        y = [p.sb(f"y{i}", [P, DM]) for i in range(2)]
        ps_x = [p.ps(f"ps_rx{i}", [P, KD * P]) for i in range(2)]
        ps_gu = [p.ps(f"ps_gu{i}", [P, 2 * FI]) for i in range(2)]
        ps_h = [p.ps(f"ps_h{i}", [FI // 2, 2 * P]) for i in range(2)]
        ps_o = [p.ps(f"ps_o{i}", [P, DM]) for i in range(2)]
        w_loaded = [p.sem("w_loaded0"), p.sem("w_loaded1")]
        rows_loaded = [p.sem("rows_loaded0"), p.sem("rows_loaded1")]
        y_stored = [p.sem("y_stored0"), p.sem("y_stored1")]
        ended = p.sem("ended")
        rows_turned = p.sem("rows_turned")
        rows_t_made = p.sem("rows_t_made")
        gu_made = p.sem("gu_made")
        silu_made = p.sem("silu_made")
        hid_made = p.sem("hid_made")
        hid_turned = p.sem("hid_turned")
        hid_t_made = p.sem("hid_t_made")
        out_made = p.sem("out_made")
        y_made = p.sem("y_made")

        def pairs(eng):
            return eng.value_load(m.table[0:1, T_PAIRS:T_PAIRS + 1], min_val=NE // 2, max_val=MAXT // 2)

        @block.gpsimd
        def _(pool):
            def load(e, slot):
                pool.dma_start(w_gu[:, bass.ds(slot * KD, KD), :].rearrange("p k f -> p (k f)"),
                               d["gate_up"][ds1(e), :, :].rearrange("a p f -> (a p) f")).then_inc(w_loaded[slot], 16)
                pool.dma_start(w_dn[:, bass.ds(slot * 2, 2), :].rearrange("p k f -> p (k f)"),
                               d["down"][ds1(e), :, :].rearrange("a p f -> (a p) f")).then_inc(w_loaded[slot], 16)
            load(0, 0)
            pool.dma_start(w_dn[:, 2, :], d["down"][1, :, 0:DM]).then_inc(w_loaded[1], 32)
            pool.wait_ge(w_loaded[1], 32)
            load(1, 1)
            with pool.Fori(1, NE // 2) as e2:
                for slot in range(2):
                    done = pool.value_load(m.table[0:1, bass.ds(e2 * 2 + (T_END + slot - 2), 1)], min_val=1,
                                           max_val=MAXT)
                    pool_waits(pool, c, out_made, done + 2)
                    load(e2 * 2 + slot, slot)

        @block.sync
        def _(sp):
            np = pairs(sp)

            def load(i, par):
                sp.dma_start(rows[par][:, :], m.rows_dram[bass.ds(i * P, P), :]).then_inc(rows_loaded[par], 16)
            sp.sem_inc(y_stored[0], 16)
            sp.sem_inc(y_stored[1], 16)
            load(0, 0)
            load(1, 1)
            with sp.Fori(0, np) as j:
                for par in range(2):
                    i = j * 2 + par
                    sp.wait_ge(rows_turned, i + 1)
                    load(i + 2, par)
                    sp.wait_ge(y_made, i + 3)
                    sp.dma_start(m.y_dram[bass.ds(i * P, P), :], y[par][:, :]).then_inc(y_stored[par], 16)
            for par in range(2):
                sp.wait_ge(y_stored[par], np * 16 + 16).then_inc(ended, 1)
                sp.wait_ge(rows_loaded[par], np * 16 + 16).then_inc(ended, 1)

        @block.tensor
        def _(pe):
            for s in (gu_made, hid_turned, out_made):
                pe.sem_inc(s, 2)

            def turn_rows(i, j, par, first=False):
                pe.wait_ge(rows_loaded[par], j * 16 + 16)
                pe.wait_ge(rows_t_made, i + 1)
                for k in range(KD):
                    tr = pe.transpose(ps_x[par][:, k * P:(k + 1) * P], rows[par][:, k * P:(k + 1) * P],
                                      c.ident[:, :])
                tr.then_inc(rows_turned, 1)

            def gate_up(i, par, e):
                pe.wait_ge(w_loaded[0], (e >> 1) * 32 + 32)
                pe.wait_ge(w_loaded[1], ((e + 1) >> 1) * 32 + 32)
                pe.wait_ge(rows_t_made, i + 3)
                pe.wait_ge(hid_made, i + 1)
                for k in range(KD):
                    mm = pe.matmul(ps_gu[par][:, :], rows_t[par][:, k, :],
                                   w_gu[:, ds1((e & 1) * KD + k), :].rearrange("p a f -> p (a f)"),
                                   start=k == 0, stop=k == KD - 1)
                mm.then_inc(gu_made, 1)

            def turn_hidden(i, par):
                pe.wait_ge(hid_made, i + 3)
                pe.wait_ge(hid_t_made, i + 1)
                for k in range(2):
                    tr = pe.transpose(ps_h[par][:, k * P:(k + 1) * P],
                                      hid[par][:, k * FI // 2:(k + 1) * FI // 2], c.ident[:, :])
                tr.then_inc(hid_turned, 1)

            def down(i, par, e):
                pe.wait_ge(hid_t_made, i + 3)
                pe.wait_ge(y_made, i + 1)
                for k in range(2):
                    mm = pe.matmul(ps_o[par][:, :], hid_t[par][:, k, :],
                                   w_dn[:, ds1((e & 1) * 2 + k), :].rearrange("p a f -> p (a f)"),
                                   start=k == 0, stop=k == 1)
                mm.then_inc(out_made, 1)

            def expert(i):
                return pe.value_load(m.table[0:1, bass.ds(i, 1)], min_val=0, max_val=NE - 1)

            np = pairs(pe)
            turn_rows(0, 0, 0)
            gate_up(0, 0, expert(0))
            turn_rows(1, 0, 1)
            turn_hidden(0, 0)
            with pe.Fori(0, np) as j:
                for par in range(2):
                    i = j * 2 + par
                    gate_up(i + 1, 1 - par, expert(i + 1))
                    turn_rows(i + 2, j + 1, par)
                    down(i, par, expert(i))
                    turn_hidden(i + 1, 1 - par)

        @block.scalar
        def _(act):
            act.sem_inc(rows_t_made, 2)

            def keep_rows(i, par):
                act.wait_ge(rows_turned, i + 1)
                act.wait_ge(gu_made, i + 1)
                act.activation(rows_t[par][:, :, :].rearrange("p k l -> p (k l)"), ps_x[par][:, :],
                               ACT.Copy).then_inc(rows_t_made, 1)

            def silu(i, par):
                act.wait_ge(gu_made, i + 3)
                act.wait_ge(hid_made, i + 1)
                act.activation(silu_g[par][:, :], ps_gu[par][:, 0:FI], ACT.Silu).then_inc(silu_made, 1)

            np = pairs(act)
            keep_rows(0, 0)
            silu(0, 0)
            keep_rows(1, 1)
            with act.Fori(0, np) as j:
                for par in range(2):
                    i = j * 2 + par
                    silu(i + 1, 1 - par)
                    keep_rows(i + 2, par)

        @block.vector
        def _(dve):
            for s in (hid_made, hid_t_made, y_made):
                dve.sem_inc(s, 2)

            def hidden(i, par):
                dve.wait_ge(silu_made, i + 1)
                dve.wait_ge(hid_turned, i + 1)
                dve.tensor_tensor(out=hid[par][:, :], in0=silu_g[par][:, :], in1=ps_gu[par][:, FI:2 * FI],
                                  op=ALU.mult).then_inc(hid_made, 1)

            def keep_hidden(i, par):
                dve.wait_ge(hid_turned, i + 3)
                dve.wait_ge(out_made, i + 1)
                dve.tensor_copy(hid_t[par][:, :, :].rearrange("p k l -> p (k l)"), ps_h[par][:, :])\
                    .then_inc(hid_t_made, 1)

            def keep_out(i, j, par):
                dve.wait_ge(out_made, i + 3)
                dve.wait_ge(y_stored[par], j * 16 + 16)
                dve.tensor_copy(y[par][:, :], ps_o[par][:, :]).then_inc(y_made, 1)

            np = pairs(dve)
            hidden(0, 0)
            keep_hidden(0, 0)
            with dve.Fori(0, np) as j:
                for par in range(2):
                    i = j * 2 + par
                    hidden(i + 1, 1 - par)
                    keep_out(i, j, par)
                    keep_hidden(i + 1, 1 - par)


def combine(nc, c, m):
    with ExitStack() as ctx:
        p = Pipe(nc, ctx)
        block = ctx.enter_context(nc.Block())
        got = p.sb("got", [P, 2 * TOPK, DM])
        arrived = [p.sem(f"arrived{i}") for i in range(2 * TOPK)]
        added = p.sem("added")

        @block.gpsimd
        def _(pool):
            for t in range(NT):
                for k in range(TOPK):
                    n, slot = t * TOPK + k, (t % 2) * TOPK + k
                    if t >= 2:
                        pool.wait_ge(added, n - 2 * TOPK + 1)
                    pool.indirect_dma_start(got[:, slot, :], None, m.y_dram,
                                            bass.IndirectOffsetOnAxis(ap=m.pos[:, k, t:t + 1], axis=0))\
                        .then_inc(arrived[slot], 16)

        @block.vector
        def _(dve):
            for t in range(NT):
                for k in range(TOPK):
                    n, slot = t * TOPK + k, (t % 2) * TOPK + k
                    dve.wait_ge(arrived[slot], 16 * (t // 2 + 1))
                    if k:
                        dve.wait_ge(added, n)
                    dve.scalar_tensor_tensor(out=c.X[:, t, :], in0=got[:, slot, :],
                                             scalar=m.weight[:, t, k:k + 1], in1=c.X[:, t, :],
                                             op0=ALU.mult, op1=ALU.add).then_inc(added, 1)


def wait(eng, sem, value):
    if not isinstance(value, int) or value > 0:
        eng.wait_ge(sem, value)


def turn_tokens(nc, c, m, d):
    with ExitStack() as ctx:
        p = Pipe(nc, ctx)
        block = ctx.enter_context(nc.Block())
        xn = p.sb("a_xn", [P, NT, DM])
        xn_t = p.sb("a_xn_t", [P, 2, KD, SEQ])
        g_q, g_k = p.sb("g_q", [P, 1]), p.sb("g_k", [P, 1])
        ps_xt = [p.ps(f"ps_at{i}", [P, KD * P]) for i in range(2)]
        normed, turned, kept = (p.sem(x) for x in ("a_normed", "a_turned", "a_kept"))
        stored = [p.sem("a_stored0"), p.sem("a_stored1")]
        gains = p.sem("gains")

        @block.sync
        def _(sp):
            with nc.allow_non_contiguous_dma(reason="one value a partition"):
                sp.dma_start(g_q[:, :], d["g_q"].rearrange("(p a) -> p a", a=1)).then_inc(gains, 16)
                sp.dma_start(g_k[:, :], d["g_k"].rearrange("(p a) -> p a", a=1)).then_inc(gains, 16)
            for b in range(BATCH):
                sp.wait_ge(kept, ST * (b + 1))
                sp.dma_start(m.xn_dram[b * P:(b + 1) * P, :], xn_t[:, b % 2, :, :].rearrange("p k l -> p (k l)"))\
                    .then_inc(stored[b % 2], 16)
            for s in stored:
                sp.wait_ge(s, 16 * BATCH // 2)

        @block.vector
        def _(dve):
            with dve.Fori(0, NT) as t:
                row = lambda x: x[:, ds1(t), :].rearrange("p a l -> p (a l)")
                dve.tensor_scalar(out=row(xn), in0=row(c.X), scalar1=c.rstd[:, ds1(t)],
                                  scalar2=c.nbias[:, ds1(t)], op0=ALU.mult, op1=ALU.add).then_inc(normed, 1)
            dve.wait_ge(gains, 32)
            dve.tensor_tensor(out=m.gain[:, :], in0=g_q[:, :], in1=g_k[:, :], op=ALU.mult)

        @block.tensor
        def _(pe):
            for t in range(NT):
                pe.wait_ge(normed, t + 1)
                wait(pe, kept, t - 1)
                for k in range(KD):
                    tr = pe.transpose(ps_xt[t % 2][:, k * P:(k + 1) * P], xn[:, t, k * P:(k + 1) * P],
                                      c.ident[:, :])
                tr.then_inc(turned, 1)

        @block.scalar
        def _(act):
            for t in range(NT):
                b, j = t // ST, t % ST
                act.wait_ge(turned, t + 1)
                wait(act, stored[b % 2], 16 * (b // 2))
                act.activation(xn_t[:, b % 2, :, j * P:(j + 1) * P],
                               ps_xt[t % 2][:, :].rearrange("p (k l) -> p k l", k=KD), ACT.Copy).then_inc(kept, 1)


def attention(nc, c, m, d):
    with ExitStack() as ctx:
        p = Pipe(nc, ctx)
        block = ctx.enter_context(nc.Block())
        w_q, w_o = p.sb("w_q", [P, 2 * KD, HG * HD]), p.sb("w_o", [P, 2 * HG, DM])
        w_k, w_v = p.sb("w_k", [P, 2 * KC, HG * HD]), p.sb("w_v", [P, 2 * KC, HG * HD])
        x_t = p.sb("x_t", [P, 2, KD, SEQ])
        c_t = p.sb("c_t", [P, 2, KC, SEQ])
        q_t, k_t = p.sb("q_t", [P, 2, HG, SEQ]), p.sb("k_t", [P, 2, HG, SEQ])
        v_s = p.sb("v_s", [P, 2, ST, HG * HD])
        q_raw, k_raw = p.sb("q_raw", [P, HG * HD]), p.sb("k_raw", [P, HG * HD])
        q_sq, k_sq = p.sb("q_sq", [P, HG * HD]), p.sb("k_sq", [P, HG * HD])
        q_ss, k_ss = p.sb("q_ss", [P, HG]), p.sb("k_ss", [P, HG])
        q_r, k_r = p.sb("q_r", [P, HG]), p.sb("k_r", [P, HG])
        prob = p.sb("prob", [P, ST, SEQ])
        prob_t = p.sb("prob_t", [P, ST, SEQ])
        o_t = p.sb("o_t", [P, 2, HG, SEQ])
        high, neg, den, rden = (p.sb(x, [P, ST]) for x in ("high", "neg", "a_den", "rden"))
        ps_s = [p.ps(f"ps_s{i}", [P, SEQ]) for i in range(2)]
        ps_p = [p.ps(f"ps_p{i}", [P, SEQ]) for i in range(2)]
        ps_a, ps_b = p.ps("ps_pa", [P, HG * HD]), p.ps("ps_pb", [P, HG * HD])
        ps_o, ps_y = p.ps("ps_o", [P, SEQ]), p.ps("ps_yo", [P, DM])
        x_loaded = [p.sem("xt_loaded0"), p.sem("xt_loaded1")]
        w_loaded = p.sem("aw_loaded")
        q_made, k_made, v_made = p.sem("q_made"), p.sem("k_made"), p.sem("v_made2")
        q_evac, k_evac, v_kept = p.sem("q_evac"), p.sem("k_evac"), p.sem("v_kept")
        q_summed, k_summed = p.sem("q_summed"), p.sem("k_summed")
        q_mean, k_mean = p.sem("q_mean"), p.sem("k_mean")
        q_rooted, k_rooted = p.sem("q_rooted"), p.sem("k_rooted")
        q_normed, k_normed = p.sem("q_normed"), p.sem("k_normed")
        q_turned, k_turned = p.sem("q_turned"), p.sem("k_turned")
        q_kept, k_kept = p.sem("q_kept"), p.sem("k_kept")
        s_made, high_made, neg_made = p.sem("s_made"), p.sem("high_made"), p.sem("neg_made")
        exp_done, rden_made, p_normed = p.sem("exp_done2"), p.sem("rden_made"), p.sem("p_normed")
        p_turned, p_kept = p.sem("p_turned"), p.sem("p_kept")
        pv_made, o_kept, y_made, y_added = (p.sem(x) for x in ("pv_made", "o_kept", "wo_made", "y_added"))
        scale = HD ** -0.5

        def flat(x):
            return x.rearrange("p a l -> p (a l)")

        def schedule(eng, piece, unit):
            for j in range(ST):
                piece(eng, 0, 0, j, None)
            for par in range(2):
                for h in range(HG):
                    unit(eng, par, par, h, True)
            with eng.Fori(1, NGRP // 2 - 1) as g2:
                for par in range(2):
                    for h in range(HG):
                        unit(eng, g2 * 2 + par, par, h, True)
            for par in range(2):
                for h in range(HG):
                    unit(eng, NGRP - 2 + par, par, h, par == 0)

        @block.sync
        def _(sp):
            def load_w(hg):
                s = hg % 2
                cols = slice(hg * HG * HD, (hg + 1) * HG * HD)
                for w, k, src in ((w_q, KD, d["w_q"]), (w_k, KC, d["w_k"]), (w_v, KC, d["w_v"])):
                    sp.dma_start(w[:, s * k:(s + 1) * k, :], src[:, cols].rearrange("(k p) n -> p k n", p=P))\
                        .then_inc(w_loaded, 16)
                sp.dma_start(w_o[:, s * HG:(s + 1) * HG, :], d["w_o"][cols, :].rearrange("(k p) n -> p k n", p=P))\
                    .then_inc(w_loaded, 16)
            for g in range(NGRP):
                hg, b, par = g // BATCH, g % BATCH, g % 2
                wait(sp, v_made, ST * (g - 1))
                sp.dma_start(flat(x_t[:, par, :, :]), m.xn_dram[b * P:(b + 1) * P, :]).then_inc(x_loaded[par], 16)
                sp.dma_start(c_t[:, par, :, :],
                             d["ctx_t"][b * CD:(b + 1) * CD, :].rearrange("(k p) l -> p k l", p=P))\
                    .then_inc(x_loaded[par], 16)
                if g == 0:
                    load_w(0)
                if g % BATCH == 1 and hg + 1 < NH // HG:
                    sp.wait_ge(w_loaded, 64 * (hg + 1))
                    wait(sp, y_made, BATCH * HG * hg)
                    load_w(hg + 1)

        @block.tensor
        def _(pe):
            def q_product(g, par, j):
                w = g * ST + j
                pe.wait_ge(x_loaded[par], (g >> 1) * 32 + 32)
                pe.wait_ge(w_loaded, (g >> 2) * 64 + 64)
                wait(pe, k_kept, w)
                s = ((g >> 2) & 1) * KD
                for k in range(KD):
                    mm = pe.matmul(ps_a[:, :], x_t[:, par, k, j * P:(j + 1) * P], flat(w_q[:, ds1(s + k), :]),
                                   start=k == 0, stop=k == KD - 1)
                mm.then_inc(q_made, 1)

            def kv_products(g, par, j):
                w = g * ST + j
                s = ((g >> 2) & 1) * KC
                wait(pe, q_kept, w)
                for k in range(KC):
                    mm = pe.matmul(ps_b[:, :], c_t[:, par, k, j * P:(j + 1) * P], flat(w_k[:, ds1(s + k), :]),
                                   start=k == 0, stop=k == KC - 1)
                mm.then_inc(k_made, 1)
                pe.wait_ge(q_evac, w + 1)
                for k in range(KC):
                    mm = pe.matmul(ps_a[:, :], c_t[:, par, k, j * P:(j + 1) * P], flat(w_v[:, ds1(s + k), :]),
                                   start=k == 0, stop=k == KC - 1)
                mm.then_inc(v_made, 1)

            def turns(g, par, j):
                w = g * ST + j
                for ps, raw, free, normed, turned in ((ps_b, q_raw, k_evac, q_normed, q_turned),
                                                      (ps_a, k_raw, v_kept, k_normed, k_turned)):
                    pe.wait_ge(free, w + 1)
                    pe.wait_ge(normed, w + 1)
                    for h in range(HG):
                        tr = pe.transpose(ps[:, h * P:(h + 1) * P], raw[:, h * P:(h + 1) * P], c.ident[:, :])
                    tr.then_inc(turned, 1)

            def scores(g, par, h, qt):
                n = (g * HG + h) * ST + qt
                if h == 0 and qt == 0:
                    pe.wait_ge(q_kept, g * ST + ST)
                    pe.wait_ge(k_kept, g * ST + ST)
                wait(pe, exp_done, n - 1)
                pe.matmul(ps_s[qt % 2][:, :], q_t[:, par, h, qt * P:(qt + 1) * P], k_t[:, par, h, :],
                          start=True, stop=True).then_inc(s_made, 1)

            def piece(pe, g, par, j, _):
                q_product(g, par, j)
                kv_products(g, par, j)
                turns(g, par, j)

            def unit(pe, g, par, h, more):
                u = g * HG + h
                scores(g, par, h, 0)
                scores(g, par, h, 1)
                if more:
                    q_product(g + 1, 1 - par, h)
                scores(g, par, h, 2)
                scores(g, par, h, 3)
                if more:
                    kv_products(g + 1, 1 - par, h)
                for qt in range(ST):
                    n = u * ST + qt
                    pe.wait_ge(p_normed, n + 1)
                    wait(pe, p_kept, n - 1)
                    for kt in range(ST):
                        tr = pe.transpose(ps_p[qt % 2][:, kt * P:(kt + 1) * P], prob[:, qt, kt * P:(kt + 1) * P],
                                          c.ident[:, :])
                    tr.then_inc(p_turned, 1)
                if more:
                    turns(g + 1, 1 - par, h)
                if h == 0:
                    pe.wait_ge(v_kept, g * ST + ST)
                pe.wait_ge(p_kept, u * ST + ST)
                wait(pe, o_kept, u)
                for kt in range(ST):
                    mm = pe.matmul(ps_o[:, :], v_s[:, par, kt, h * HD:(h + 1) * HD], prob_t[:, kt, :],
                                   start=kt == 0, stop=kt == ST - 1)
                mm.then_inc(pv_made, 1)
                if not isinstance(g, int) or g > 0:
                    output(g - 1, 1 - par, h)

            def output(g, par, j):
                pe.wait_ge(o_kept, g * HG + HG)
                wait(pe, y_added, g * HG + j)
                s = ((g >> 2) & 1) * HG
                for h in range(HG):
                    mm = pe.matmul(ps_y[:, :], o_t[:, par, h, j * P:(j + 1) * P], flat(w_o[:, ds1(s + h), :]),
                                   start=h == 0, stop=h == HG - 1)
                mm.then_inc(y_made, 1)

            schedule(pe, piece, unit)
            for j in range(ST):
                output(NGRP - 1, 1, j)

        @block.scalar
        def _(act):
            def evacuate(w, ps, made, turned, raw, sq, evac):
                act.wait_ge(made, w + 1)
                wait(act, turned, w)
                act.activation(raw[:, :], ps[:, :], ACT.Copy)
                act.activation(sq[:, :], ps[:, :], ACT.Square).then_inc(evac, 1)

            def q_part(g, j):
                evacuate(g * ST + j, ps_a, q_made, q_turned, q_raw, q_sq, q_evac)

            def kv_part(g, par, j):
                w = g * ST + j
                evacuate(w, ps_b, k_made, k_turned, k_raw, k_sq, k_evac)
                act.wait_ge(v_made, w + 1)
                wait(act, pv_made, (g - 1) * HG)
                act.activation(v_s[:, par, j, :], ps_a[:, :], ACT.Copy).then_inc(v_kept, 1)

            def keep(g, par, j):
                w = g * ST + j
                wait(act, s_made, (g - 1) * HG * ST)
                act.wait_ge(q_turned, w + 1)
                act.activation(q_t[:, par, :, j * P:(j + 1) * P],
                               ps_b[:, :].rearrange("p (h l) -> p h l", h=HG), ACT.Copy).then_inc(q_kept, 1)
                act.wait_ge(k_turned, w + 1)
                act.activation(k_t[:, par, :, j * P:(j + 1) * P],
                               ps_a[:, :].rearrange("p (h l) -> p h l", h=HG), ACT.Copy,
                               scale=m.gain[:, :]).then_inc(k_kept, 1)

            def exponent(u, qt):
                n = u * ST + qt
                act.wait_ge(neg_made, n + 1)
                wait(act, p_turned, n - ST + 1)
                act.activation(prob[:, qt, :], ps_s[qt % 2][:, :], ACT.Exp, scale=scale, bias=neg[:, qt:qt + 1],
                               accum_out=den[:, qt:qt + 1]).then_inc(exp_done, 1)

            def piece(act, g, par, j, _):
                q_part(g, j)
                kv_part(g, par, j)
                keep(g, par, j)

            def unit(act, g, par, h, more):
                u = g * HG + h
                exponent(u, 0)
                exponent(u, 1)
                if more:
                    q_part(g + 1, h)
                exponent(u, 2)
                exponent(u, 3)
                if more:
                    kv_part(g + 1, 1 - par, h)
                    keep(g + 1, 1 - par, h)

            schedule(act, piece, unit)

        @block.gpsimd
        def _(pool):
            with pool.Fori(0, NGRP * ST) as w:
                for summed, mean, rooted, ss, r in ((q_summed, q_mean, q_rooted, q_ss, q_r),
                                                    (k_summed, k_mean, k_rooted, k_ss, k_r)):
                    pool_waits(pool, c, summed, w + 1)
                    pool.tensor_scalar(out=ss[:, :], in0=ss[:, :], scalar1=1.0 / HD, scalar2=EPS,
                                       op0=ALU.mult, op1=ALU.add).then_inc(mean, 1)
                    pool_waits(pool, c, mean, w + 1)
                    pool.tensor_tensor(out=r[:, :], in0=ss[:, :], in1=c.power[:, 0:HG], op=ALU.pow)\
                        .then_inc(rooted, 1)

        @block.vector
        def _(dve):
            def squares(w, evac, sq, ss, rooted, summed):
                dve.wait_ge(evac, w + 1)
                wait(dve, rooted, w)
                dve.tensor_reduce(ss[:, :], sq[:, :].rearrange("p (h l) -> p h l", h=HG), AX.X, ALU.add)\
                    .then_inc(summed, 1)

            def norm(w, rooted, raw, r, normed):
                dve.wait_ge(rooted, w + 1)
                x = raw[:, :].rearrange("p (h l) -> p h l", h=HG)
                dve.tensor_tensor(out=x, in0=x, in1=r[:, :].rearrange("p (h a) -> p h a", a=1)
                                  .broadcast_to([P, HG, HD]), op=ALU.mult).then_inc(normed, 1)

            def q_squares(w):
                squares(w, q_evac, q_sq, q_ss, q_rooted, q_summed)

            def k_squares(w):
                squares(w, k_evac, k_sq, k_ss, k_rooted, k_summed)

            def q_norm(w):
                norm(w, q_rooted, q_raw, q_r, q_normed)

            def k_norm(w):
                norm(w, k_rooted, k_raw, k_r, k_normed)

            def maximum(u, qt):
                n = u * ST + qt
                dve.wait_ge(s_made, n + 1)
                wait(dve, exp_done, n - ST + 1)
                dve.reduce_max(high[:, qt:qt + 1], ps_s[qt % 2][:, :], AX.X).then_inc(high_made, 1)
                dve.wait_ge(high_made, n + 1)
                dve.tensor_scalar(out=neg[:, qt:qt + 1], in0=high[:, qt:qt + 1], scalar1=-scale, scalar2=None,
                                  op0=ALU.mult).then_inc(neg_made, 1)

            def normalize(u, qt):
                n = u * ST + qt
                dve.wait_ge(exp_done, n + 1)
                dve.reciprocal(rden[:, qt:qt + 1], den[:, qt:qt + 1]).then_inc(rden_made, 1)
                dve.wait_ge(rden_made, n + 1)
                dve.tensor_scalar(out=prob[:, qt, :], in0=prob[:, qt, :], scalar1=rden[:, qt:qt + 1],
                                  scalar2=None, op0=ALU.mult).then_inc(p_normed, 1)

            def piece(dve, g, par, j, _):
                w = g * ST + j
                q_squares(w)
                q_norm(w)
                k_squares(w)
                k_norm(w)

            def unit(dve, g, par, h, more):
                u = g * HG + h
                w = u + ST
                maximum(u, 0)
                maximum(u, 1)
                normalize(u, 0)
                normalize(u, 1)
                if more:
                    q_squares(w)
                maximum(u, 2)
                maximum(u, 3)
                if more:
                    q_norm(w)
                normalize(u, 2)
                normalize(u, 3)
                if more:
                    k_squares(w)
                    k_norm(w)
                wait(dve, pv_made, u)
                for qt in range(ST):
                    dve.wait_ge(p_turned, u * ST + qt + 1)
                    dve.tensor_copy(prob_t[:, :, qt * P:(qt + 1) * P],
                                    ps_p[qt % 2][:, :].rearrange("p (k l) -> p k l", k=ST)).then_inc(p_kept, 1)
                dve.wait_ge(pv_made, u + 1)
                wait(dve, y_made, (g - 1) * HG)
                dve.tensor_copy(o_t[:, par, h, :], ps_o[:, :]).then_inc(o_kept, 1)
                if not isinstance(g, int) or g > 0:
                    add(g - 1, h)

            def add(g, j):
                dve.wait_ge(y_made, g * HG + j + 1)
                x = flat(c.X[:, ds1((g & (BATCH - 1)) * ST + j), :])
                dve.tensor_tensor(out=x, in0=ps_y[:, :], in1=x, op=ALU.add).then_inc(y_added, 1)

            schedule(dve, piece, unit)
            for j in range(ST):
                add(NGRP - 1, j)


def quantize_weights(nc, c, m, d):
    with ExitStack() as ctx:
        p = Pipe(nc, ctx)
        block = ctx.enter_context(nc.Block())
        raw = [p.sb(f"raw{i}", [P, FN]) for i in range(2)]
        junk = p.sb("junk", [P, FN])
        part, sums = p.sb("part", [P, 2]), p.sb("sums", [P, 2])
        ones = p.sb("ones_f", [P, P])
        scale = p.sb("w_scale", [P, 2])
        ps_sum = p.ps("ps_sum", [P, 2])
        loaded = [p.sem("raw_loaded0"), p.sem("raw_loaded1")]
        ones_made, step, totals = p.sem("ones_made"), p.sem("wq_step"), p.sem("totals")
        part_made = [p.sem("part_made0"), p.sem("part_made1")]

        @block.sync
        def _(sp):
            sp.dma_start(raw[0][:, :].rearrange("p (k n) -> p k n", k=KD),
                         d["w1"].rearrange("(k p) n -> p k n", p=P)).then_inc(loaded[0], 16)
            sp.dma_start(raw[1][:, :].rearrange("p (k n) -> p k n", k=KF),
                         d["w2"].rearrange("(k p) n -> p k n", p=P)).then_inc(loaded[1], 16)

        @block.scalar
        def _(act):
            act.wait_ge(loaded[0], 16)
            act.activation(junk[:, :], raw[0][:, :], ACT.Abs, accum_out=part[:, 0:1]).then_inc(part_made[0], 1)

        @block.gpsimd
        def _(pool):
            pool.memset(ones[:, :], 1.0).then_inc(ones_made, 1)

        @block.tensor
        def _(pe):
            pe.wait_ge(ones_made, 1)
            pe.wait_ge(part_made[0], 1)
            pe.wait_ge(part_made[1], 1)
            pe.matmul(ps_sum[:, :], ones[:, :], part[:, :], start=True, stop=True).then_inc(totals, 1)

        @block.vector
        def _(dve):
            n = [0]

            def link(ins):
                n[0] += 1
                ins.then_inc(step, 1)
                dve.wait_ge(step, n[0])

            dve.wait_ge(loaded[1], 16)
            dve.tensor_reduce(part[:, 1:2], raw[1][:, :], AX.X, ALU.add, apply_absolute_value=True)\
                .then_inc(part_made[1], 1)
            dve.wait_ge(totals, 1)
            link(dve.tensor_scalar(out=sums[:, :], in0=ps_sum[:, :], scalar1=1.0 / (P * FN), scalar2=EPS,
                                   op0=ALU.mult, op1=ALU.max))
            link(dve.reciprocal(scale[:, :], sums[:, :]))
            link(dve.reciprocal(m.w_step[:, :], scale[:, :]))
            for i, out in ((0, m.w1q), (1, m.w2q)):
                link(dve.tensor_scalar(out=raw[i][:, :], in0=raw[i][:, :], scalar1=scale[:, i:i + 1], scalar2=1.0,
                                       op0=ALU.mult, op1=ALU.min))
                link(dve.tensor_scalar(out=raw[i][:, :], in0=raw[i][:, :], scalar1=-1.0, scalar2=MAGIC,
                                       op0=ALU.max, op1=ALU.add))
                link(dve.tensor_scalar(out=out[:, :, :].rearrange("p k n -> p (k n)"), in0=raw[i][:, :],
                                       scalar1=-MAGIC, scalar2=None, op0=ALU.add))


def feed_forward(nc, c, m):
    with ExitStack() as ctx:
        p = Pipe(nc, ctx)
        block = ctx.enter_context(nc.Block())
        ident = p.sb("ident_b", [P, P], BF16)
        xf = [p.sb(f"xf{i}", [P, DM]) for i in range(2)]
        xq = [p.sb(f"xq{i}", [P, DM], BF16) for i in range(2)]
        xq_t = [p.sb(f"xq_t{i}", [P, KD, P], BF16) for i in range(2)]
        hf = [p.sb(f"hf{i}", [P, DF]) for i in range(2)]
        hq = [p.sb(f"hq{i}", [P, DF], BF16) for i in range(2)]
        hq_t = p.sb("hq_t", [P, KF, P], BF16)
        stat = p.sb("stat", [P, 2, 6])
        ps_h = [p.ps(f"ps_fh{i}", [P, SEQ]) for i in range(4)]
        ps_x = p.ps("ps_fx", [P, DM])[:, :].bitcast(BF16)[:, 0:KD * P]
        ps_t = [p.ps(f"ps_ft{i}", [P, DM])[:, :].bitcast(BF16) for i in range(2)]
        ps_y = p.ps("ps_fy", [P, DM])
        ident_made = p.sem("ident_made")
        step = p.sem("ff_step")
        xq_made, xq_turned, xq_kept = p.sem("xq_made"), p.sem("xq_turned"), p.sem("xq_kept")
        h_made, gelu_made = p.sem("h_made"), p.sem("gelu_made")
        hq_made, hq_turned, hq_kept = p.sem("hq_made"), p.sem("hq_turned"), p.sem("hq_kept")
        y_made, y_added = p.sem("fy_made"), p.sem("fy_added")
        STEPS = 12

        def schedule(eng, ahead, behind):
            ahead(0, 0)
            for t in range(2):
                ahead(t + 1, (t + 1) % 2)
                behind(t, t)
            with eng.Fori(1, NT // 2 - 1) as t2:
                for par in range(2):
                    ahead(t2 * 2 + par + 1, 1 - par)
                    behind(t2 * 2 + par, par)
            ahead(NT - 1, 1)
            behind(NT - 2, 0)
            behind(NT - 1, 1)

        @block.tensor
        def _(pe):
            def ahead(t, par):
                pe.wait_ge(xq_made, t + 1)
                wait(pe, xq_kept, t)
                for k in range(KD):
                    tr = pe.transpose(ps_x[:, k * P:(k + 1) * P], xq[par][:, k * P:(k + 1) * P], ident[:, :])
                tr.then_inc(xq_turned, 1)
                pe.wait_ge(xq_kept, t + 1)
                for n in range(4):
                    wait(pe, gelu_made, t * 4 + n - 3)
                    for k in range(KD):
                        mm = pe.matmul(ps_h[n][:, :], xq_t[par][:, k, :], m.w1q[:, k, n * SEQ:(n + 1) * SEQ],
                                       start=k == 0, stop=k == KD - 1)
                    mm.then_inc(h_made, 1)

            def behind(t, par):
                pe.wait_ge(hq_made, t + 1)
                for i in range(2):
                    wait(pe, hq_kept, t * 2 + i - 1)
                    for k in range(8):
                        tr = pe.transpose(ps_t[i][:, k * P:(k + 1) * P],
                                          hq[par][:, (i * 8 + k) * P:(i * 8 + k + 1) * P], ident[:, :])
                    tr.then_inc(hq_turned, 1)
                wait(pe, y_added, t)
                for k in range(KF):
                    if k % 8 == 0:
                        pe.wait_ge(hq_kept, t * 2 + k // 8 + 1)
                    mm = pe.matmul(ps_y[:, :], hq_t[:, k, :], m.w2q[:, k, :], start=k == 0, stop=k == KF - 1)
                mm.then_inc(y_made, 1)

            pe.wait_ge(ident_made, 1)
            schedule(pe, ahead, behind)

        @block.scalar
        def _(act):
            def ahead(t, par):
                act.wait_ge(xq_turned, t + 1)
                wait(act, h_made, (t - 1) * 4)
                act.activation(xq_t[par][:, :, :].rearrange("p k l -> p (k l)"), ps_x, ACT.Copy)\
                    .then_inc(xq_kept, 1)
                wait(act, hq_made, t - 1)
                for n in range(4):
                    act.wait_ge(h_made, t * 4 + n + 1)
                    act.activation(hf[par][:, n * SEQ:(n + 1) * SEQ], ps_h[n][:, :], ACT.Gelu,
                                   scale=stat[:, par, 2:3]).then_inc(gelu_made, 1)

            def behind(t, par):
                wait(act, y_made, t)
                for i in range(2):
                    act.wait_ge(hq_turned, t * 2 + i + 1)
                    act.activation(hq_t[:, i * 8:(i + 1) * 8, :].rearrange("p k l -> p (k l)"), ps_t[i][:, :],
                                   ACT.Copy).then_inc(hq_kept, 1)

            schedule(act, ahead, behind)

        @block.vector
        def _(dve):
            def link(t, n, ins):
                ins.then_inc(step, 1)
                dve.wait_ge(step, n + 1)

            def quantize(t, n, x, s, out, made, w_step):
                link(t, n, dve.tensor_reduce(s[:, 0:1], x, AX.X, ALU.max, apply_absolute_value=True))
                link(t, n + 1, dve.tensor_scalar(out=s[:, 0:1], in0=s[:, 0:1], scalar1=EPS, scalar2=1.0 / QMAX,
                                                 op0=ALU.max, op1=ALU.mult))
                link(t, n + 2, dve.reciprocal(s[:, 1:2], s[:, 0:1]))
                link(t, n + 3, dve.tensor_scalar(out=s[:, 2:3], in0=s[:, 0:1], scalar1=w_step, scalar2=None,
                                                 op0=ALU.mult))
                link(t, n + 4, dve.tensor_scalar(out=x, in0=x, scalar1=s[:, 1:2], scalar2=QMAX,
                                                 op0=ALU.mult, op1=ALU.min))
                link(t, n + 5, dve.tensor_scalar(out=x, in0=x, scalar1=-QMAX - 1.0, scalar2=MAGIC,
                                                 op0=ALU.max, op1=ALU.add))
                dve.tensor_scalar(out=out, in0=x, scalar1=-MAGIC, scalar2=None, op0=ALU.add).then_inc(made, 1)

            def ahead(t, par):
                n = base_ahead(t)
                wait(dve, gelu_made, (t - 1) * 4)
                link(t, n, dve.tensor_scalar(out=xf[par][:, :], in0=c.X[:, ds1(t), :].rearrange("p a l -> p (a l)"),
                                             scalar1=c.rstd[:, ds1(t)], scalar2=c.nbias[:, ds1(t)],
                                             op0=ALU.mult, op1=ALU.add))
                quantize(t, n + 1, xf[par][:, :], stat[:, par, 0:3], xq[par][:, :], xq_made, m.w_step[:, 0:1])

            def behind(t, par):
                n = base_behind(t)
                dve.wait_ge(gelu_made, t * 4 + 4)
                wait(dve, hq_turned, (t - 1) * 2)
                quantize(t, n, hf[par][:, :], stat[:, par, 3:6], hq[par][:, :], hq_made, m.w_step[:, 1:2])
                dve.wait_ge(y_made, t + 1)
                x = c.X[:, ds1(t), :].rearrange("p a l -> p (a l)")
                dve.scalar_tensor_tensor(out=x, in0=ps_y[:, :], scalar=stat[:, par, 5:6], in1=x,
                                         op0=ALU.mult, op1=ALU.add).then_inc(y_added, 1)

            def base_ahead(t):
                return 0 if isinstance(t, int) and t == 0 else t * 7 + (t - 1) * 6

            def base_behind(t):
                return NT * 7 + t * 6 if isinstance(t, int) and t == NT - 1 else (t + 2) * 7 + t * 6

            dve.tensor_copy(ident[:, :], c.ident[:, :]).then_inc(ident_made, 1)
            schedule(dve, ahead, behind)


class Holder:
    pass


STAGES = 4


def program(nc, d, out, stages=STAGES):
    with ExitStack() as ctx:
        p = Pipe(nc, ctx)
        c = Holder()
        c.X = p.sb("X", [P, NT, DM])
        c.ident = p.sb("ident", [P, P])
        c.power = p.sb("power", [P, P])
        c.rstd = p.sb("rstd", [P, NT])
        c.nbias = p.sb("nbias", [P, NT])
        c.pool_passed = nc.alloc_semaphore("pool_passed")
        c.const_made = nc.alloc_semaphore("const_made")
        load_constants(nc, c, d)
        with nc.cleanup_on_exit(), ExitStack() as ssm:
            q = Pipe(nc, ssm)
            m = Holder()
            m.u = q.sb("u", [P, BATCH * EC, SEQ])
            m.delta = q.sb("delta", [P, BATCH * EC, SEQ])
            m.du = q.sb("du", [P, BATCH * EC, SEQ])
            m.d_a = q.sb("d_a", [P, 2, G, SEQ])
            m.a_neg = q.sb("a_neg", [P, EC * DS])
            m.d_diag = q.sb("d_diag", [P, EC, P])
            m.zero2 = q.sb("zero2", [P, 2])
            m.zeros = q.sb("zeros", [P, DM])
            m.rows_dram = nc.dram_tensor("rows_dram", [FILLS * FILL * P, DM], FP32, kind="Internal").ap()
            m.y_dram = nc.dram_tensor("y_dram", [(MINT + FILLS * FILL_Y) * P, DM], FP32, kind="Internal").ap()
            assert min(m.rows_dram.shape[0], m.y_dram.shape[0]) >= (MAXT + 2) * P
            m.bc_dram = nc.dram_tensor("bc_dram", [BATCH, 2 * DS, SEQ], FP32, kind="Internal").ap()
            norm_statistics(nc, c, "n0")
            ssm_inputs(nc, c, m, d)
            ssm_scan(nc, c, m)
        if stages >= 2:
            with nc.cleanup_on_exit():
                norm_statistics(nc, c, "n1")
                with ExitStack() as moe:
                    q = Pipe(nc, moe)
                    m.pos = q.sb("pos_row", [P, TOPK, NT], U32)
                    m.weight = q.sb("weight", [P, NT, TOPK])
                    m.table = q.sb("table", [1, T_PAIRS + 1], I32)
                    with ExitStack() as first:
                        q = Pipe(nc, first)
                        m.xn = q.sb("xn", [P, NT, DM])
                        m.logits = q.sb("logits", [P, NT, NE])
                        m.sim = q.sb("sim", [NE, NE])
                        m.sim_loaded = q.sem("sim_loaded")
                        router_logits(nc, c, m, d)
                        route(nc, c, m)
                        dispatch(nc, c, m)
                    experts(nc, c, m, d)
                    combine(nc, c, m)
        if stages >= 3:
            m = Holder()
            m.xn_dram = nc.dram_tensor("xn_dram", [BATCH * P, KD * SEQ], FP32, kind="Internal").ap()
            m.gain = p.sb("gain", [P, 1])
            with nc.cleanup_on_exit():
                norm_statistics(nc, c, "n2")
                turn_tokens(nc, c, m, d)
                attention(nc, c, m, d)
        if stages >= 4:
            norm_statistics(nc, c, "n3")
            m.w1q = p.sb("w1q", [P, KD, DF], BF16)
            m.w2q = p.sb("w2q", [P, KF, DM], BF16)
            m.w_step = p.sb("w_step", [P, 2])
            quantize_weights(nc, c, m, d)
            feed_forward(nc, c, m)
        store_output(nc, c, out)


def store_output(nc, c, out):
    stored = nc.alloc_semaphore("stored")
    with nc.Block() as block:
        @block.sync
        def _(sp):
            sp.dma_start(out.rearrange("(t p) n -> p t n", p=P), c.X[:, :, :]).then_inc(stored, 16)
            sp.wait_ge(stored, 16)


def kernel(x, ctx_1024, L0_xattn_in_proj_w, L0_xattn_conv_w, L0_xattn_conv_b, L0_xattn_x_proj_w,
           L0_xattn_dt_proj_w, L0_xattn_dt_proj_b, L0_xattn_A_log, L0_xattn_D, L0_ffn_gate_weight,
           L0_ffn_gate_up_proj, L0_ffn_down_proj, L0_ffn_similarity, L1_xattn_Wq, L1_xattn_Wk,
           L1_xattn_Wv, L1_xattn_Wo, L1_xattn_gq, L1_xattn_gk, L1_ffn_w1, L1_ffn_w2):
    import numpy as np
    import concourse.bacc as bacc
    from concourse.bass_utils import run_bass_kernel_spmd as run
    A = np.asarray
    arrays = {
        "x": A(x).reshape(BATCH * SEQ, DM),
        "ctx_t": A(ctx_1024).transpose(0, 2, 1).reshape(BATCH * CD, SEQ),
        "in_proj": A(L0_xattn_in_proj_w).T,
        "conv_w": A(L0_xattn_conv_w),
        "conv_b": A(L0_xattn_conv_b),
        "x_proj": A(L0_xattn_x_proj_w).T,
        "dt_proj": A(L0_xattn_dt_proj_w).T,
        "dt_b": A(L0_xattn_dt_proj_b),
        "a_log": A(L0_xattn_A_log),
        "d_skip": A(L0_xattn_D),
        "gate_w": A(L0_ffn_gate_weight).T,
        "similarity": A(L0_ffn_similarity),
        "w_q": A(L1_xattn_Wq), "w_k": A(L1_xattn_Wk), "w_v": A(L1_xattn_Wv), "w_o": A(L1_xattn_Wo),
        "g_q": A(L1_xattn_gq), "g_k": A(L1_xattn_gk),
        "w1": A(L1_ffn_w1).T, "w2": A(L1_ffn_w2).T,
        "gate_up": A(L0_ffn_gate_up_proj).reshape(NE, 2 * FI, KD, P).transpose(0, 3, 2, 1).reshape(NE, P, KD * 2 * FI),
        "down": A(L0_ffn_down_proj).reshape(NE, DM, 2, FI // 2).transpose(0, 3, 2, 1).reshape(NE, FI // 2, 2 * DM),
    }
    arrays = {k: np.ascontiguousarray(v) for k, v in arrays.items()}
    nc = bacc.Bacc("TRN2", target_bir_lowering=False, num_devices=1)
    d = {k: nc.dram_tensor("in_" + k, v.shape, mybir.dt.from_np(v.dtype), kind="ExternalInput").ap()
         for k, v in arrays.items()}
    out = nc.dram_tensor("out", (BATCH * SEQ, DM), FP32, kind="ExternalOutput").ap()
    program(nc, d, out)
    r = run(nc, [{"in_" + k: v for k, v in arrays.items()}], core_ids=[0])
    return r.results[0]["out"].reshape(BATCH, SEQ, DM)
```

```python
import concourse.bass as bass
from concourse import mybir
from contextlib import ExitStack

FP32 = mybir.dt.float32
F32R = mybir.dt.float32r
BF16 = mybir.dt.bfloat16
I32 = mybir.dt.int32
U32 = mybir.dt.uint32
ALU = mybir.AluOpType
ACT = mybir.ActivationFunctionType
AX = mybir.AxisListType

P = 128
BATCH, SEQ, DM = 4, 512, 512
ST = SEQ // P
NT = BATCH * ST
EPS = 1e-5

CD = 256
KC = CD // P
DI = 512
EC = DI // P
DS = 16
DR = 16
TAPS = 4
G = 2
NG = DS // G

NE, TOPK, SELK, THRESH = 64, 8, 4, 0.5
FI = 192
KD = DM // P
MAXT = BATCH * SEQ * TOPK // P + NE
MINT = BATCH * SEQ * TOPK // P
FILLS, FILL, FILL_Y = BATCH * NG // 2 - 1, 14, 5
T_END, T_PAIRS = P, P + NE
EB = (NE - 1).bit_length()

NH, HD = 16, 128
NP = NH // 2
UP = 2 * BATCH
NU = NP * UP

DF = 2048
KF = DF // P
FN = DM * DF // P
MAGIC = 1.5 * 2.0 ** 23
QMAX = 127.0


def ds1(i):
    return bass.ds(i, 1)


def pool_waits(pool, c, sem, value):
    pool.wait_ge(sem, value).then_inc(c.pool_passed, 1)


class Pipe:

    def __init__(self, nc, ctx):
        self.nc, self.ctx = nc, ctx

    def sb(self, name, shape, dt=FP32):
        return self.ctx.enter_context(self.nc.sbuf_tensor(name, shape, dt))

    def ps(self, name, shape, dt=FP32):
        return self.ctx.enter_context(self.nc.psum_tensor(name, shape, dt))

    def sem(self, name):
        return self.nc.alloc_semaphore(name)


def load_constants(nc, c, d):
    x_loaded = nc.alloc_semaphore("x_loaded")
    const_made = c.const_made
    with nc.Block() as block:
        @block.sync
        def _(sp):
            sp.dma_start(c.X[:, :, :], d["x"].rearrange("(t p) n -> p t n", p=P)).then_inc(x_loaded, 16)
            sp.wait_ge(x_loaded, 16)

        @block.gpsimd
        def _(pool):
            pool.memset(c.ident[:, :], 0.0).then_inc(const_made, 1)
            pool.memset(c.power[:, :], -0.5)
            pool.wait_ge(const_made, 1)
            pool.affine_select(out=c.ident[:, :], in_=c.ident[:, :], compare_op=ALU.not_equal, fill=1.0,
                               base=0, pattern=[[-1, P]], channel_multiplier=1).then_inc(const_made, 1)


def norm_statistics(nc, c, tag):
    with ExitStack() as ctx:
        p = Pipe(nc, ctx)
        block = ctx.enter_context(nc.Block())
        bn6, bn2 = p.sb(f"{tag}_bn6", [P, NT, 6]), p.sb(f"{tag}_bn2", [P, NT, 2])
        vare = p.sb(f"{tag}_vare", [P, NT])
        stats_made, aggregated = p.sem(f"{tag}_stats_made"), p.sem(f"{tag}_aggregated")
        eps_added, rooted = p.sem(f"{tag}_eps_added"), p.sem(f"{tag}_rooted")

        @block.vector
        def _(dve):
            with dve.Fori(0, NT) as t:
                dve.bn_stats(bn6[:, ds1(t), :].rearrange("p a b -> p (a b)"),
                             c.X[:, ds1(t), :].rearrange("p a b -> p (a b)")).then_inc(stats_made, 1)
            dve.wait_ge(stats_made, NT)
            for t in range(NT):
                aggr = dve.bn_aggr(bn2[:, t, :], bn6[:, t, :])
            aggr.then_inc(aggregated, 1)
            dve.wait_ge(aggregated, 1)
            dve.tensor_scalar(out=vare[:, :], in0=bn2[:, :, 1], scalar1=EPS, scalar2=None,
                              op0=ALU.add).then_inc(eps_added, 1)
            dve.wait_ge(rooted, 1)
            dve.scalar_tensor_tensor(out=c.nbias[:, :], in0=bn2[:, :, 0], scalar=-1.0, in1=c.rstd[:, :],
                                     op0=ALU.mult, op1=ALU.mult)

        @block.gpsimd
        def _(pool):
            pool.wait_ge(eps_added, 1)
            pool.tensor_tensor(out=c.rstd[:, :], in0=vare[:, :], in1=c.power[:, 0:NT],
                               op=ALU.pow).then_inc(rooted, 1)


def ssm_inputs(nc, c, m, d):
    with ExitStack() as ctx:
        p = Pipe(nc, ctx)
        block = ctx.enter_context(nc.Block())
        w_in = p.sb("w_in", [P, KC, DI])
        w_x = p.sb("w_x", [P, EC, DR + 2 * DS])
        w_dt = p.sb("w_dt", [DR, DI])
        conv_w = p.sb("conv_w", [P, EC, TAPS])
        conv_b = p.sb("conv_b", [P, EC])
        dt_b = p.sb("dt_b", [P, EC])
        a_log = p.sb("a_log", [P, EC * DS])
        d_skip = p.sb("d_skip", [P, EC])
        ctx_t = p.sb("ctx_t", [P, BATCH * KC, SEQ])
        x_pad = p.sb("x_pad", [P, EC, SEQ + TAPS - 1])
        conv = p.sb("conv", [P, EC, SEQ])
        dbc = p.sb("dbc", [DR + 2 * DS, SEQ])
        pos = p.sb("pos", [P, EC, SEQ])
        mag = p.sb("mag", [P, EC, SEQ])
        log1 = p.sb("log1", [P, EC, SEQ])
        den = conv
        ps_a = [p.ps(f"ps_a{i}", [P, SEQ]) for i in range(EC)]
        ps_x = p.ps("ps_x", [DR + 2 * DS, SEQ])
        small_loaded, ctx_loaded = p.sem("small_loaded"), p.sem("ctx_loaded")
        x_made, x_copied, padded = p.sem("x_made"), p.sem("x_copied"), p.sem("padded")
        conv_step, conv_done, u_made = p.sem("conv_step"), p.sem("conv_done"), p.sem("u_made")
        dbc_made, dbc_copied, dbc_stored = p.sem("dbc_made"), p.sem("dbc_copied"), p.sem("dbc_stored")
        mag_made = p.sem("mag_made")
        v_made, v_taken = p.sem("v_made"), p.sem("v_taken")
        exp_made, log_made = p.sem("exp_made"), p.sem("log_made")
        den_made, recip_made, ratio_made = p.sem("den_made"), p.sem("recip_made"), p.sem("ratio_made")
        sp_step, delta_made, a_exp = p.sem("sp_step"), p.sem("delta_made"), p.sem("a_exp")

        @block.sync
        def _(sp):
            col = lambda v: v.rearrange("(c p) -> p c", p=P)
            sp.dma_start(w_in[:, :, :], d["in_proj"].rearrange("(c p) e -> p c e", p=P)).then_inc(small_loaded, 16)
            sp.dma_start(ctx_t[:, :, :], d["ctx_t"].rearrange("(k p) l -> p k l", p=P)).then_inc(ctx_loaded, 16)
            sp.dma_start(w_x[:, :, :], d["x_proj"].rearrange("(c p) e -> p c e", p=P)).then_inc(small_loaded, 16)
            sp.dma_start(w_dt[:, :], d["dt_proj"]).then_inc(small_loaded, 16)
            sp.dma_start(conv_w[:, :, :], d["conv_w"].rearrange("(c p) k -> p c k", p=P)).then_inc(small_loaded, 16)
            with nc.allow_non_contiguous_dma(reason="one value a partition"):
                sp.dma_start(conv_b[:, :], col(d["conv_b"])).then_inc(small_loaded, 16)
                sp.dma_start(dt_b[:, :], col(d["dt_b"])).then_inc(small_loaded, 16)
                sp.dma_start(d_skip[:, :], col(d["d_skip"])).then_inc(small_loaded, 16)
            sp.dma_start(a_log[:, :].rearrange("p (c n) -> p c n", n=DS),
                         d["a_log"].rearrange("(c p) n -> p c n", p=P)).then_inc(small_loaded, 16)
            sp.sem_inc(dbc_stored, 16)
            with sp.Fori(0, BATCH) as b:
                sp.wait_ge(dbc_copied, b + 1)
                sp.dma_start(m.bc_dram[ds1(b), :, :].rearrange("a n l -> (a n) l"),
                             dbc[DR:DR + 2 * DS, :]).then_inc(dbc_stored, 16)
            sp.wait_ge(dbc_stored, 16 * BATCH + 16)

        @block.tensor
        def _(pe):
            pe.wait_ge(small_loaded, 128)
            pe.wait_ge(ctx_loaded, 16)
            with pe.Fori(0, BATCH) as b:
                pe.wait_ge(v_taken, b * EC + 1)
                pe.wait_ge(exp_made, b + 1)
                for ec in range(EC):
                    for k in range(KC):
                        mm = pe.matmul(ps_a[ec][:, :], w_in[:, k, ec * P:(ec + 1) * P],
                                       ctx_t[:, ds1(b * KC + k), :].rearrange("p a l -> p (a l)"),
                                       start=k == 0, stop=k == KC - 1)
                    mm.then_inc(x_made, 1)
                pe.wait_ge(u_made, b + 1)
                for ec in range(EC):
                    mm = pe.matmul(ps_x[:, :], w_x[:, ec, :],
                                   m.u[:, ds1(b * EC + ec), :].rearrange("p a l -> p (a l)"),
                                   start=ec == 0, stop=ec == EC - 1)
                mm.then_inc(dbc_made, 1)
                pe.wait_ge(dbc_copied, b + 1)
                for ec in range(EC):
                    mm = pe.matmul(ps_a[ec][:, :], w_dt[:, ec * P:(ec + 1) * P], dbc[0:DR, :],
                                   start=True, stop=True)
                mm.then_inc(v_made, 1)

        @block.scalar
        def _(act):
            act.wait_ge(small_loaded, 128)
            act.activation(m.a_neg[:, :], a_log[:, :], ACT.Exp).then_inc(a_exp, 1)
            with act.Fori(0, BATCH) as b:
                act.wait_ge(conv_done, b * EC + 1)
                for ec in range(EC):
                    act.wait_ge(x_made, b * EC + ec + 1)
                    act.activation(x_pad[:, ec, TAPS - 1:], ps_a[ec][:, :], ACT.Copy).then_inc(x_copied, 1)
                for ec in range(EC):
                    act.wait_ge(conv_done, b * EC + ec + 2)
                    u = act.activation(m.u[:, ds1(b * EC + ec), :].rearrange("p a l -> p (a l)"), conv[:, ec, :],
                                       ACT.Silu, bias=conv_b[:, ec:ec + 1])
                u.then_inc(u_made, 1)
                act.wait_ge(dbc_made, b + 1)
                act.wait_ge(dbc_stored, b * 16 + 16)
                act.activation(dbc[:, :], ps_x[:, :], ACT.Copy).then_inc(dbc_copied, 1)
                act.wait_ge(delta_made, b + 1)
                for ec in range(EC):
                    act.wait_ge(v_taken, b * EC + ec + 2)
                    v = act.activation(mag[:, ec, :], ps_a[ec][:, :], ACT.Abs, bias=dt_b[:, ec:ec + 1])
                v.then_inc(mag_made, 1)
                act.wait_ge(mag_made, b + 1)
                act.activation(mag[:, :, :], mag[:, :, :], ACT.Exp, scale=-1.0).then_inc(exp_made, 1)
                act.wait_ge(exp_made, b + 2)
                act.activation(log1[:, :, :], mag[:, :, :], ACT.Ln, bias=1.0).then_inc(log_made, 1)

        @block.vector
        def _(dve):
            dve.sem_inc(v_taken, 1)
            dve.sem_inc(ratio_made, 1)
            dve.sem_inc(exp_made, 1)
            dve.sem_inc(conv_done, 1)
            dve.memset(x_pad[:, :, 0:TAPS - 1], 0.0).then_inc(padded, 1)
            dve.wait_ge(a_exp, 1)
            dve.tensor_scalar(out=m.a_neg[:, :], in0=m.a_neg[:, :], scalar1=-1.0, scalar2=None,
                              op0=ALU.mult)
            for ec in range(EC):
                dve.tensor_scalar(out=m.d_diag[:, ec, :], in0=c.ident[:, :], scalar1=d_skip[:, ec:ec + 1],
                                  scalar2=None, op0=ALU.mult)
            dve.memset(m.d_a[:, :, :, 0:1], 0.0)
            dve.memset(m.zero2[:, :], 0.0)
            dve.memset(m.zeros[:, :], 0.0)
            dve.wait_ge(padded, 1)
            with dve.Fori(0, BATCH) as b:
                dve.wait_ge(ratio_made, b + 1)
                for ec in range(EC):
                    dve.wait_ge(x_copied, b * EC + ec + 1)
                    dve.tensor_scalar(out=conv[:, ec, :], in0=x_pad[:, ec, 0:SEQ], scalar1=conv_w[:, ec, 0:1],
                                      scalar2=None, op0=ALU.mult).then_inc(conv_step, 1)
                for k in range(1, TAPS):
                    for ec in range(EC):
                        dve.wait_ge(conv_step, b * (TAPS - 1) * EC + (k - 1) * EC + ec + 1)
                        dve.scalar_tensor_tensor(out=conv[:, ec, :], in0=x_pad[:, ec, k:k + SEQ],
                                                 scalar=conv_w[:, ec, k:k + 1], in1=conv[:, ec, :],
                                                 op0=ALU.mult, op1=ALU.add)\
                            .then_inc(conv_done if k == TAPS - 1 else conv_step, 1)
                dve.wait_ge(v_made, b + 1)
                dve.wait_ge(delta_made, b + 1)
                for ec in range(EC):
                    dve.tensor_scalar(out=pos[:, ec, :], in0=ps_a[ec][:, :], scalar1=dt_b[:, ec:ec + 1],
                                          scalar2=0.0, op0=ALU.add, op1=ALU.max).then_inc(v_taken, 1)
                dve.wait_ge(den_made, 2 * b + 2)
                dve.reciprocal(den[:, :, :], den[:, :, :]).then_inc(recip_made, 1)
                dve.wait_ge(recip_made, b + 1)
                dve.wait_ge(log_made, b + 1)
                dve.scalar_tensor_tensor(out=log1[:, :, :].rearrange("p a l -> p (a l)"),
                                         in0=log1[:, :, :].rearrange("p a l -> p (a l)"), scalar=1e-30,
                                         in1=den[:, :, :].rearrange("p a l -> p (a l)"),
                                         op0=ALU.max, op1=ALU.mult).then_inc(ratio_made, 1)

        @block.gpsimd
        def _(pool):
            pool.sem_inc(delta_made, 1)
            with pool.Fori(0, BATCH) as b:
                pool_waits(pool, c, exp_made, b + 2)
                pool.tensor_scalar(out=den[:, :, :], in0=mag[:, :, :], scalar1=1.0, scalar2=-1.0,
                                   op0=ALU.add, op1=ALU.add).then_inc(den_made, 1)
                pool_waits(pool, c, den_made, 2 * b + 1)
                pool.tensor_scalar(out=den[:, :, :], in0=den[:, :, :], scalar1=1e-30, scalar2=None,
                                   op0=ALU.max).then_inc(den_made, 1)
                pool_waits(pool, c, ratio_made, b + 2)
                pool.tensor_tensor(out=log1[:, :, :], in0=log1[:, :, :], in1=mag[:, :, :],
                                   op=ALU.mult).then_inc(sp_step, 1)
                pool_waits(pool, c, sp_step, 2 * b + 1)
                pool.tensor_tensor(out=m.delta[:, bass.ds(b * EC, EC), :], in0=log1[:, :, :], in1=pos[:, :, :],
                                   op=ALU.add).then_inc(sp_step, 1)
                pool_waits(pool, c, sp_step, 2 * b + 2)
                pool.tensor_tensor(out=m.du[:, bass.ds(b * EC, EC), :], in0=m.delta[:, bass.ds(b * EC, EC), :],
                                   in1=m.u[:, bass.ds(b * EC, EC), :], op=ALU.mult).then_inc(delta_made, 1)


def ssm_scan(nc, c, m):
    with ExitStack() as ctx:
        p = Pipe(nc, ctx)
        block = ctx.enter_context(nc.Block())
        bc = p.sb("bc", [P, 2, 2, G, SEQ])
        b_u = p.sb("b_u", [P, 2, G, SEQ])
        state = p.sb("state", [P, 2, G * SEQ])
        c_state = p.sb("c_state", [P, 2, G, SEQ])
        gate = p.sb("gate", [P, EC, SEQ])
        gated = p.sb("gated", [P, EC, SEQ])
        ps_y = [p.ps(f"ps_y{i}", [P, SEQ]) for i in range(EC)]
        ps_t = [p.ps(f"ps_t{i}", [P, DM]) for i in range(ST)]
        filled = p.sem("filled")
        bc_loaded = [p.sem("bc_loaded0"), p.sem("bc_loaded1")]
        decay_made, input_made = p.sem("decay_made"), p.sem("input_made")
        scanned, product_made, product_used = p.sem("scanned"), p.sem("product_made"), p.sem("product_used")
        y_summed, y_gated, gate_made = p.sem("y_summed"), p.sem("y_gated"), p.sem("gate_made")
        y_turned, x_added = p.sem("y_turned"), p.sem("x_added")

        def rows(k, ng, n):
            return m.bc_dram[k, n * DS + ng * G:n * DS + ng * G + G, :]

        @block.sync
        def _(sp):
            def load(k, par, b, ng):
                for n in range(2):
                    src = m.bc_dram[ds1(b), bass.ds(n * DS + ng * G, G), :]\
                        .rearrange("a n l -> a (n l)").broadcast_to([P, G * SEQ])
                    sp.dma_start(bc[:, par, n, :, :].rearrange("p g l -> p (g l)"), src)\
                        .then_inc(bc_loaded[par], 16)
            for k in range(2):
                load(k, k, 0, k)
            with sp.Fori(1, BATCH * NG // 2) as k2:
                for par in range(2):
                    k = k2 * 2 + par
                    sp.wait_ge(product_made, (k - 1) * EC + 2)
                    load(k, par, k // NG, k % NG)
                for dram, skip, n in ((m.rows_dram, 0, FILL), (m.y_dram, MINT, FILL_Y)):
                    sp.dma_start(dram[bass.ds((k2 - 1) * (n * P) + skip * P, n * P), :]
                                 .rearrange("(t p) n -> p t n", p=P),
                                 m.zeros[:, :].rearrange("p (a n) -> p a n", a=1).broadcast_to([P, n, DM]))\
                        .then_inc(filled, 16)
            sp.wait_ge(filled, 2 * 16 * FILLS)

        @block.scalar
        def _(act):
            with act.Fori(0, BATCH) as b:
                with act.Fori(0, NG) as ng:
                    for ec in range(EC):
                        q = (b * NG + ng) * EC + ec
                        act.wait_ge(scanned, q + 1)
                        for g in range(G):
                            e = act.activation(m.d_a[:, ec % 2, g, 1:], m.delta[:, ds1(b * EC + ec), 1:].rearrange("p a l -> p (a l)"),
                                               ACT.Exp, scale=m.a_neg[:, ds1(ec * DS + ng * G + g)])
                        e.then_inc(decay_made, 1)
                act.wait_ge(y_gated, b * EC + EC)
                for ec in range(EC):
                    t = b * ST + ec
                    g = act.activation(gate[:, ec, :], c.X[:, ds1(t), :].rearrange("p a l -> p (a l)"), ACT.Silu,
                                       scale=c.rstd[:, ds1(t)], bias=c.nbias[:, ds1(t)])
                g.then_inc(gate_made, 1)

        @block.gpsimd
        def _(pool):
            with pool.Fori(0, BATCH) as b:
                with pool.Fori(0, NG // 2) as n2:
                    for par in range(2):
                        pool_waits(pool, c, bc_loaded[par], (b * (NG // 2) + n2) * 32 + 32)
                        for ec in range(EC):
                            q = (b * NG + n2 * 2 + par) * EC + ec
                            pool_waits(pool, c, scanned, q + 1)
                            pool.tensor_tensor(out=b_u[:, ec % 2, :, :],
                                               in0=m.du[:, ds1(b * EC + ec), :].broadcast_to([P, G, SEQ]),
                                               in1=bc[:, par, 0, :, :], op=ALU.mult).then_inc(input_made, 1)

        @block.vector
        def _(dve):
            dve.sem_inc(scanned, 2)
            dve.sem_inc(product_made, 2)
            dve.sem_inc(y_gated, EC)
            dve.sem_inc(x_added, 1)
            with dve.Fori(0, BATCH) as b:
                with dve.Fori(0, NG // 2) as n2:
                    for par in range(2):
                        q0 = (b * NG + n2 * 2 + par) * EC
                        dve.wait_ge(bc_loaded[par], (b * (NG // 2) + n2) * 32 + 32)

                        def scan(ec):
                            dve.wait_ge(decay_made, q0 + ec + 1)
                            dve.wait_ge(input_made, q0 + ec + 1)
                            dve.wait_ge(product_made, q0 + ec + 1)
                            dve.tensor_tensor_scan(state[:, ec % 2, :],
                                                   m.d_a[:, ec % 2, :, :].rearrange("p g l -> p (g l)"),
                                                   b_u[:, ec % 2, :, :].rearrange("p g l -> p (g l)"),
                                                   0.0, ALU.mult, ALU.add).then_inc(scanned, 1)

                        def product(ec):
                            dve.wait_ge(scanned, q0 + ec + 3)
                            dve.wait_ge(product_used, q0 + ec + 1)
                            dve.tensor_tensor(out=c_state[:, ec % 2, :, :],
                                              in0=state[:, ec % 2, :].rearrange("p (g l) -> p g l", g=G),
                                              in1=bc[:, par, 1, :, :], op=ALU.mult).then_inc(product_made, 1)

                        scan(0)
                        for ec in range(1, EC):
                            scan(ec)
                            product(ec - 1)
                        product(EC - 1)
                dve.wait_ge(gate_made, b + 1)
                for ec in range(EC):
                    dve.wait_ge(y_summed, b * EC + ec + 1)
                    dve.tensor_tensor(out=gated[:, ec, :], in0=ps_y[ec][:, :], in1=gate[:, ec, :],
                                      op=ALU.mult).then_inc(y_gated, 1)
                dve.wait_ge(y_turned, b + 1)
                for j in range(ST):
                    xt = c.X[:, ds1(b * ST + j), :].rearrange("p a l -> p (a l)")
                    add = dve.tensor_tensor(out=xt, in0=ps_t[j][:, :], in1=xt, op=ALU.add)
                add.then_inc(x_added, 1)

        @block.tensor
        def _(pe):
            pe.sem_inc(product_used, 2)
            with pe.Fori(0, BATCH) as b:
                for ec in range(EC):
                    pe.wait_ge(y_gated, b * EC + ec + 1)
                    pe.matmul(ps_y[ec][:, :], m.d_diag[:, ec, :], m.u[:, ds1(b * EC + ec), :].rearrange("p a l -> p (a l)"),
                              start=True, stop=False)
                with pe.Fori(0, NG) as ng:
                    for ec in range(EC):
                        pe.wait_ge(product_made, (b * NG + ng) * EC + ec + 3)
                        for g in range(G):
                            mm = pe.matmul(ps_y[ec][:, :], c.ident[:, :], c_state[:, ec % 2, g, :],
                                           start=False, stop=False)
                        mm.then_inc(product_used, 1)
                for ec in range(EC):
                    pe.matmul(ps_y[ec][:, 0:2], c.ident[:, :], m.zero2[:, :], start=False, stop=True)\
                        .then_inc(y_summed, 1)
                pe.wait_ge(x_added, b + 1)
                for ec in range(EC):
                    pe.wait_ge(y_gated, b * EC + EC + ec + 1)
                    for j in range(ST):
                        tr = pe.transpose(ps_t[j][:, ec * P:(ec + 1) * P], gated[:, ec, j * P:(j + 1) * P],
                                          c.ident[:, :])
                tr.then_inc(y_turned, 1)


def router_logits(nc, c, m, d):
    with ExitStack() as ctx:
        p = Pipe(nc, ctx)
        block = ctx.enter_context(nc.Block())
        w_gate = p.sb("w_gate", [P, KD, NE])
        xn_t = p.sb("xn_t", [P, 2, KD, P])
        ps_xt = [p.ps(f"ps_xt{i}", [P, KD * P]) for i in range(2)]
        ps_l = [p.ps(f"ps_l{i}", [P, NE]) for i in range(2)]
        gate_loaded, normed = p.sem("gate_loaded"), p.sem("normed")
        xn_turned, xn_t_made = p.sem("xn_turned"), p.sem("xn_t_made")
        logits_made, logits_kept = p.sem("logits_made"), p.sem("logits_kept")

        @block.sync
        def _(sp):
            sp.dma_start(w_gate[:, :, :], d["gate_w"].rearrange("(k p) e -> p k e", p=P)).then_inc(gate_loaded, 16)
            sp.dma_start(m.sim[:, :], d["similarity"]).then_inc(m.sim_loaded, 16)

        @block.vector
        def _(dve):
            with dve.Fori(0, NT) as t:
                row = lambda x: x[:, ds1(t), :].rearrange("p a l -> p (a l)")
                dve.tensor_scalar(out=row(m.xn), in0=row(c.X), scalar1=c.rstd[:, ds1(t)],
                                  scalar2=c.nbias[:, ds1(t)], op0=ALU.mult, op1=ALU.add).then_inc(normed, 1)

        @block.tensor
        def _(pe):
            pe.wait_ge(gate_loaded, 16)
            for t in range(NT + 1):
                if t < NT:
                    pe.wait_ge(normed, t + 1)
                    if t >= 2:
                        pe.wait_ge(xn_t_made, t - 1)
                    for k in range(KD):
                        tr = pe.transpose(ps_xt[t % 2][:, k * P:(k + 1) * P], m.xn[:, t, k * P:(k + 1) * P],
                                          c.ident[:, :])
                    tr.then_inc(xn_turned, 1)
                if t >= 1:
                    s = t - 1
                    pe.wait_ge(xn_t_made, s + 1)
                    if s >= 2:
                        pe.wait_ge(logits_kept, s - 1)
                    for k in range(KD):
                        mm = pe.matmul(ps_l[s % 2][:, :], xn_t[:, s % 2, k, :], w_gate[:, k, :],
                                       start=k == 0, stop=k == KD - 1)
                    mm.then_inc(logits_made, 1)

        @block.scalar
        def _(act):
            for t in range(NT + 1):
                if t < NT:
                    act.wait_ge(xn_turned, t + 1)
                    if t >= 2:
                        act.wait_ge(logits_made, t - 1)
                    act.activation(xn_t[:, t % 2, :, :].rearrange("p k l -> p (k l)"), ps_xt[t % 2][:, :],
                                   ACT.Copy).then_inc(xn_t_made, 1)
                if t >= 1:
                    act.wait_ge(logits_made, t)
                    act.activation(m.logits[:, t - 1, :], ps_l[(t - 1) % 2][:, :], ACT.Copy)\
                        .then_inc(logits_kept, 1)


def route(nc, c, m):
    with ExitStack() as ctx:
        p = Pipe(nc, ctx)
        block = ctx.enter_context(nc.Block())
        iota_e = p.sb("iota_e", [P, NT, NE])
        tile_no = p.sb("tile_no", [P, 2])
        expert_no = p.sb("expert_no", [NE, 1])
        ones = p.sb("ones", [P, P], BF16)
        before = p.sb("before", [P, P], BF16)
        line1 = p.sb("line1", [P, NE])
        most, total = p.sb("most", [P, NT]), p.sb("total", [P, NT])
        top = p.sb("top", [P, NT, TOPK])
        idx = p.sb("idx", [P, NT, TOPK], U32)
        idx_f = p.sb("idx_f", [P, NT, TOPK])
        chosen = p.sb("chosen", [P, TOPK, NT, NE], BF16)
        tmp = p.sb("tmp", [P, NT, NE])
        first = p.sb("first", [P, NT, NE], BF16)
        second = p.sb("second", [P, NT, NE], BF16)
        ahead = p.sb("ahead", [P, NT + 1, NE], BF16)
        mask, cand = p.sb("mask", [NE, NE]), p.sb("cand", [NE, NE])
        best8, best_i = p.sb("best8", [NE, 8]), p.sb("best_i", [NE, 8], U32)
        r1, r2 = p.sb("r1", [NE, 1]), p.sb("r2", [NE, 1])
        map_col, map_b = p.sb("map_col", [NE, 1]), p.sb("map_b", [NE, P])
        map_row = p.sb("map_row", [P, NE])
        cnt_i, tiles = p.sb("cnt_i", [P, NE], I32), p.sb("tiles", [P, NE])
        end, base = p.sb("end", [P, NE]), p.sb("base", [P, NE])
        row_of = p.sb("row_of", [P, NT, NE])
        pos_f = p.sb("pos_f", [P, TOPK, NT])
        lt = p.sb("lt", [P, 2, NE])
        te = p.sb("te", [P, 2])
        te_row, packed = p.sb("te_row", [1, 2 * P]), p.sb("packed", [1, P])
        ps_first = p.ps("ps_first", [P, NE])
        ps_fc, ps_sc = p.ps("ps_fc", [NE, 1]), p.ps("ps_sc", [NE, 1])
        ps_map = p.ps("ps_map", [P, NE])
        ps_row = [p.ps(f"ps_row{i}", [P, NT * NE // 2]) for i in range(2)]
        ps_cnt = p.ps("ps_cnt", [P, NE])
        ps_te = p.ps("ps_te", [1, 2 * P])
        consts, dve_step, exp_done = p.sem("consts"), p.sem("dve_step"), p.sem("exp_done")
        shifted, chosen_made, counted = p.sem("shifted"), p.sem("chosen_made"), p.sem("counted")
        mapped, map_spread, all_made = p.sem("mapped"), p.sem("map_spread"), p.sem("all_made")
        rows_made, te_made, te_turned = p.sem("rows_made"), p.sem("te_made"), p.sem("te_turned")
        diag_set = p.sem("diag_set")
        H = NT // 2

        @block.gpsimd
        def _(pool):
            pool.memset(before[:, :], 1.0).then_inc(diag_set, 1)
            pool.iota(iota_e[:, :, :], pattern=[[0, NT], [1, NE]], base=0, channel_multiplier=0,
                      allow_small_or_imprecise_dtypes=True)
            pool.iota(tile_no[:, :], pattern=[[P, 2]], base=0, channel_multiplier=1,
                      allow_small_or_imprecise_dtypes=True)
            pool.iota(expert_no[:, :], pattern=[[0, 1]], base=0, channel_multiplier=1,
                      allow_small_or_imprecise_dtypes=True)
            pool.memset(ones[:, :], 1.0)
            pool.memset(line1[:, :], 1.0)
            pool.memset(ahead[:, 0, :], 0.0)
            pool.wait_ge(diag_set, 1)
            pool.affine_select(out=before[:, :], in_=before[:, :], compare_op=ALU.is_gt, fill=0.0,
                               base=0, pattern=[[1, P]], channel_multiplier=-1)
            pool.wait_ge(m.sim_loaded, 16)
            pool.affine_select(out=m.sim[:, :], in_=m.sim[:, :], compare_op=ALU.not_equal, fill=1.0,
                               base=0, pattern=[[-1, NE]], channel_multiplier=1).then_inc(consts, 1)

        @block.scalar
        def _(act):
            act.wait_ge(shifted, 1)
            act.activation(m.logits[:, :, :], m.logits[:, :, :], ACT.Exp).then_inc(exp_done, 1)

        @block.vector
        def _(dve):
            n = [0]

            def link(ins):
                n[0] += 1
                ins.then_inc(dve_step, 1)
                dve.wait_ge(dve_step, n[0])

            def spread(x, last=NE):
                return x.rearrange("p (a b) -> p a b", b=1).broadcast_to([x.shape[0], x.shape[1], last])

            link(dve.tensor_reduce(most[:, :], m.logits[:, :, :], AX.X, ALU.max))
            dve.tensor_tensor(out=m.logits[:, :, :], in0=m.logits[:, :, :], in1=spread(most[:, :]),
                              op=ALU.subtract).then_inc(shifted, 1)
            dve.wait_ge(exp_done, 1)
            link(dve.tensor_reduce(total[:, :], m.logits[:, :, :], AX.X, ALU.add))
            link(dve.reciprocal(total[:, :], total[:, :]))
            link(dve.tensor_tensor(out=m.logits[:, :, :], in0=m.logits[:, :, :], in1=spread(total[:, :]),
                                   op=ALU.mult))
            for t in range(NT):
                mx = dve.max(top[:, t, :], m.logits[:, t, :])
            link(mx)
            for t in range(NT):
                mi = dve.max_index(idx[:, t, :], top[:, t, :], m.logits[:, t, :])
            link(mi)
            link(dve.tensor_reduce(total[:, :], top[:, :, :], AX.X, ALU.add))
            link(dve.tensor_scalar(out=total[:, :], in0=total[:, :], scalar1=1e-12, scalar2=None, op0=ALU.max))
            link(dve.reciprocal(total[:, :], total[:, :]))
            link(dve.tensor_tensor(out=m.weight[:, :, :], in0=top[:, :, :], in1=spread(total[:, :], TOPK),
                                   op=ALU.mult))
            link(dve.tensor_copy(idx_f[:, :, :], idx[:, :, :]))
            dve.wait_ge(consts, 1)

            def one_hot(k):
                return dve.tensor_tensor(out=chosen[:, k, :, :], in0=spread(idx_f[:, :, k]),
                                         in1=iota_e[:, :, :], op=ALU.is_equal)

            for k in range(TOPK):
                oh = one_hot(k)
            link(oh)

            def add(out, a, b):
                return dve.tensor_tensor(out=out, in0=a, in1=b, op=ALU.add)

            for out, k0 in ((first, 0), (second, SELK)):
                link(add(out[:, :, :], chosen[:, k0, :, :], chosen[:, k0 + 1, :, :]))
                link(add(out[:, :, :], out[:, :, :], chosen[:, k0 + 2, :, :]))
                link(add(out[:, :, :], out[:, :, :], chosen[:, k0 + 3, :, :]))
            dve.sem_inc(chosen_made, 1)
            dve.wait_ge(counted, 1)
            link(dve.tensor_scalar(out=mask[:, :], in0=ps_first[0:NE, :], scalar1=1.0, scalar2=None,
                                   op0=ALU.min))
            link(dve.tensor_tensor(out=cand[:, :], in0=m.sim[:, :], in1=mask[:, :], op=ALU.mult))
            link(dve.tensor_scalar(out=mask[:, :], in0=mask[:, :], scalar1=-1.0, scalar2=1e30,
                                   op0=ALU.add, op1=ALU.mult))
            link(add(cand[:, :], cand[:, :], mask[:, :]))
            link(dve.max(best8[:, :], cand[:, :]))
            link(dve.max_index(best_i[:, :], best8[:, :], cand[:, :]))
            link(dve.tensor_copy(map_col[:, :], best_i[:, 0:1]))
            link(dve.tensor_scalar(out=r1[:, :], in0=ps_fc[:, :], scalar1=0.0, scalar2=None, op0=ALU.is_equal))
            link(dve.tensor_scalar(out=r2[:, :], in0=ps_sc[:, :], scalar1=0.0, scalar2=None, op0=ALU.is_gt))
            link(dve.tensor_tensor(out=r1[:, :], in0=r1[:, :], in1=r2[:, :], op=ALU.mult))
            link(dve.tensor_scalar(out=r2[:, :], in0=best8[:, 0:1], scalar1=THRESH, scalar2=None, op0=ALU.is_ge))
            link(dve.tensor_tensor(out=r1[:, :], in0=r1[:, :], in1=r2[:, :], op=ALU.mult))
            link(dve.tensor_tensor(out=map_col[:, :], in0=map_col[:, :], in1=expert_no[:, :], op=ALU.subtract))
            link(dve.tensor_tensor(out=map_col[:, :], in0=map_col[:, :], in1=r1[:, :], op=ALU.mult))
            link(add(map_col[:, :], map_col[:, :], expert_no[:, :]))
            dve.tensor_copy(map_b[:, :], map_col[:, :].broadcast_to([NE, P])).then_inc(mapped, 1)
            dve.wait_ge(map_spread, 1)
            link(dve.tensor_copy(map_row[:, :], ps_map[:, :]))
            map_all = map_row[:, :].rearrange("p (a e) -> p a e", a=1).broadcast_to([P, NT, NE])
            for k in range(SELK, TOPK):
                link(dve.tensor_tensor(out=tmp[:, :, :], in0=chosen[:, k, :, :], in1=map_all, op=ALU.mult))
                link(dve.tensor_reduce(idx_f[:, :, k], tmp[:, :, :], AX.X, ALU.add))
                link(one_hot(k))
            for k in range(SELK, TOPK):
                link(add(first[:, :, :], first[:, :, :], chosen[:, k, :, :]))
            for t in range(NT):
                link(add(ahead[:, t + 1, :], ahead[:, t, :], first[:, t, :]))
            dve.sem_inc(all_made, 1)
            dve.wait_ge(rows_made, 1)
            link(dve.tensor_scalar(out=cnt_i[:, :], in0=ps_cnt[:, :], scalar1=float(P - 1), scalar2=None,
                                   op0=ALU.add))
            link(dve.tensor_scalar(out=cnt_i[:, :], in0=cnt_i[:, :], scalar1=7, scalar2=None,
                                   op0=ALU.logical_shift_right))
            link(dve.tensor_scalar(out=tiles[:, :], in0=cnt_i[:, :], scalar1=1.0, scalar2=None, op0=ALU.max))
            link(dve.tensor_tensor_scan(end[:, :], line1[:, :], tiles[:, :], 0.0, ALU.mult, ALU.add))
            link(dve.tensor_tensor(out=base[:, :], in0=end[:, :], in1=tiles[:, :], op=ALU.subtract))
            link(dve.tensor_scalar(out=base[:, :], in0=base[:, :], scalar1=float(P), scalar2=None, op0=ALU.mult))
            base_all = base[:, :].rearrange("p (a e) -> p a e", a=1).broadcast_to([P, H, NE])
            for h in range(2):
                link(add(row_of[:, h * H:(h + 1) * H, :],
                         ps_row[h][:, :].rearrange("p (t e) -> p t e", e=NE), base_all))
            link(dve.tensor_tensor(out=lt[:, :, :],
                                   in0=end[:, :].rearrange("p (a e) -> p a e", a=1).broadcast_to([P, 2, NE]),
                                   in1=spread(tile_no[:, :]), op=ALU.is_le))
            link(dve.tensor_reduce(te[:, :], lt[:, :, :], AX.X, ALU.add))
            dve.tensor_scalar(out=te[:, :], in0=te[:, :], scalar1=float(NE - 1), scalar2=None,
                              op0=ALU.min).then_inc(te_made, 1)
            for k in range(TOPK):
                link(dve.tensor_tensor(out=tmp[:, :, :], in0=chosen[:, k, :, :], in1=row_of[:, :, :],
                                       op=ALU.mult))
                link(dve.tensor_reduce(pos_f[:, k, :], tmp[:, :, :], AX.X, ALU.add))
                link(add(row_of[:, :, :], row_of[:, :, :], chosen[:, k, :, :]))
            link(dve.tensor_copy(m.pos[:, :, :], pos_f[:, :, :]))
            dve.wait_ge(te_turned, 1)
            tile_pairs = te_row[:, 0:2 * P].rearrange("p (j two) -> p j two", two=2)
            link(dve.tensor_copy(te_row[:, 0:2 * P], ps_te[:, :]))
            link(dve.scalar_tensor_tensor(out=packed[:, :], in0=tile_pairs[:, :, 1], scalar=float(1 << EB),
                                          in1=tile_pairs[:, :, 0], op0=ALU.mult, op1=ALU.add))
            link(dve.scalar_tensor_tensor(out=packed[:, 0:P - 1], in0=tile_pairs[:, 1:P, 0],
                                          scalar=float(1 << 2 * EB), in1=packed[:, 0:P - 1],
                                          op0=ALU.mult, op1=ALU.add))
            dve.tensor_copy(m.table[:, 0:P], packed[:, :])
            dve.tensor_copy(m.table[:, T_END:T_END + NE], end[0:1, :])
            link(dve.tensor_scalar(out=cnt_i[0:1, 0:1], in0=end[0:1, NE - 1:NE], scalar1=1.0, scalar2=None,
                                   op0=ALU.add))
            dve.tensor_scalar(out=m.table[:, T_PAIRS:T_PAIRS + 1], in0=cnt_i[0:1, 0:1], scalar1=1,
                              scalar2=None, op0=ALU.logical_shift_right)

        @block.tensor
        def _(pe):
            pe.wait_ge(consts, 1)
            pe.wait_ge(chosen_made, 1)
            for t in range(NT):
                st = dict(start=t == 0, stop=t == NT - 1)
                pe.matmul(ps_first[:, :], ones[:, :], first[:, t, :], **st)
                pe.matmul(ps_fc[:, :], first[:, t, :], ones[:, 0:1], **st)
                mm = pe.matmul(ps_sc[:, :], second[:, t, :], ones[:, 0:1], **st)
            mm.then_inc(counted, 1)
            pe.wait_ge(mapped, 1)
            pe.matmul(ps_map[:, :], map_b[:, :], c.ident[0:NE, 0:NE], start=True, stop=True).then_inc(map_spread, 1)
            pe.wait_ge(all_made, 1)
            for h in range(2):
                pe.matmul(ps_row[h][:, :], before[:, :],
                          first[:, h * H:(h + 1) * H, :].rearrange("p t e -> p (t e)"), start=True, stop=False)
                pe.matmul(ps_row[h][:, :], ones[:, :],
                          ahead[:, h * H:(h + 1) * H, :].rearrange("p t e -> p (t e)"), start=False, stop=True)
            pe.matmul(ps_cnt[:, :], ones[:, :], ahead[:, NT, :], start=True, stop=True).then_inc(rows_made, 1)
            pe.wait_ge(te_made, 1)
            for h in range(2):
                mm = pe.matmul(ps_te[:, h * P:(h + 1) * P], te[:, h:h + 1], c.ident[:, :], start=True, stop=True)
            mm.then_inc(te_turned, 1)


def dispatch(nc, c, m):
    with ExitStack() as ctx:
        sent = Pipe(nc, ctx).sem("sent")
        block = ctx.enter_context(nc.Block())

        @block.gpsimd
        def _(pool):
            for t in range(NT):
                for k in range(TOPK):
                    pool.indirect_dma_start(m.rows_dram, bass.IndirectOffsetOnAxis(ap=m.pos[:, k, t:t + 1], axis=0),
                                            m.xn[:, t, :], None).then_inc(sent, 16)
            pool.wait_ge(sent, 16 * NT * TOPK)


def experts(nc, c, m, d):
    with ExitStack() as ctx:
        p = Pipe(nc, ctx)
        block = ctx.enter_context(nc.Block())
        w_gu = p.sb("w_gu", [P, 2, KD, 2 * FI])
        w_dn = p.sb("w_dn", [FI // 2, 2, 2, DM])
        rows = [p.sb(f"rows{i}", [P, DM]) for i in range(2)]
        rows_t = [p.sb(f"rows_t{i}", [P, KD, P]) for i in range(2)]
        silu_g = [p.sb(f"silu_g{i}", [P, FI]) for i in range(2)]
        hid = [p.sb(f"hid{i}", [P, FI]) for i in range(2)]
        hid_t = [p.sb(f"hid_t{i}", [FI // 2, 2, P]) for i in range(2)]
        y = [p.sb(f"y{i}", [P, DM]) for i in range(2)]
        ps_x = [p.ps(f"ps_rx{i}", [P, KD * P]) for i in range(2)]
        ps_gu = [p.ps(f"ps_gu{i}", [P, 2 * FI]) for i in range(2)]
        ps_h = [p.ps(f"ps_h{i}", [FI // 2, 2 * P]) for i in range(2)]
        ps_o = [p.ps(f"ps_o{i}", [P, DM]) for i in range(2)]
        w_loaded, w_ready = [p.sem("w_loaded0"), p.sem("w_loaded1")], p.sem("w_ready")
        rows_loaded = [p.sem("rows_loaded0"), p.sem("rows_loaded1")]
        y_stored = [p.sem("y_stored0"), p.sem("y_stored1")]
        ended = p.sem("ended")
        rows_turned = p.sem("rows_turned")
        rows_t_made = p.sem("rows_t_made")
        gu_made = p.sem("gu_made")
        silu_made = p.sem("silu_made")
        hid_made = p.sem("hid_made")
        hid_turned = p.sem("hid_turned")
        hid_t_made = p.sem("hid_t_made")
        out_made = p.sem("out_made")
        y_made = p.sem("y_made")

        def pairs(eng):
            return eng.value_load(m.table[0:1, T_PAIRS:T_PAIRS + 1], min_val=NE // 2, max_val=MAXT // 2)

        @block.gpsimd
        def _(pool):
            def load(e, slot):
                pool.dma_start(w_gu[:, slot, :, :].rearrange("p k f -> p (k f)"),
                               d["gate_up"][ds1(e), :, :].rearrange("a p f -> (a p) f")).then_inc(w_loaded[slot], 16)
                pool.dma_start(w_dn[:, slot, :, :].rearrange("p k f -> p (k f)"),
                               d["down"][ds1(e), :, :].rearrange("a p f -> (a p) f")).then_inc(w_loaded[slot], 16)

            load(0, 0)
            load(1, 1)
            for slot in range(2):
                pool.wait_ge(w_loaded[slot], 32).then_inc(w_ready, 1)
            with pool.Fori(1, NE // 2) as e2:
                for slot in range(2):
                    done = pool.value_load(m.table[0:1, bass.ds(e2 * 2 + (T_END + slot - 2), 1)], min_val=1,
                                           max_val=MAXT)
                    pool_waits(pool, c, out_made, done + 2)
                    load(e2 * 2 + slot, slot)
                    pool.wait_ge(w_loaded[slot], e2 * 32 + 32).then_inc(w_ready, 1)

        @block.sync
        def _(sp):
            np = pairs(sp)

            def load(i, par):
                sp.dma_start(rows[par][:, :], m.rows_dram[bass.ds(i * P, P), :]).then_inc(rows_loaded[par], 16)
            sp.sem_inc(y_stored[0], 16)
            sp.sem_inc(y_stored[1], 16)
            load(0, 0)
            load(1, 1)

            def next_load(i, par):
                sp.wait_ge(rows_turned, i + 1)
                load(i + 2, par)

            def store(i, par):
                sp.wait_ge(y_made, i + 3)
                sp.dma_start(m.y_dram[bass.ds(i * P, P), :], y[par][:, :]).then_inc(y_stored[par], 16)

            next_load(0, 0)
            next_load(1, 1)
            store(0, 0)
            with sp.Fori(1, np) as j:
                for par in range(2):
                    i = j * 2 + par
                    next_load(i, par)
                    store(i - 1, 1 - par)
            store(np * 2 - 1, 1)
            for par in range(2):
                sp.wait_ge(y_stored[par], np * 16 + 16).then_inc(ended, 1)
                sp.wait_ge(rows_loaded[par], np * 16 + 16).then_inc(ended, 1)

        @block.tensor
        def _(pe):
            for s in (gu_made, hid_turned, out_made):
                pe.sem_inc(s, 2)

            def turn_rows(i, j, par, first=False):
                pe.wait_ge(rows_loaded[par], j * 16 + 16)
                pe.wait_ge(rows_t_made, i + 1)
                for k in range(KD):
                    tr = pe.transpose(ps_x[par][:, k * P:(k + 1) * P], rows[par][:, k * P:(k + 1) * P],
                                      c.ident[:, :])
                tr.then_inc(rows_turned, 1)

            def gate_up(i, par, e, slot):
                pe.wait_ge(w_ready, e + 1)
                pe.wait_ge(rows_t_made, i + 3)
                pe.wait_ge(hid_made, i + 1)
                for k in range(KD):
                    mm = pe.matmul(ps_gu[par][:, :], rows_t[par][:, k, :],
                                   w_gu[:, ds1(slot), k, :].rearrange("p a f -> p (a f)"),
                                   start=k == 0, stop=k == KD - 1)
                mm.then_inc(gu_made, 1)

            def turn_hidden(i, par):
                pe.wait_ge(hid_made, i + 3)
                pe.wait_ge(hid_t_made, i + 1)
                for k in range(2):
                    tr = pe.transpose(ps_h[par][:, k * P:(k + 1) * P],
                                      hid[par][:, k * FI // 2:(k + 1) * FI // 2], c.ident[:, :])
                tr.then_inc(hid_turned, 1)

            def down(i, par, slot):
                pe.wait_ge(hid_t_made, i + 3)
                pe.wait_ge(y_made, i + 1)
                for k in range(2):
                    mm = pe.matmul(ps_o[par][:, :], hid_t[par][:, k, :],
                                   w_dn[:, ds1(slot), k, :].rearrange("p a f -> p (a f)"),
                                   start=k == 0, stop=k == 1)
                mm.then_inc(out_made, 1)

            np = pairs(pe)
            turn_rows(0, 0, 0)
            gate_up(0, 0, 0, 0)
            turn_rows(1, 0, 1)
            turn_hidden(0, 0)
            with pe.Fori(0, np) as j:
                word = pe.value_load(m.table[0:1, ds1(j)], min_val=0, max_val=(1 << 3 * EB) - 1)
                of_tile = [word & (NE - 1), (word >> EB) & (NE - 1), word >> 2 * EB]
                slots = [e & 1 for e in of_tile]
                for par in range(2):
                    i = j * 2 + par
                    gate_up(i + 1, 1 - par, of_tile[par + 1], slots[par + 1])
                    turn_rows(i + 2, j + 1, par)
                    down(i, par, slots[par])
                    turn_hidden(i + 1, 1 - par)

        @block.scalar
        def _(act):
            act.sem_inc(rows_t_made, 2)

            def keep_rows(i, par):
                act.wait_ge(rows_turned, i + 1)
                act.wait_ge(gu_made, i + 1)
                act.activation(rows_t[par][:, :, :].rearrange("p k l -> p (k l)"), ps_x[par][:, :],
                               ACT.Copy).then_inc(rows_t_made, 1)

            def silu(i, par):
                act.wait_ge(gu_made, i + 3)
                act.wait_ge(hid_made, i + 1)
                act.activation(silu_g[par][:, :], ps_gu[par][:, 0:FI], ACT.Silu).then_inc(silu_made, 1)

            np = pairs(act)
            keep_rows(0, 0)
            silu(0, 0)
            keep_rows(1, 1)
            with act.Fori(0, np) as j:
                for par in range(2):
                    i = j * 2 + par
                    silu(i + 1, 1 - par)
                    keep_rows(i + 2, par)

        @block.vector
        def _(dve):
            for s in (hid_made, hid_t_made, y_made):
                dve.sem_inc(s, 2)

            def hidden(i, par):
                dve.wait_ge(silu_made, i + 1)
                dve.wait_ge(hid_turned, i + 1)
                dve.tensor_tensor(out=hid[par][:, :], in0=silu_g[par][:, :], in1=ps_gu[par][:, FI:2 * FI],
                                  op=ALU.mult).then_inc(hid_made, 1)

            def keep_hidden(i, par):
                dve.wait_ge(hid_turned, i + 3)
                dve.wait_ge(out_made, i + 1)
                dve.tensor_copy(hid_t[par][:, :, :].rearrange("p k l -> p (k l)"), ps_h[par][:, :])\
                    .then_inc(hid_t_made, 1)

            def keep_out(i, j, par):
                dve.wait_ge(out_made, i + 3)
                dve.wait_ge(y_stored[par], j * 16 + 16)
                dve.tensor_copy(y[par][:, :], ps_o[par][:, :]).then_inc(y_made, 1)

            np = pairs(dve)
            hidden(0, 0)
            keep_hidden(0, 0)
            with dve.Fori(0, np) as j:
                for par in range(2):
                    i = j * 2 + par
                    hidden(i + 1, 1 - par)
                    keep_out(i, j, par)
                    keep_hidden(i + 1, 1 - par)


def combine(nc, c, m):
    with ExitStack() as ctx:
        p = Pipe(nc, ctx)
        block = ctx.enter_context(nc.Block())
        got = p.sb("got", [P, 2 * TOPK, DM])
        arrived = [p.sem(f"arrived{i}") for i in range(2 * TOPK)]
        added = p.sem("added")

        @block.gpsimd
        def _(pool):
            for t in range(NT):
                for k in range(TOPK):
                    n, slot = t * TOPK + k, (t % 2) * TOPK + k
                    if t >= 2:
                        pool.wait_ge(added, n - 2 * TOPK + 1)
                    pool.indirect_dma_start(got[:, slot, :], None, m.y_dram,
                                            bass.IndirectOffsetOnAxis(ap=m.pos[:, k, t:t + 1], axis=0))\
                        .then_inc(arrived[slot], 16)

        @block.vector
        def _(dve):
            for t in range(NT):
                for k in range(TOPK):
                    n, slot = t * TOPK + k, (t % 2) * TOPK + k
                    dve.wait_ge(arrived[slot], 16 * (t // 2 + 1))
                    if k:
                        dve.wait_ge(added, n)
                    dve.scalar_tensor_tensor(out=c.X[:, t, :], in0=got[:, slot, :],
                                             scalar=m.weight[:, t, k:k + 1], in1=c.X[:, t, :],
                                             op0=ALU.mult, op1=ALU.add).then_inc(added, 1)


def wait(eng, sem, value):
    if not isinstance(value, int) or value > 0:
        eng.wait_ge(sem, value)


def turn_tokens(nc, c, m, d):
    with ExitStack() as ctx:
        p = Pipe(nc, ctx)
        block = ctx.enter_context(nc.Block())
        xn = p.sb("a_xn", [P, NT, DM])
        xn_t = p.sb("a_xn_t", [P, 2, KD, SEQ])
        g_q, g_k = p.sb("g_q", [P, 1]), p.sb("g_k", [P, 1])
        ps_xt = [p.ps(f"ps_at{i}", [P, KD * P]) for i in range(2)]
        normed, turned, kept = (p.sem(x) for x in ("a_normed", "a_turned", "a_kept"))
        stored = [p.sem("a_stored0"), p.sem("a_stored1")]
        gains = p.sem("gains")

        @block.sync
        def _(sp):
            with nc.allow_non_contiguous_dma(reason="one value a partition"):
                sp.dma_start(g_q[:, :], d["g_q"].rearrange("(p a) -> p a", a=1)).then_inc(gains, 16)
                sp.dma_start(g_k[:, :], d["g_k"].rearrange("(p a) -> p a", a=1)).then_inc(gains, 16)
            for b in range(BATCH):
                sp.wait_ge(kept, ST * (b + 1))
                sp.dma_start(m.xn_dram[b * P:(b + 1) * P, :], xn_t[:, b % 2, :, :].rearrange("p k l -> p (k l)"))\
                    .then_inc(stored[b % 2], 16)
            for s in stored:
                sp.wait_ge(s, 16 * BATCH // 2)

        @block.vector
        def _(dve):
            with dve.Fori(0, NT) as t:
                row = lambda x: x[:, ds1(t), :].rearrange("p a l -> p (a l)")
                dve.tensor_scalar(out=row(xn), in0=row(c.X), scalar1=c.rstd[:, ds1(t)],
                                  scalar2=c.nbias[:, ds1(t)], op0=ALU.mult, op1=ALU.add).then_inc(normed, 1)
            dve.wait_ge(gains, 32)
            dve.scalar_tensor_tensor(out=m.gain[:, :], in0=g_q[:, :], scalar=HD ** 0.5, in1=g_k[:, :],
                                     op0=ALU.mult, op1=ALU.mult)

        @block.tensor
        def _(pe):
            for t in range(NT):
                pe.wait_ge(normed, t + 1)
                wait(pe, kept, t - 1)
                for k in range(KD):
                    tr = pe.transpose(ps_xt[t % 2][:, k * P:(k + 1) * P], xn[:, t, k * P:(k + 1) * P],
                                      c.ident[:, :])
                tr.then_inc(turned, 1)

        @block.scalar
        def _(act):
            for t in range(NT):
                b, j = t // ST, t % ST
                act.wait_ge(turned, t + 1)
                wait(act, stored[b % 2], 16 * (b // 2))
                act.activation(xn_t[:, b % 2, :, j * P:(j + 1) * P],
                               ps_xt[t % 2][:, :].rearrange("p (k l) -> p k l", k=KD), ACT.Copy).then_inc(kept, 1)


def attention(nc, c, m, d):
    with ExitStack() as ctx:
        p = Pipe(nc, ctx)
        block = ctx.enter_context(nc.Block())

        def halves(name, shape):
            return p.sb(name + "_high", shape, F32R), p.sb(name + "_low", shape, F32R)

        w_q, w_k = halves("w_q", [P, 2, KD, HD]), halves("w_k", [P, 2, KC, HD])
        w_v, w_o = halves("w_v", [P, KC, 2 * HD]), halves("w_o", [P, 2, DM])
        x_t = halves("x_t", [P, 2, KD + KC, SEQ])
        q_t, k_t = halves("q_t", [P, 2, SEQ]), halves("k_t", [P, 2, SEQ])
        v_s = halves("v_s", [P, 2, ST, 2 * HD])
        prob_t = halves("prob_t", [P, ST, SEQ])
        o_t = halves("o_t", [P, 2, SEQ])
        raw_x, raw_w = p.sb("raw_x", [P, 2, 3, SEQ]), p.sb("raw_w", [P, 2, 2 * DM])
        prob = p.sb("prob", [P, ST, SEQ])
        q_sq, k_sq = p.sb("q_sq", [P, SEQ]), p.sb("k_sq", [P, SEQ])
        k_raw = p.sb("k_raw", [P, SEQ])
        k_ms, k_rs = p.sb("k_ms", [P, ST]), p.sb("k_rs", [P, ST])
        k_diag = p.sb("k_diag", [P, ST, P])
        q_ms, q_rs = p.sb("q_ms", [P, ST]), p.sb("q_rs", [P, 2, ST])
        ones = p.sb("a_ones", [P, P])
        high, neg, den, rden = (p.sb(x, [P, ST]) for x in ("high", "neg", "a_den", "rden"))
        ps_s = [p.ps(f"ps_s{i}", [P, SEQ]) for i in range(2)]
        ps_p = [p.ps(f"ps_p{i}", [P, SEQ]) for i in range(2)]
        ps_a, ps_b = p.ps("ps_pa", [P, SEQ]), p.ps("ps_pb", [P, SEQ])
        ps_o, ps_y = p.ps("ps_o", [P, SEQ]), p.ps("ps_yo", [P, DM])
        x_loaded = [p.sem("xt_loaded0"), p.sem("xt_loaded1")]
        w_loaded = [p.sem("aw_loaded0"), p.sem("aw_loaded1")]
        x_high, x_low = p.sem("x_high"), p.sem("x_low")
        w_high, w_low = p.sem("w_high"), p.sem("w_low")
        k_made, k_evac, ksum_made, k_mean = p.sem("k_made"), p.sem("k_evac"), p.sem("ksum_made"), p.sem("k_mean")
        k_rooted, k_diag_made, krow_made = p.sem("k_rooted"), p.sem("k_diag_made"), p.sem("krow_made")
        k_normed, k_high, k_low = p.sem("k_normed"), p.sem("k_high"), p.sem("k_low")
        q_made, q_high, q_low = p.sem("q_made"), p.sem("q_high"), p.sem("q_low")
        qsum_made, q_mean, q_rooted = p.sem("qsum_made"), p.sem("q_mean"), p.sem("q_rooted")
        v_made, v_high, v_low = p.sem("v_made2"), p.sem("v_high"), p.sem("v_low")
        s_made, high_made, neg_made = p.sem("s_made"), p.sem("high_made"), p.sem("neg_made")
        exp_done, rden_made, p_normed = p.sem("exp_done2"), p.sem("rden_made"), p.sem("p_normed")
        p_turned, p_high, p_low = p.sem("p_turned"), p.sem("p_high"), p.sem("p_low")
        pv_made, o_high, o_low = p.sem("pv_made"), p.sem("o_high"), p.sem("o_low")
        y_made, y_added = p.sem("wo_made"), p.sem("y_added")
        consts = p.sem("a_consts")
        HALF_W = HD * KD
        QK0, WV, QK1, WO = range(4)

        def schedule(eng, prologue, unit):
            prologue(eng)
            for k in range(UP):
                unit(eng, 0, k)
            with eng.Fori(1, NP - 1) as hp:
                for k in range(UP):
                    unit(eng, hp, k)
            for k in range(UP):
                unit(eng, NP - 1, k)

        def prepares(hp, k):
            return not (isinstance(hp, int) and hp == NP - 1 and k == UP - 1)

        def splits(hp, k):
            return not (isinstance(hp, int) and hp == NP - 1 and k + 3 >= UP)

        def weight_parts(hp, k):
            last, first = isinstance(hp, int) and hp == NP - 1, isinstance(hp, int) and hp == 0
            if k == 1 and not first:
                return [], [(hp, WO)]
            if k == UP - 2 and not last:
                return [], [(hp + 1, QK0)]
            if k == UP - 1 and not last:
                return [(hp + 1, WV)], [(hp + 1, QK1)]
            return [], []

        def part_pieces(part):
            raw = raw_w[:, part % 2, :]
            if part == WO:
                return [tuple(w.rearrange("p k n -> p (k n)") for w in (w_o[0][:, :, :], w_o[1][:, :, :])) + (raw,)]
            if part == WV:
                n = KC * 2 * HD
                return [tuple(w.rearrange("p k n -> p (k n)") for w in (w_v[0][:, :, :], w_v[1][:, :, :]))
                        + (raw[:, 0:n],)]
            h = 0 if part == QK0 else 1
            return [tuple(w.rearrange("p k n -> p (k n)") for w in (w_q[0][:, h], w_q[1][:, h]))
                    + (raw[:, 0:HALF_W],),
                    tuple(w.rearrange("p k n -> p (k n)") for w in (w_k[0][:, h], w_k[1][:, h]))
                    + (raw[:, HALF_W:HALF_W + KC * HD],)]

        @block.sync
        def _(sp):
            def load_x(s):
                b = (s // 2) % BATCH
                wait(sp, x_low, 3 * (s - 1))
                rows = m.xn_dram[b * P:(b + 1) * P, :]
                if s % 2 == 0:
                    sp.dma_start(raw_x[:, 0, :, :].rearrange("p k l -> p (k l)"), rows[:, 0:3 * SEQ])\
                        .then_inc(x_loaded[0], 16)
                else:
                    sp.dma_start(raw_x[:, 1, 0, :], rows[:, 3 * SEQ:4 * SEQ]).then_inc(x_loaded[1], 16)
                    sp.dma_start(raw_x[:, 1, 1:3, :],
                                 d["ctx_t"][b * CD:(b + 1) * CD, :].rearrange("(k p) l -> p k l", p=P))\
                        .then_inc(x_loaded[1], 16)

            def load_w(hp, part):
                cols = slice(hp * 2 * HD, (hp + 1) * 2 * HD)
                wait(sp, w_low, 4 * hp + part - 1)
                out, done = raw_w[:, part % 2, :], w_loaded[part % 2]
                if part == WO:
                    sp.dma_start(out.rearrange("p (k n) -> p k n", k=2),
                                 d["w_o"][cols, :].rearrange("(k p) n -> p k n", p=P)).then_inc(done, 16)
                elif part == WV:
                    sp.dma_start(out[:, 0:KC * 2 * HD].rearrange("p (k n) -> p k n", k=KC),
                                 d["w_v"][:, cols].rearrange("(k p) n -> p k n", p=P)).then_inc(done, 16)
                else:
                    h = hp * 2 + (part == QK1)
                    sp.dma_start(out[:, 0:HALF_W].rearrange("p (k n) -> p k n", k=KD),
                                 d["w_q"][:, h * HD:(h + 1) * HD].rearrange("(k p) n -> p k n", p=P))\
                        .then_inc(done, 16)
                    sp.dma_start(out[:, HALF_W:HALF_W + KC * HD].rearrange("p (k n) -> p k n", k=KC),
                                 d["w_k"][:, h * HD:(h + 1) * HD].rearrange("(k p) n -> p k n", p=P))\
                        .then_inc(done, 16)

            load_x(0)
            load_x(1)
            for part in range(4):
                load_w(0, part)
            load_x(2)
            for hp in range(NP):
                for k in range(UP):
                    if hp * UP + k + 3 < NU:
                        load_x(hp * UP + k + 3)
                    if k == UP - 3 and hp + 1 < NP:
                        load_w(hp + 1, QK0)
                        load_w(hp + 1, WV)
                    if k == UP - 2 and hp + 1 < NP:
                        load_w(hp + 1, QK1)
                    if k == 0 and hp > 0:
                        load_w(hp, WO)

        @block.tensor
        def _(pe):
            def product(out, terms):
                n = 3 * len(terms)
                i = 0
                for lhs, rhs in terms:
                    for a, b in ((0, 0), (0, 1), (1, 0)):
                        mm = pe.matmul(out, lhs[a], rhs[b], start=i == 0, stop=i == n - 1)
                        i += 1
                return mm

            def both(x, f):
                return f(x[0]), f(x[1])

            def prep_of(hp, k):
                return (hp, k + 1) if k + 1 < UP else (hp + 1, 0)

            def k_product(hp, k):
                w, par, h = hp * UP + k, (k // 2) % 2, k % 2
                pe.wait_ge(x_low, 3 * (w - h) + 6)
                pe.wait_ge(w_low, 4 * hp + 1 + 2 * h)
                wait(pe, q_mean, w)
                product(ps_b[:, :], [(both(w_k, lambda x: x[:, h, i, :]), both(x_t, lambda x: x[:, par, KD + i, :]))
                                     for i in range(KC)]).then_inc(k_made, 1)

            def q_product(hp, k):
                w, par, h = hp * UP + k, (k // 2) % 2, k % 2
                wait(pe, v_low, w)
                product(ps_a[:, :], [(both(w_q, lambda x: x[:, h, i, :]), both(x_t, lambda x: x[:, par, i, :]))
                                     for i in range(KD)]).then_inc(q_made, 1)

            def sums(sq, sem):
                for t in range(ST):
                    mm = pe.matmul(ps_b[:, t:t + 1], sq[:, t * P:(t + 1) * P], ones[:, 0:1],
                                   start=True, stop=True)
                mm.then_inc(sem, 1)

            def k_sums(hp, k):
                pe.wait_ge(k_evac, hp * UP + k + 1)
                sums(k_sq, ksum_made)

            def k_rows(hp, k):
                pe.wait_ge(k_diag_made, hp * UP + k + 1)
                pe.matmul(ps_b[:, :], ones[:, :], k_diag[:, :, :].rearrange("p t n -> p (t n)"),
                          start=True, stop=True).then_inc(krow_made, 1)

            def q_sums(hp, k):
                w = hp * UP + k
                pe.wait_ge(q_high, w + 1)
                pe.wait_ge(k_normed, w + 1)
                sums(q_sq, qsum_made)

            def v_product(hp, k):
                w, par, h = hp * UP + k, (k // 2) % 2, k % 2
                pe.wait_ge(w_low, 4 * hp + 2)
                pe.wait_ge(q_low, w + 1)
                for i in range(2):
                    tok = slice((2 * h + i) * P, (2 * h + i + 1) * P)
                    mm = product(ps_a[:, i * 2 * HD:(i + 1) * 2 * HD],
                                 [(both(x_t, lambda x: x[:, par, KD + j, tok]), both(w_v, lambda x: x[:, j, :]))
                                  for j in range(KC)])
                mm.then_inc(v_made, 1)

            def scores(hp, k, qt):
                u, h = hp * UP + k, k % 2
                n = u * ST + qt
                if qt == 0:
                    pe.wait_ge(k_low, u + 1)
                    pe.wait_ge(q_low, u + 1)
                wait(pe, exp_done, n - 1)
                product(ps_s[qt % 2][:, :], [(both(q_t, lambda x: x[:, h, qt * P:(qt + 1) * P]),
                                              both(k_t, lambda x: x[:, h, :]))]).then_inc(s_made, 1)

            def turn(hp, k, qt):
                n = (hp * UP + k) * ST + qt
                pe.wait_ge(p_normed, n + 1)
                wait(pe, p_low, n - 1)
                for kt in range(ST):
                    tr = pe.transpose(ps_p[qt % 2][:, kt * P:(kt + 1) * P], prob[:, qt, kt * P:(kt + 1) * P],
                                      c.ident[:, :])
                tr.then_inc(p_turned, 1)

            def value(hp, k):
                u, par, h = hp * UP + k, (k // 2) % 2, k % 2
                pe.wait_ge(v_low, u - h + 2)
                pe.wait_ge(p_low, u * ST + ST)
                wait(pe, o_low, u)
                product(ps_o[:, :], [(both(v_s, lambda x: x[:, par, kt, h * HD:(h + 1) * HD]),
                                      both(prob_t, lambda x: x[:, kt, :])) for kt in range(ST)])\
                    .then_inc(pv_made, 1)

            def output(hp, k, t):
                g = hp * BATCH + k // 2 - 1
                pe.wait_ge(o_low, 2 * g + 2)
                if k == 2:
                    pe.wait_ge(w_low, 4 * hp + 4)
                wait(pe, y_added, g * ST + t)
                product(ps_y[:, :], [(both(o_t, lambda x: x[:, h, t * P:(t + 1) * P]), both(w_o, lambda x: x[:, h, :]))
                                     for h in range(2)]).then_inc(y_made, 1)

            def prologue(pe):
                pe.wait_ge(consts, 1)
                k_product(0, 0)
                k_sums(0, 0)
                q_product(0, 0)
                k_rows(0, 0)
                v_product(0, 0)
                q_sums(0, 0)

            def unit(pe, hp, k):
                nxt, more = prep_of(hp, k), prepares(hp, k)
                outs = k % 2 == 0 and not (isinstance(hp, int) and hp == 0 and k == 0)
                scores(hp, k, 0)
                scores(hp, k, 1)
                if more:
                    k_product(*nxt)
                if outs:
                    output(hp, k, 0)
                scores(hp, k, 2)
                scores(hp, k, 3)
                if more:
                    k_sums(*nxt)
                    q_product(*nxt)
                if outs:
                    output(hp, k, 1)
                turn(hp, k, 0)
                if more:
                    k_rows(*nxt)
                turn(hp, k, 1)
                if more:
                    v_product(*nxt)
                if outs:
                    output(hp, k, 2)
                turn(hp, k, 2)
                turn(hp, k, 3)
                if more:
                    q_sums(*nxt)
                if outs:
                    output(hp, k, 3)
                value(hp, k)

            schedule(pe, prologue, unit)
            for t in range(ST):
                output(NP, 0, t)

        def following(hp, k):
            return (hp, k + 1) if k + 1 < UP else (hp + 1, 0)

        @block.scalar
        def _(act):
            def copy(out, in_, sem, **kw):
                act.activation(out, in_, ACT.Copy, **kw).then_inc(sem, 1)

            def split_x(hp, k, i):
                s, par, odd = hp * UP + k, (k // 2) % 2, k % 2
                if i == 0:
                    act.wait_ge(x_loaded[odd], (16 + 16 * odd) * (hp * BATCH + k // 2 + 1))
                    wait(act, v_made, s - odd - 2)
                copy(x_t[0][:, par, 3 * odd + i, :], raw_x[:, odd, i, :], x_high)

            def split_w(hp, part):
                if part in (QK0, QK1):
                    act.wait_ge(w_loaded[0], 64 * hp + (32 if part == QK0 else 64))
                else:
                    act.wait_ge(w_loaded[1], 32 * hp + (16 if part == WV else 32))
                if part == WO:
                    wait(act, y_made, hp * BATCH * ST)
                else:
                    wait(act, v_made, hp * UP - (part == QK0))
                pieces = part_pieces(part)
                for hi, _, raw in pieces:
                    a = act.activation(hi, raw, ACT.Copy)
                a.then_inc(w_high, 1)

            def k_part(hp, k):
                w = hp * UP + k
                act.wait_ge(k_made, w + 1)
                wait(act, k_low, w)
                act.activation(k_sq[:, :], ps_b[:, :], ACT.Square)
                copy(k_raw[:, :], ps_b[:, :], k_evac, scale=m.gain[:, :])

            def q_part(hp, k):
                w = hp * UP + k
                act.wait_ge(q_made, w + 1)
                wait(act, qsum_made, w)
                wait(act, s_made, (w - 1) * ST)
                act.activation(q_sq[:, :], ps_a[:, :], ACT.Square)
                copy(q_t[0][:, k % 2, :], ps_a[:, :], q_high)

            def v_part(hp, k):
                w, par, h = hp * UP + k, (k // 2) % 2, k % 2
                act.wait_ge(v_made, w + 1)
                wait(act, pv_made, w - h - 2)
                copy(v_s[0][:, par, 2 * h:2 * h + 2, :].rearrange("p t n -> p (t n)"), ps_a[:, :], v_high)

            def exponent(hp, k, qt):
                n = (hp * UP + k) * ST + qt
                act.wait_ge(neg_made, n + 1)
                wait(act, p_turned, n - ST + 1)
                act.activation(prob[:, qt, :], ps_s[qt % 2][:, :], ACT.Exp, scale=q_rs[:, k % 2, qt:qt + 1],
                               bias=neg[:, qt:qt + 1], accum_out=den[:, qt:qt + 1]).then_inc(exp_done, 1)

            def turned(hp, k, qt):
                u = hp * UP + k
                act.wait_ge(p_turned, u * ST + qt + 1)
                if qt == 0:
                    wait(act, pv_made, u)
                copy(prob_t[0][:, :, qt * P:(qt + 1) * P], ps_p[qt % 2][:, :].rearrange("p (k l) -> p k l", k=ST),
                     p_high)

            def out_part(hp, k):
                u = hp * UP + k
                act.wait_ge(pv_made, u + 1)
                wait(act, y_made, (hp * BATCH + k // 2) * ST)
                copy(o_t[0][:, k % 2, :], ps_o[:, :], o_high)

            def prologue(act):
                for s in range(2):
                    for i in range(3):
                        split_x(0, s, i)
                for part in range(4):
                    split_w(0, part)
                k_part(0, 0)
                q_part(0, 0)
                v_part(0, 0)
                for i in range(3):
                    split_x(0, 2, i)

            def unit(act, hp, k):
                nxt, more, split = following(hp, k), prepares(hp, k), splits(hp, k)
                step = (hp, k + 3) if k + 3 < UP else (hp + 1, k + 3 - UP)
                early, late = weight_parts(hp, k)
                exponent(hp, k, 0)
                exponent(hp, k, 1)
                for w in early:
                    split_w(*w)
                if more:
                    k_part(*nxt)
                if split:
                    split_x(*step, 0)
                exponent(hp, k, 2)
                exponent(hp, k, 3)
                if more:
                    q_part(*nxt)
                if split:
                    split_x(*step, 1)
                turned(hp, k, 0)
                turned(hp, k, 1)
                if more:
                    v_part(*nxt)
                if split:
                    split_x(*step, 2)
                turned(hp, k, 2)
                turned(hp, k, 3)
                for w in late:
                    split_w(*w)
                out_part(hp, k)

            schedule(act, prologue, unit)

        @block.gpsimd
        def _(pool):
            def waits(sem, value):
                pool_waits(pool, c, sem, value)

            def split_x(hp, k, i):
                s, par, odd = hp * UP + k, (k // 2) % 2, k % 2
                waits(x_high, 3 * s + i + 1)
                pool.tensor_tensor(out=x_t[1][:, par, 3 * odd + i, :], in0=raw_x[:, odd, i, :],
                                   in1=x_t[0][:, par, 3 * odd + i, :], op=ALU.subtract).then_inc(x_low, 1)

            def split_w(hp, part):
                waits(w_high, 4 * hp + part + 1)
                for hi, lo, raw in part_pieces(part):
                    i = pool.tensor_tensor(out=lo, in0=raw, in1=hi, op=ALU.subtract)
                i.then_inc(w_low, 1)

            def k_root(hp, k):
                waits(k_mean, hp * UP + k + 1)
                pool.tensor_tensor(out=k_rs[:, :], in0=k_ms[:, :], in1=c.power[:, 0:ST], op=ALU.pow)\
                    .then_inc(k_rooted, 1)

            def k_part(hp, k):
                w, h = hp * UP + k, k % 2
                waits(k_normed, w + 1)
                pool.tensor_copy(k_t[0][:, h, :], k_raw[:, :]).then_inc(k_high, 1)
                waits(k_high, w + 1)
                pool.tensor_tensor(out=k_t[1][:, h, :], in0=k_raw[:, :], in1=k_t[0][:, h, :], op=ALU.subtract)\
                    .then_inc(k_low, 1)

            def q_root(hp, k):
                w = hp * UP + k
                waits(q_mean, w + 1)
                pool.tensor_tensor(out=q_rs[:, k % 2, :], in0=q_ms[:, :], in1=c.power[:, 0:ST], op=ALU.pow)\
                    .then_inc(q_rooted, 1)

            def prologue(pool):
                pool.memset(ones[:, :], 1.0).then_inc(consts, 1)
                for s in range(2):
                    for i in range(3):
                        split_x(0, s, i)
                for part in range(4):
                    split_w(0, part)
                k_root(0, 0)
                k_part(0, 0)
                q_root(0, 0)
                for i in range(3):
                    split_x(0, 2, i)

            def unit(pool, hp, k):
                nxt, more, split = following(hp, k), prepares(hp, k), splits(hp, k)
                step = (hp, k + 3) if k + 3 < UP else (hp + 1, k + 3 - UP)
                early, late = weight_parts(hp, k)
                for w in early:
                    split_w(*w)
                if split:
                    split_x(*step, 0)
                if more:
                    k_root(*nxt)
                if split:
                    split_x(*step, 1)
                if more:
                    k_part(*nxt)
                if split:
                    split_x(*step, 2)
                if more:
                    q_root(*nxt)
                for w in late:
                    split_w(*w)

            schedule(pool, prologue, unit)

        @block.vector
        def _(dve):
            def low(out, ps, hi, waits_for, count, sem):
                dve.wait_ge(waits_for, count)
                dve.tensor_tensor(out=out, in0=ps, in1=hi, op=ALU.subtract).then_inc(sem, 1)

            def k_mean_part(hp, k):
                w = hp * UP + k
                dve.wait_ge(ksum_made, w + 1)
                wait(dve, k_rooted, w)
                dve.tensor_scalar(out=k_ms[:, :], in0=ps_b[:, 0:ST], scalar1=HD * EPS, scalar2=None, op0=ALU.add)\
                    .then_inc(k_mean, 1)

            def k_diagonals(hp, k):
                w = hp * UP + k
                dve.wait_ge(k_rooted, w + 1)
                wait(dve, krow_made, w)
                dve.tensor_tensor(out=k_diag[:, :, :],
                                  in0=c.ident[:, :].rearrange("p (t n) -> p t n", t=1).broadcast_to([P, ST, P]),
                                  in1=k_rs[:, :].rearrange("p (t n) -> p t n", n=1).broadcast_to([P, ST, P]),
                                  op=ALU.mult).then_inc(k_diag_made, 1)

            def k_norm(hp, k):
                dve.wait_ge(krow_made, hp * UP + k + 1)
                dve.tensor_tensor(out=k_raw[:, :], in0=ps_b[:, :], in1=k_raw[:, :], op=ALU.mult)\
                    .then_inc(k_normed, 1)

            def q_mean_part(hp, k):
                w = hp * UP + k
                dve.wait_ge(qsum_made, w + 1)
                wait(dve, q_rooted, w)
                dve.tensor_scalar(out=q_ms[:, :], in0=ps_b[:, 0:ST], scalar1=HD * EPS, scalar2=None, op0=ALU.add)\
                    .then_inc(q_mean, 1)

            def q_part(hp, k):
                w, h = hp * UP + k, k % 2
                low(q_t[1][:, h, :], ps_a[:, :], q_t[0][:, h, :], q_high, w + 1, q_low)

            def v_part(hp, k):
                w, par, h = hp * UP + k, (k // 2) % 2, k % 2
                view = lambda x: x[:, par, 2 * h:2 * h + 2, :].rearrange("p t n -> p (t n)")
                low(view(v_s[1]), ps_a[:, :], view(v_s[0]), v_high, w + 1, v_low)

            def maximum(hp, k, qt):
                u = hp * UP + k
                n = u * ST + qt
                dve.wait_ge(s_made, n + 1)
                wait(dve, exp_done, n - ST + 1)
                dve.reduce_max(high[:, qt:qt + 1], ps_s[qt % 2][:, :], AX.X).then_inc(high_made, 1)
                dve.wait_ge(high_made, n + 1)
                if qt == 0:
                    dve.wait_ge(q_rooted, u + 1)
                dve.scalar_tensor_tensor(out=neg[:, qt:qt + 1], in0=high[:, qt:qt + 1], scalar=-1.0,
                                         in1=q_rs[:, k % 2, qt:qt + 1], op0=ALU.mult, op1=ALU.mult)\
                    .then_inc(neg_made, 1)

            def normalize(hp, k, qt):
                n = (hp * UP + k) * ST + qt
                dve.wait_ge(exp_done, n + 1)
                dve.reciprocal(rden[:, qt:qt + 1], den[:, qt:qt + 1]).then_inc(rden_made, 1)
                dve.wait_ge(rden_made, n + 1)
                dve.tensor_scalar(out=prob[:, qt, :], in0=prob[:, qt, :], scalar1=rden[:, qt:qt + 1],
                                  scalar2=None, op0=ALU.mult).then_inc(p_normed, 1)

            def turned(hp, k, qt):
                n = (hp * UP + k) * ST + qt
                cols = slice(qt * P, (qt + 1) * P)
                low(prob_t[1][:, :, cols], ps_p[qt % 2][:, :].rearrange("p (k l) -> p k l", k=ST),
                    prob_t[0][:, :, cols], p_high, n + 1, p_low)

            def add(hp, k, t):
                g = hp * BATCH + k // 2 - 1
                dve.wait_ge(y_made, g * ST + t + 1)
                x = c.X[:, ((k // 2 - 1) % BATCH) * ST + t, :]
                dve.tensor_tensor(out=x, in0=ps_y[:, :], in1=x, op=ALU.add).then_inc(y_added, 1)

            def prologue(dve):
                k_mean_part(0, 0)
                k_diagonals(0, 0)
                q_part(0, 0)
                k_norm(0, 0)
                v_part(0, 0)
                q_mean_part(0, 0)

            def unit(dve, hp, k):
                nxt, more = following(hp, k), prepares(hp, k)
                outs = k % 2 == 0 and not (isinstance(hp, int) and hp == 0 and k == 0)
                maximum(hp, k, 0)
                maximum(hp, k, 1)
                if outs:
                    add(hp, k, 0)
                normalize(hp, k, 0)
                normalize(hp, k, 1)
                maximum(hp, k, 2)
                maximum(hp, k, 3)
                if more:
                    k_mean_part(*nxt)
                normalize(hp, k, 2)
                normalize(hp, k, 3)
                if more:
                    k_diagonals(*nxt)
                    q_part(*nxt)
                if outs:
                    add(hp, k, 1)
                if more:
                    k_norm(*nxt)
                turned(hp, k, 0)
                turned(hp, k, 1)
                if more:
                    v_part(*nxt)
                if outs:
                    add(hp, k, 2)
                turned(hp, k, 2)
                turned(hp, k, 3)
                if more:
                    q_mean_part(*nxt)
                if outs:
                    add(hp, k, 3)
                u = hp * UP + k
                low(o_t[1][:, k % 2, :], ps_o[:, :], o_t[0][:, k % 2, :], o_high, u + 1, o_low)

            schedule(dve, prologue, unit)
            for t in range(ST):
                add(NP, 0, t)


def quantize_weights(nc, c, m, d):
    with ExitStack() as ctx:
        p = Pipe(nc, ctx)
        block = ctx.enter_context(nc.Block())
        raw = [p.sb(f"raw{i}", [P, FN]) for i in range(2)]
        junk = p.sb("junk", [P, FN])
        part, sums = p.sb("part", [P, 2]), p.sb("sums", [P, 2])
        ones = p.sb("ones_f", [P, P])
        scale = p.sb("w_scale", [P, 2])
        ps_sum = p.ps("ps_sum", [P, 2])
        loaded = [p.sem("raw_loaded0"), p.sem("raw_loaded1")]
        ones_made, step, totals = p.sem("ones_made"), p.sem("wq_step"), p.sem("totals")
        part_made = [p.sem("part_made0"), p.sem("part_made1")]

        @block.sync
        def _(sp):
            sp.dma_start(raw[0][:, :].rearrange("p (k n) -> p k n", k=KD),
                         d["w1"].rearrange("(k p) n -> p k n", p=P)).then_inc(loaded[0], 16)
            sp.dma_start(raw[1][:, :].rearrange("p (k n) -> p k n", k=KF),
                         d["w2"].rearrange("(k p) n -> p k n", p=P)).then_inc(loaded[1], 16)

        @block.scalar
        def _(act):
            act.wait_ge(loaded[0], 16)
            act.activation(junk[:, :], raw[0][:, :], ACT.Abs, accum_out=part[:, 0:1]).then_inc(part_made[0], 1)

        @block.gpsimd
        def _(pool):
            pool.memset(ones[:, :], 1.0).then_inc(ones_made, 1)

        @block.tensor
        def _(pe):
            pe.wait_ge(ones_made, 1)
            pe.wait_ge(part_made[0], 1)
            pe.wait_ge(part_made[1], 1)
            pe.matmul(ps_sum[:, :], ones[:, :], part[:, :], start=True, stop=True).then_inc(totals, 1)

        @block.vector
        def _(dve):
            n = [0]

            def link(ins):
                n[0] += 1
                ins.then_inc(step, 1)
                dve.wait_ge(step, n[0])

            dve.wait_ge(loaded[1], 16)
            dve.tensor_reduce(part[:, 1:2], raw[1][:, :], AX.X, ALU.add, apply_absolute_value=True)\
                .then_inc(part_made[1], 1)
            dve.wait_ge(totals, 1)
            link(dve.tensor_scalar(out=sums[:, :], in0=ps_sum[:, :], scalar1=1.0 / (P * FN), scalar2=EPS,
                                   op0=ALU.mult, op1=ALU.max))
            link(dve.reciprocal(scale[:, :], sums[:, :]))
            link(dve.reciprocal(m.w_step[:, :], scale[:, :]))
            for i, out in ((0, m.w1q), (1, m.w2q)):
                link(dve.tensor_scalar(out=raw[i][:, :], in0=raw[i][:, :], scalar1=scale[:, i:i + 1], scalar2=1.0,
                                       op0=ALU.mult, op1=ALU.min))
                link(dve.tensor_scalar(out=raw[i][:, :], in0=raw[i][:, :], scalar1=-1.0, scalar2=MAGIC,
                                       op0=ALU.max, op1=ALU.add))
                link(dve.tensor_scalar(out=out[:, :, :].rearrange("p k n -> p (k n)"), in0=raw[i][:, :],
                                       scalar1=-MAGIC, scalar2=None, op0=ALU.add))


def feed_forward(nc, c, m):
    with ExitStack() as ctx:
        p = Pipe(nc, ctx)
        block = ctx.enter_context(nc.Block())
        ident = p.sb("ident_b", [P, P], BF16)
        xf = [p.sb(f"xf{i}", [P, DM]) for i in range(2)]
        xq = [p.sb(f"xq{i}", [P, DM], BF16) for i in range(2)]
        xq_t = [p.sb(f"xq_t{i}", [P, KD, P], BF16) for i in range(2)]
        hf = [p.sb(f"hf{i}", [P, DF]) for i in range(2)]
        hq = [p.sb(f"hq{i}", [P, DF], BF16) for i in range(2)]
        hq_t = p.sb("hq_t", [P, KF, P], BF16)
        stat = p.sb("stat", [P, 2, 6])
        ps_h = [p.ps(f"ps_fh{i}", [P, SEQ]) for i in range(4)]
        ps_x = p.ps("ps_fx", [P, DM])[:, :].bitcast(BF16)[:, 0:KD * P]
        ps_t = [p.ps(f"ps_ft{i}", [P, DM])[:, :].bitcast(BF16) for i in range(2)]
        ps_y = p.ps("ps_fy", [P, DM])
        ident_made = p.sem("ident_made")
        step = p.sem("ff_step")
        xq_made, xq_turned, xq_kept = p.sem("xq_made"), p.sem("xq_turned"), p.sem("xq_kept")
        h_made, gelu_made = p.sem("h_made"), p.sem("gelu_made")
        hq_made, hq_turned, hq_kept = p.sem("hq_made"), p.sem("hq_turned"), p.sem("hq_kept")
        y_made, y_added = p.sem("fy_made"), p.sem("fy_added")
        h_scaled, h_shifted, h_clipped = p.sem("h_scaled"), p.sem("h_shifted"), p.sem("h_clipped")

        def schedule(eng, *parts):
            def turn(t, par):
                for lag, part in parts:
                    if not isinstance(t, int) or 0 <= t - lag < NT:
                        part(t - lag, (par + lag) % 2)
            for t in range(-1, 4):
                turn(t, t % 2)
            with eng.Fori(2, NT // 2 - 1) as t2:
                for par in range(2):
                    turn(t2 * 2 + par, par)
            for t in range(NT - 2, NT + 2):
                turn(t, t % 2)

        @block.tensor
        def _(pe):
            def ahead(t, par):
                pe.wait_ge(xq_made, t + 1)
                wait(pe, xq_kept, t)
                for k in range(KD):
                    tr = pe.transpose(ps_x[:, k * P:(k + 1) * P], xq[par][:, k * P:(k + 1) * P], ident[:, :])
                tr.then_inc(xq_turned, 1)
                pe.wait_ge(xq_kept, t + 1)
                for n in range(4):
                    wait(pe, gelu_made, t * 4 + n - 3)
                    for k in range(KD):
                        mm = pe.matmul(ps_h[n][:, :], xq_t[par][:, k, :], m.w1q[:, k, n * SEQ:(n + 1) * SEQ],
                                       start=k == 0, stop=k == KD - 1)
                    mm.then_inc(h_made, 1)

            def behind(t, par):
                pe.wait_ge(hq_made, t + 1)
                for i in range(2):
                    wait(pe, hq_kept, t * 2 + i - 1)
                    for k in range(8):
                        tr = pe.transpose(ps_t[i][:, k * P:(k + 1) * P],
                                          hq[par][:, (i * 8 + k) * P:(i * 8 + k + 1) * P], ident[:, :])
                    tr.then_inc(hq_turned, 1)
                wait(pe, y_added, t)
                for k in range(KF):
                    if k % 8 == 0:
                        pe.wait_ge(hq_kept, t * 2 + k // 8 + 1)
                    mm = pe.matmul(ps_y[:, :], hq_t[:, k, :], m.w2q[:, k, :], start=k == 0, stop=k == KF - 1)
                mm.then_inc(y_made, 1)

            pe.wait_ge(ident_made, 1)
            schedule(pe, (2, behind), (0, ahead))

        @block.scalar
        def _(act):
            def ahead(t, par):
                act.wait_ge(xq_turned, t + 1)
                wait(act, h_made, (t - 1) * 4)
                act.activation(xq_t[par][:, :, :].rearrange("p k l -> p (k l)"), ps_x, ACT.Copy)\
                    .then_inc(xq_kept, 1)
                wait(act, hq_made, t - 1)
                for n in range(4):
                    act.wait_ge(h_made, t * 4 + n + 1)
                    act.activation(hf[par][:, n * SEQ:(n + 1) * SEQ], ps_h[n][:, :], ACT.Gelu,
                                   scale=stat[:, par, 2:3]).then_inc(gelu_made, 1)

            def behind(t, par):
                wait(act, y_made, t)
                for i in range(2):
                    act.wait_ge(hq_turned, t * 2 + i + 1)
                    act.activation(hq_t[:, i * 8:(i + 1) * 8, :].rearrange("p k l -> p (k l)"), ps_t[i][:, :],
                                   ACT.Copy).then_inc(hq_kept, 1)

            def shift(t, par):
                act.wait_ge(h_scaled, t + 1)
                act.activation(hf[par][:, :], hf[par][:, :], ACT.Copy, scale=stat[:, par, 4:5], bias=MAGIC)\
                    .then_inc(h_shifted, 1)

            schedule(act, (2, behind), (1, shift), (0, ahead))

        @block.gpsimd
        def _(pool):
            def part(t, par):
                pool_waits(pool, c, h_clipped, t + 1)
                if not isinstance(t, int) or t >= 2:
                    pool_waits(pool, c, hq_turned, (t - 1) * 2)
                pool.tensor_scalar(out=hq[par][:, :], in0=hf[par][:, :], scalar1=-MAGIC, scalar2=None,
                                   op0=ALU.add).then_inc(hq_made, 1)

            schedule(pool, (1, part))

        @block.vector
        def _(dve):
            def link(t, n, ins):
                ins.then_inc(step, 1)
                dve.wait_ge(step, n + 1)

            def scales(t, n, x, s, w_step):
                link(t, n, dve.tensor_reduce(s[:, 0:1], x, AX.X, ALU.max, apply_absolute_value=True))
                link(t, n + 1, dve.tensor_scalar(out=s[:, 0:1], in0=s[:, 0:1], scalar1=EPS, scalar2=1.0 / QMAX,
                                                 op0=ALU.max, op1=ALU.mult))
                link(t, n + 2, dve.reciprocal(s[:, 1:2], s[:, 0:1]))
                link(t, n + 3, dve.tensor_scalar(out=s[:, 2:3], in0=s[:, 0:1], scalar1=w_step, scalar2=None,
                                                 op0=ALU.mult))

            def ahead(t, par):
                n = base_ahead(t)
                x, s = xf[par][:, :], stat[:, par, 0:3]
                wait(dve, gelu_made, (t - 1) * 4)
                link(t, n, dve.tensor_scalar(out=x, in0=c.X[:, ds1(t), :].rearrange("p a l -> p (a l)"),
                                             scalar1=c.rstd[:, ds1(t)], scalar2=c.nbias[:, ds1(t)],
                                             op0=ALU.mult, op1=ALU.add))
                scales(t, n + 1, x, s, m.w_step[:, 0:1])
                link(t, n + 5, dve.tensor_scalar(out=x, in0=x, scalar1=s[:, 1:2], scalar2=QMAX,
                                                 op0=ALU.mult, op1=ALU.min))
                link(t, n + 6, dve.tensor_scalar(out=x, in0=x, scalar1=-QMAX - 1.0, scalar2=MAGIC,
                                                 op0=ALU.max, op1=ALU.add))
                dve.tensor_scalar(out=xq[par][:, :], in0=x, scalar1=-MAGIC, scalar2=None, op0=ALU.add)\
                    .then_inc(xq_made, 1)

            def hidden_scales(t, par):
                dve.wait_ge(gelu_made, t * 4 + 4)
                wait(dve, y_added, t - 1)
                scales(t, base_hidden(t), hf[par][:, :], stat[:, par, 3:6], m.w_step[:, 1:2])
                dve.sem_inc(h_scaled, 1)

            def clip(t, par):
                dve.wait_ge(h_shifted, t + 1)
                dve.tensor_scalar(out=hf[par][:, :], in0=hf[par][:, :], scalar1=MAGIC - QMAX - 1.0,
                                  scalar2=MAGIC + QMAX, op0=ALU.max, op1=ALU.min).then_inc(h_clipped, 1)

            def add(t, par):
                dve.wait_ge(y_made, t + 1)
                x = c.X[:, ds1(t), :].rearrange("p a l -> p (a l)")
                dve.scalar_tensor_tensor(out=x, in0=ps_y[:, :], scalar=stat[:, par, 5:6], in1=x,
                                         op0=ALU.mult, op1=ALU.add).then_inc(y_added, 1)

            def base_ahead(t):
                return 0 if isinstance(t, int) and t == 0 else t * 7 + (t - 1) * 4

            def base_hidden(t):
                return NT * 7 + t * 4 if isinstance(t, int) and t == NT - 1 else (t + 2) * 7 + t * 4

            dve.tensor_copy(ident[:, :], c.ident[:, :]).then_inc(ident_made, 1)
            schedule(dve, (1, hidden_scales), (-1, ahead), (1, clip), (2, add))


class Holder:
    pass


STAGES = 4


def program(nc, d, out, stages=STAGES):
    with ExitStack() as ctx:
        p = Pipe(nc, ctx)
        c = Holder()
        c.X = p.sb("X", [P, NT, DM])
        c.ident = p.sb("ident", [P, P])
        c.power = p.sb("power", [P, P])
        c.rstd = p.sb("rstd", [P, NT])
        c.nbias = p.sb("nbias", [P, NT])
        c.pool_passed = nc.alloc_semaphore("pool_passed")
        c.const_made = nc.alloc_semaphore("const_made")
        load_constants(nc, c, d)
        with nc.cleanup_on_exit(), ExitStack() as ssm:
            q = Pipe(nc, ssm)
            m = Holder()
            m.u = q.sb("u", [P, BATCH * EC, SEQ])
            m.delta = q.sb("delta", [P, BATCH * EC, SEQ])
            m.du = q.sb("du", [P, BATCH * EC, SEQ])
            m.d_a = q.sb("d_a", [P, 2, G, SEQ])
            m.a_neg = q.sb("a_neg", [P, EC * DS])
            m.d_diag = q.sb("d_diag", [P, EC, P])
            m.zero2 = q.sb("zero2", [P, 2])
            m.zeros = q.sb("zeros", [P, DM])
            m.rows_dram = nc.dram_tensor("rows_dram", [FILLS * FILL * P, DM], FP32, kind="Internal").ap()
            m.y_dram = nc.dram_tensor("y_dram", [(MINT + FILLS * FILL_Y) * P, DM], FP32, kind="Internal").ap()
            assert min(m.rows_dram.shape[0], m.y_dram.shape[0]) >= (MAXT + 2) * P
            m.bc_dram = nc.dram_tensor("bc_dram", [BATCH, 2 * DS, SEQ], FP32, kind="Internal").ap()
            norm_statistics(nc, c, "n0")
            ssm_inputs(nc, c, m, d)
            ssm_scan(nc, c, m)
        if stages >= 2:
            with nc.cleanup_on_exit():
                norm_statistics(nc, c, "n1")
                with ExitStack() as moe:
                    q = Pipe(nc, moe)
                    m.pos = q.sb("pos_row", [P, TOPK, NT], U32)
                    m.weight = q.sb("weight", [P, NT, TOPK])
                    m.table = q.sb("table", [1, T_PAIRS + 1], I32)
                    with ExitStack() as first:
                        q = Pipe(nc, first)
                        m.xn = q.sb("xn", [P, NT, DM])
                        m.logits = q.sb("logits", [P, NT, NE])
                        m.sim = q.sb("sim", [NE, NE])
                        m.sim_loaded = q.sem("sim_loaded")
                        router_logits(nc, c, m, d)
                        route(nc, c, m)
                        dispatch(nc, c, m)
                    experts(nc, c, m, d)
                    combine(nc, c, m)
        if stages >= 3:
            m = Holder()
            m.xn_dram = nc.dram_tensor("xn_dram", [BATCH * P, KD * SEQ], FP32, kind="Internal").ap()
            m.gain = p.sb("gain", [P, 1])
            with nc.cleanup_on_exit():
                norm_statistics(nc, c, "n2")
                turn_tokens(nc, c, m, d)
                attention(nc, c, m, d)
        if stages >= 4:
            norm_statistics(nc, c, "n3")
            m.w1q = p.sb("w1q", [P, KD, DF], BF16)
            m.w2q = p.sb("w2q", [P, KF, DM], BF16)
            m.w_step = p.sb("w_step", [P, 2])
            quantize_weights(nc, c, m, d)
            feed_forward(nc, c, m)
        store_output(nc, c, out)


def store_output(nc, c, out):
    stored = nc.alloc_semaphore("stored")
    with nc.Block() as block:
        @block.sync
        def _(sp):
            sp.dma_start(out.rearrange("(t p) n -> p t n", p=P), c.X[:, :, :]).then_inc(stored, 16)
            sp.wait_ge(stored, 16)


def kernel(x, ctx_1024, L0_xattn_in_proj_w, L0_xattn_conv_w, L0_xattn_conv_b, L0_xattn_x_proj_w,
           L0_xattn_dt_proj_w, L0_xattn_dt_proj_b, L0_xattn_A_log, L0_xattn_D, L0_ffn_gate_weight,
           L0_ffn_gate_up_proj, L0_ffn_down_proj, L0_ffn_similarity, L1_xattn_Wq, L1_xattn_Wk,
           L1_xattn_Wv, L1_xattn_Wo, L1_xattn_gq, L1_xattn_gk, L1_ffn_w1, L1_ffn_w2):
    import numpy as np
    import concourse.bacc as bacc
    from concourse.bass_utils import run_bass_kernel_spmd as run
    A = np.asarray
    arrays = {
        "x": A(x).reshape(BATCH * SEQ, DM),
        "ctx_t": A(ctx_1024).transpose(0, 2, 1).reshape(BATCH * CD, SEQ),
        "in_proj": A(L0_xattn_in_proj_w).T,
        "conv_w": A(L0_xattn_conv_w),
        "conv_b": A(L0_xattn_conv_b),
        "x_proj": A(L0_xattn_x_proj_w).T,
        "dt_proj": A(L0_xattn_dt_proj_w).T,
        "dt_b": A(L0_xattn_dt_proj_b),
        "a_log": A(L0_xattn_A_log),
        "d_skip": A(L0_xattn_D),
        "gate_w": A(L0_ffn_gate_weight).T,
        "similarity": A(L0_ffn_similarity),
        "w_q": A(L1_xattn_Wq), "w_k": A(L1_xattn_Wk), "w_v": A(L1_xattn_Wv), "w_o": A(L1_xattn_Wo),
        "g_q": A(L1_xattn_gq), "g_k": A(L1_xattn_gk),
        "w1": A(L1_ffn_w1).T, "w2": A(L1_ffn_w2).T,
        "gate_up": A(L0_ffn_gate_up_proj).reshape(NE, 2 * FI, KD, P).transpose(0, 3, 2, 1).reshape(NE, P, KD * 2 * FI),
        "down": A(L0_ffn_down_proj).reshape(NE, DM, 2, FI // 2).transpose(0, 3, 2, 1).reshape(NE, FI // 2, 2 * DM),
    }
    arrays = {k: np.ascontiguousarray(v) for k, v in arrays.items()}
    nc = bacc.Bacc("TRN2", target_bir_lowering=False, num_devices=1)
    d = {k: nc.dram_tensor("in_" + k, v.shape, mybir.dt.from_np(v.dtype), kind="ExternalInput").ap()
         for k, v in arrays.items()}
    out = nc.dram_tensor("out", (BATCH * SEQ, DM), FP32, kind="ExternalOutput").ap()
    program(nc, d, out)
    r = run(nc, [{"in_" + k: v for k, v in arrays.items()}], core_ids=[0])
    return r.results[0]["out"].reshape(BATCH, SEQ, DM)
```
